# Optimizing a Trainium2 kernel written in Bass

```python
import numpy as np
import jax
import jax.numpy as jnp

def _softmax(x, axis=-1):
    return jax.nn.softmax(x, axis=axis)

def _gelu(x):
    return jax.nn.gelu(x, approximate=True)

def _silu(x):
    return jax.nn.silu(x)

def _sigmoid(x):
    return jax.nn.sigmoid(x)

def _layernorm(x, axis=-1, eps=1e-05):
    m = jnp.mean(x, axis=axis, keepdims=True)
    v = jnp.var(x, axis=axis, keepdims=True)
    return (x - m) / jnp.sqrt(v + eps)

def _scatter_add(tgt, idx, src, axis=0):
    return tgt.at[idx].add(src)

def _segment_sum(src, seg, n):
    return jax.ops.segment_sum(src, seg, n)
kernel_name = 'mk_flamingo_gated_d1_seqx_r8_dad20b'

def setup_inputs(seed: int=0):
    np.random.seed(seed)
    _w = jnp.asarray

    def _rec_inputs():
        import jax
        import jax.numpy as jnp
        _rk = jax.random.key(seed)
        x = 7.22e-05 + 1 * jax.random.normal(jax.random.fold_in(_rk, 1), (32, 64, 512), jnp.float32)
        _lenS = 64 - jax.random.randint(jax.random.fold_in(_rk, 7), (32,), 0, max(1, 64 // 4) + 1, jnp.int32)
        _lenS2 = 64 - jax.random.randint(jax.random.fold_in(_rk, 8), (32,), 0, max(1, 64 // 4) + 1, jnp.int32)
        _ctx_4096P = jax.random.normal(jax.random.fold_in(_rk, 11), (32, 16, 512), jnp.float32)
        _ctx_4096c = jax.random.dirichlet(jax.random.fold_in(_rk, 511), 0.3 * jnp.ones((16,), jnp.float32), (32, 64))
        _ctx_4096t = jnp.einsum('bsk,bkd->bsd', _ctx_4096c, _ctx_4096P)
        _ctx_4096t = _ctx_4096t * jax.lax.rsqrt(jnp.mean(jnp.square(_ctx_4096t)) + 1e-12) * 0.953939
        ctx_4096 = 4.13588e-05 + 0.999923 * (_ctx_4096t + 0.3 * jax.random.normal(jax.random.fold_in(_rk, 611), (32, 64, 512), jnp.float32))
        _g = jax.random.normal(jax.random.fold_in(_rk, 9001), (2, 1), jnp.float32)
        _g = jnp.sign(_g) * jnp.maximum(jnp.abs(_g), 1.0) + (_g == 0) * 1.0
        g_xattn = _g[0]
        g_ffn = _g[1]
        return (x, ctx_4096, g_xattn, g_ffn)
    x, ctx_4096, g_xattn, g_ffn = _rec_inputs()

    def _L0_xattn_setup():
        import jax, jax.numpy as jnp
        import numpy as np
        B, C, N = (4, 64, 512)
        CH = C // 2
        key = jax.random.key(seed)
        ks = jax.random.split(key, 10)
        s = 1.0 / np.sqrt(C)
        return {'Q': jax.random.normal(ks[0], (B, C, N), dtype=jnp.float32), 'K': jax.random.normal(ks[1], (B, C, N), dtype=jnp.float32), 'V': jax.random.normal(ks[2], (B, C, N), dtype=jnp.float32), 'Wq': jax.random.normal(ks[3], (CH, C), dtype=jnp.float32) * s, 'bq': jax.random.normal(ks[4], (CH,), dtype=jnp.float32) * s, 'Wk': jax.random.normal(ks[5], (CH, C), dtype=jnp.float32) * s, 'bk': jax.random.normal(ks[6], (CH,), dtype=jnp.float32) * s, 'Wv': jax.random.normal(ks[7], (C, C), dtype=jnp.float32) * s, 'bv': jax.random.normal(ks[8], (C,), dtype=jnp.float32) * s, 'gamma': jnp.full((1,), 0.5, dtype=jnp.float32)}
    _L0_xattn_all = _L0_xattn_setup()
    _L0_xattn_in = {k: v for k, v in _L0_xattn_all.items() if k in ('Wq', 'bq', 'Wk', 'bk', 'Wv', 'bv', 'gamma')}
    del _L0_xattn_all

    def _L0_ffn_setup():
        import jax, jax.numpy as jnp
        import numpy as np
        BLK = 16
        FP8_MAX = 448.0
        GSCALE_DIV = 448.0 * 6.0
        SELECT = 128

        def _ste(x, q):
            return x + jax.lax.stop_gradient(q - x)

        def _fp8_block_qdq(v):
            lead, C = (v.shape[:-1], v.shape[-1])
            vb = v.reshape(*lead, C // BLK, BLK)
            s = jnp.maximum(jnp.max(jnp.abs(vb), axis=-1, keepdims=True) / FP8_MAX, 1e-08)
            q = (vb / s).astype(jnp.float8_e4m3fn).astype(jnp.float32) * s
            return _ste(vb, q).reshape(*lead, C)

        def _int4_block_qdq(w):
            out, C = w.shape
            wb = w.reshape(out, C // BLK, BLK)
            s = jnp.maximum(jnp.max(jnp.abs(wb), axis=-1, keepdims=True) / 7.0, 1e-08)
            q = jnp.round(jnp.clip(wb / s, -8.0, 7.0)) * s
            return _ste(wb, q).reshape(out, C)

        def _quant_act(x2d, reorder_index, select_num):
            g = jnp.maximum(jnp.max(jnp.abs(x2d)) / GSCALE_DIV, 1e-08)
            xr = (x2d / g)[:, reorder_index]
            n = xr.shape[1] - select_num
            normal = _fp8_block_qdq(xr[:, :n])
            outl = xr[:, n:]
            q1 = _fp8_block_qdq(outl)
            q2 = _fp8_block_qdq(outl - q1)
            A = jnp.concatenate([normal, q1, q2], axis=1)
            return (A, g)

        def _quant_w(w, reorder_index, select_num):
            wr = w[:, reorder_index]
            n = wr.shape[1] - select_num
            wq = jnp.concatenate([wr[:, :n], wr[:, n:], wr[:, n:]], axis=1)
            return _int4_block_qdq(wq)
        key = jax.random.key(seed)
        k0, k1, k2, k3 = jax.random.split(key, 4)
        B, L, H, I = (2, 256, 512, 1376)
        return {'x': jax.random.normal(k0, (B, L, H), dtype=jnp.float32), 'w_gate': jax.random.normal(k1, (I, H), dtype=jnp.float32) * 0.02, 'w_up': jax.random.normal(k2, (I, H), dtype=jnp.float32) * 0.02, 'w_down': jax.random.normal(k3, (H, I), dtype=jnp.float32) * 0.02, 'ri_in': jnp.arange(H, dtype=jnp.int32), 'ri_mid': jnp.arange(I, dtype=jnp.int32)}
    _L0_ffn_all = _L0_ffn_setup()
    _L0_ffn_in = {k: v for k, v in _L0_ffn_all.items() if k in ('w_gate', 'w_up', 'w_down', 'ri_in', 'ri_mid')}
    del _L0_ffn_all
    return {'x': x, 'ctx_4096': ctx_4096, 'g_xattn': g_xattn, 'g_ffn': g_ffn, 'L0_xattn_Wq': _L0_xattn_in['Wq'], 'L0_xattn_bq': _L0_xattn_in['bq'], 'L0_xattn_Wk': _L0_xattn_in['Wk'], 'L0_xattn_bk': _L0_xattn_in['bk'], 'L0_xattn_Wv': _L0_xattn_in['Wv'], 'L0_xattn_bv': _L0_xattn_in['bv'], 'L0_xattn_gamma': _L0_xattn_in['gamma'], 'L0_ffn_w_gate': _L0_ffn_in['w_gate'], 'L0_ffn_w_up': _L0_ffn_in['w_up'], 'L0_ffn_w_down': _L0_ffn_in['w_down'], 'L0_ffn_ri_in': _L0_ffn_in['ri_in'], 'L0_ffn_ri_mid': _L0_ffn_in['ri_mid']}

def reference(x, ctx_4096, g_xattn, g_ffn, L0_xattn_Wq, L0_xattn_bq, L0_xattn_Wk, L0_xattn_bk, L0_xattn_Wv, L0_xattn_bv, L0_xattn_gamma, L0_ffn_w_gate, L0_ffn_w_up, L0_ffn_w_down, L0_ffn_ri_in, L0_ffn_ri_mid):
    import jax
    import jax.numpy as jnp

    def _L0_xattn_ref(Q, K, V, Wq, bq, Wk, bk, Wv, bv, gamma):
        import jax, jax.numpy as jnp
        import numpy as np
        B, C, N = (4, 64, 512)
        CH = C // 2
        q = jnp.einsum('oc,bcn->bon', Wq, Q) + bq[None, :, None]
        k = jnp.einsum('oc,bcn->bon', Wk, K) + bk[None, :, None]
        v = jnp.einsum('oc,bcn->bon', Wv, V) + bv[None, :, None]
        energy = jnp.einsum('bcn,bcm->bnm', q, k)
        attention = jax.nn.softmax(energy, axis=-1)
        out = jnp.einsum('bcm,bnm->bcn', v, attention)
        return gamma * out + V

    def _L0_ffn_ref(x, w_gate, w_up, w_down, ri_in, ri_mid):
        import jax, jax.numpy as jnp
        import numpy as np
        BLK = 16
        FP8_MAX = 448.0
        GSCALE_DIV = 448.0 * 6.0
        SELECT = 128

        def _ste(x, q):
            return x + jax.lax.stop_gradient(q - x)

        def _fp8_block_qdq(v):
            lead, C = (v.shape[:-1], v.shape[-1])
            vb = v.reshape(*lead, C // BLK, BLK)
            s = jnp.maximum(jnp.max(jnp.abs(vb), axis=-1, keepdims=True) / FP8_MAX, 1e-08)
            q = (vb / s).astype(jnp.float8_e4m3fn).astype(jnp.float32) * s
            return _ste(vb, q).reshape(*lead, C)

        def _int4_block_qdq(w):
            out, C = w.shape
            wb = w.reshape(out, C // BLK, BLK)
            s = jnp.maximum(jnp.max(jnp.abs(wb), axis=-1, keepdims=True) / 7.0, 1e-08)
            q = jnp.round(jnp.clip(wb / s, -8.0, 7.0)) * s
            return _ste(wb, q).reshape(out, C)

        def _quant_act(x2d, reorder_index, select_num):
            g = jnp.maximum(jnp.max(jnp.abs(x2d)) / GSCALE_DIV, 1e-08)
            xr = (x2d / g)[:, reorder_index]
            n = xr.shape[1] - select_num
            normal = _fp8_block_qdq(xr[:, :n])
            outl = xr[:, n:]
            q1 = _fp8_block_qdq(outl)
            q2 = _fp8_block_qdq(outl - q1)
            A = jnp.concatenate([normal, q1, q2], axis=1)
            return (A, g)

        def _quant_w(w, reorder_index, select_num):
            wr = w[:, reorder_index]
            n = wr.shape[1] - select_num
            wq = jnp.concatenate([wr[:, :n], wr[:, n:], wr[:, n:]], axis=1)
            return _int4_block_qdq(wq)
        B, L, H = x.shape
        x2 = x.reshape(B * L, H)
        A, g = _quant_act(x2, ri_in, SELECT)
        Wg = _quant_w(w_gate, ri_in, SELECT)
        Wu = _quant_w(w_up, ri_in, SELECT)
        gate = A @ Wg.T * g
        up = A @ Wu.T * g
        h = jax.nn.silu(gate) * up
        Am, gm = _quant_act(h, ri_mid, SELECT)
        Wd = _quant_w(w_down, ri_mid, SELECT)
        y = Am @ Wd.T * gm
        return y.reshape(B, L, -1)
    x = x + jnp.tanh(g_xattn[0]) * _L0_xattn_ref(_layernorm(x, axis=-1), ctx_4096, ctx_4096, L0_xattn_Wq, L0_xattn_bq, L0_xattn_Wk, L0_xattn_bk, L0_xattn_Wv, L0_xattn_bv, L0_xattn_gamma)
    x = x + jnp.tanh(g_ffn[0]) * _L0_ffn_ref(_layernorm(x, axis=-1), L0_ffn_w_gate, L0_ffn_w_up, L0_ffn_w_down, L0_ffn_ri_in, L0_ffn_ri_mid)
    return x

_drawn_inputs = setup_inputs


def setup_inputs(seed=0):
    import zlib

    import numpy as np

    out = dict(_drawn_inputs(seed))
    spreads = {}
    factors = {}
    for name, (base, spread) in spreads.items():
        noise = np.random.default_rng([zlib.crc32(name.encode()), seed]).standard_normal(out[name].shape)
        drawn = base * np.exp(spread * noise) if base else spread * noise
        out[name] = jnp.asarray(drawn.astype(out[name].dtype))
    for name, factor in factors.items():
        out[name] = (out[name] * factor).astype(out[name].dtype)
    return out
```

```python
from contextlib import ExitStack

import concourse.bass as bass
from concourse import mybir

ALU = mybir.AluOpType
ACT = mybir.ActivationFunctionType
AX_X = mybir.AxisListType.X
F32 = mybir.dt.float32
F16 = mybir.dt.float16
I32 = mybir.dt.int32
RMAX = bass.bass_isa.ReduceOp.max

P = 128
BLK = 16
FP8_MAX = 448.0
INT4_MAX = 7.0
SELECT = 128
SCALE_FLOOR = 1e-8
LN_EPS = 1e-5
EXPONENT = 0x7F800000
ROUND_INT = 1.5 * 2.0 ** 23
ROUND_FP8 = 1.5 * 2.0 ** 20
ROUND_FP8_LEAST = ROUND_FP8 * 2.0 ** -6
W_TOP = 64.0


class Chain:

    def __init__(self, eng, sem, start, per_pass):
        self.eng, self.sem, self.start, self.per_pass, self.k = eng, sem, start, per_pass, 0

    def step(self, ins):
        ins.then_inc(self.sem, 1)
        self.k += 1
        self.eng.wait_ge(self.sem, self.start + self.k)

    def close(self):
        assert self.k == self.per_pass, (self.k, self.per_pass)


def flamingo_block(nc, x, ctx_in, w_gu_t, w_down_t, wq_t, wk_t, wv_t, cols, ri_in, ri_mid, out):
    TOK, N = x.shape
    HID = w_down_t.shape[0]
    CH = wv_t.shape[0]
    QK = wq_t.shape[1]
    TILES = TOK // P
    NT = N // P
    IT = -(-HID // P)
    NB, HB = N // BLK, HID // BLK
    GU = 2 * HID
    CHUNK = [464, 464, 448]
    CSTART = [0, 464, 928]
    PAIRS = TILES // 2
    assert sum(CHUNK) == HID and 2 * CH == P and 2 * QK == CH and NT == 4 and TOK % (2 * P) == 0

    def rows(it):
        return min(P, HID - it * P)

    wt_scratch = nc.dram_tensor("wt_scratch", (HID, 2 * N), F32, kind="Internal").ap()
    xt_scratch = nc.dram_tensor("xt_scratch", (N, TOK), F32, kind="Internal").ap()
    x1_scratch = nc.dram_tensor("x1_scratch", (TOK, N), F32, kind="Internal").ap()

    ctx = ExitStack()
    with ctx:
        def sb(name, shape, dt=F32):
            return ctx.enter_context(nc.sbuf_tensor(name, shape, dt))

        def sem(name):
            return ctx.enter_context(nc.semaphore(name))

        PS = ctx.enter_context(nc.psum_tensor("PS", [P, 8, 512], F32))

        w_hi = sb("w_hi", [P, NT * GU], F16)
        w_lo = sb("w_lo", [P, NT * GU], F16)
        wd_hi = sb("wd_hi", [P, IT * N], F16)
        wd_lo = sb("wd_lo", [P, IT * N], F16)
        H = sb("H", [P, TILES * HID])
        XG = sb("XG", [P, NT * TOK])
        ident = sb("ident", [P, P])
        col = sb("col", [P, 8])
        idx_in = sb("idx_in", [P, NT], I32)
        idx_mid = sb("idx_mid", [P, IT], I32)
        wq2, wk2 = (XG[:, NT * TOK - 256 + 64 * i:NT * TOK - 192 + 64 * i] for i in range(2))
        wv2 = XG[:, NT * TOK - 128:NT * TOK]
        sc = sb("sc", [P, 32])
        T1, T1G, T1GBV, T2 = (sc[:, i:i + 1] for i in range(4))
        W_MAX, W_POW, W_UP, W_DOWN = (sc[:, 4 + 2 * i:6 + 2 * i] for i in range(4))
        A_G, A_RG, A_C1, A_OUT = (sc[:, 12 + i:13 + i] for i in range(4))
        H_G, H_RG, H_C1, H_OUT, H_LIM = (sc[:, 16 + i:17 + i] for i in range(5))
        A_MAX, H_MAX = sc[:, 22:23], sc[:, 23:24]
        ZERO = sc[:, 24:25]
        mv = sb("mv", [P, TILES * 2])
        ln = sb("ln", [P, 5 * TILES])
        var, rstd, nmr, ln_a, ln_b = (ln[:, i * TILES:(i + 1) * TILES] for i in range(5))
        a_max = sb("a_max", [P, TILES])

        o = 0

        def in_h(n):
            nonlocal o
            o += n
            assert o <= TILES * HID
            return H[:, o - n:o]

        GT = in_h(NT * GU)
        WR = H[:, 0:IT * 2 * N]
        o = max(o, IT * 2 * N)
        WDG = in_h(IT * N)
        wst = [in_h(2 * N) for _ in range(2)]
        WDR = XG[:, 0:NT * HID]
        wsc = XG[:, NT * HID:NT * HID + 2 * (IT * 2 * NB + NT * HB)]
        NWB = IT * 2 * NB + NT * HB
        ws, wr = wsc[:, 0:NWB], wsc[:, NWB:2 * NWB]

        o = 0
        X = in_h(TILES * N)
        Pm = [in_h(2 * N) for _ in range(2)]
        PT = [in_h(NT * 2 * P) for _ in range(2)]
        q_sb = [in_h(N) for _ in range(2)]
        k_sb = [in_h(N) for _ in range(2)]
        vt = [in_h(N) for _ in range(2)]
        ct = [in_h(N) for _ in range(2)]
        z = [in_h(N) for _ in range(2)]
        xn = [in_h(N) for _ in range(2)]
        on = [in_h(N) for _ in range(2)]
        nmx = in_h(8 * 2)
        esum = in_h(8 * 2)
        rsum = in_h(8 * 2)
        xts = [in_h(N) for _ in range(2)]
        stats = in_h(TILES * 6)

        xg = [sb(f"xg{i}", [P, N]) for i in range(2)]
        qa_all = sb("qa_all", [P, 3 * N])
        qa = [qa_all[:, i * N:(i + 1) * N] for i in range(3)]
        a_blk = sb("a_blk", [P, 3 * NB])
        at_hi = [sb(f"at_hi{i}", [P, NT * P], F16) for i in range(2)]
        at_lo = [sb(f"at_lo{i}", [P, NT * P], F16) for i in range(2)]
        sg = [sb(f"sg{i}", [P, 464]) for i in range(2)]
        h_blk = sb("h_blk", [P, TILES * HB])
        h_rcp = qa_all[:, 0:TILES * HB]

        hm = XG[:, 0:HID]
        hA = [XG[:, (1 + i) * HID:(2 + i) * HID] for i in range(2)]
        o2 = 3 * HID
        ATW = IT * P
        ht_hi = [XG[:, o2 + i * ATW // 2:o2 + (i + 1) * ATW // 2].bitcast(F16) for i in range(2)]
        o2 += ATW
        ht_lo = [XG[:, o2 + i * ATW // 2:o2 + (i + 1) * ATW // 2].bitcast(F16) for i in range(2)]
        o2 += ATW
        assert o2 <= NT * TOK
        h_s, h_rs = XG[:, o2:o2 + HB], XG[:, o2 + HB:o2 + 2 * HB]

        s_cols = sem("s_cols")
        s_ld = sem("s_ld")
        s_ident0 = sem("s_ident0")
        s_ident = sem("s_ident")
        s_zero = sem("s_zero")
        s_w2 = sem("s_w2")
        s_gt = sem("s_gt")
        s_wdg = sem("s_wdg")
        s_wt = sem("s_wt")
        s_wst = sem("s_wst")
        s_wsd = [sem(f"s_wsd{i}") for i in range(2)]
        s_wr = sem("s_wr")
        s_dt = sem("s_dt")
        s_wdr = sem("s_wdr")
        s_wv = sem("s_wv")
        s_wmax = sem("s_wmax")
        s_wall = sem("s_wall")
        s_wq = sem("s_wq")
        s_wtq = sem("s_wtq")
        s_whi = sem("s_whi")
        s_wlo = sem("s_wlo")
        s_t = sem("s_t")
        s_lnv = sem("s_lnv")
        s_lna = sem("s_lna")
        s_ln1 = sem("s_ln1")

        block = ctx.enter_context(nc.Block())
        bc = lambda ap, nb: ap.rearrange("p (b o) -> p b o", o=1).broadcast_to([ap.shape[0], nb, BLK])
        blk = lambda ap: ap.rearrange("p (b e) -> p b e", e=BLK)

        s_ct = [sem(f"s_ct{i}") for i in range(2)]
        s_xn = [sem(f"s_xn{i}") for i in range(2)]
        s_prq = [sem(f"s_prq{i}") for i in range(2)]
        s_prk = [sem(f"s_prk{i}") for i in range(2)]
        s_prv = [sem(f"s_prv{i}") for i in range(2)]
        s_q = [sem(f"s_q{i}") for i in range(2)]
        s_k = [sem(f"s_k{i}") for i in range(2)]
        s_v = [sem(f"s_v{i}") for i in range(2)]
        s_e = [sem(f"s_e{i}") for i in range(2)]
        s_mx = [sem(f"s_mx{i}") for i in range(2)]
        s_p = [sem(f"s_p{i}") for i in range(2)]
        s_pt = [sem(f"s_pt{i}") for i in range(2)]
        s_pe = [sem(f"s_pe{i}") for i in range(2)]
        s_pv = [sem(f"s_pv{i}") for i in range(2)]
        s_rsum = [sem(f"s_rsum{i}") for i in range(2)]
        s_on = [sem(f"s_on{i}") for i in range(2)]
        s_ot = [sem(f"s_ot{i}") for i in range(2)]
        s_z1 = [sem(f"s_z1{i}") for i in range(2)]
        s_z = [sem(f"s_z{i}") for i in range(2)]
        s_x1 = [sem(f"s_x1{i}") for i in range(2)]
        s_x1d = sem("s_x1d")
        s_z2 = sem("s_z2")
        s_st2 = sem("s_st2")
        s_ln2 = sem("s_ln2")
        s_x2n = [sem(f"s_x2n{i}") for i in range(2)]
        s_x2t = [sem(f"s_x2t{i}") for i in range(2)]
        s_x2s = [sem(f"s_x2s{i}") for i in range(2)]
        s_x2d = [sem(f"s_x2d{i}") for i in range(2)]
        s_amax = sem("s_amax")
        s_aall = sem("s_aall")
        s_ag = sem("s_ag")
        s_xg = sem("s_xg")
        s_gc = [sem(f"s_gc{i}") for i in range(2)]
        s_gx = [sem(f"s_gx{i}") for i in range(2)]
        s_gq = sem("s_gq")
        s_ga = [sem(f"s_ga{i}") for i in range(2)]
        s_gt2 = [sem(f"s_gat{i}") for i in range(2)]
        s_ghi = [sem(f"s_ghi{i}") for i in range(2)]
        s_glo = [sem(f"s_glo{i}") for i in range(2)]
        s_gu = [sem(f"s_gu{i}") for i in range(2)]
        s_sg = [sem(f"s_sg{i}") for i in range(2)]
        s_h = [sem(f"s_h{i}") for i in range(2)]
        s_hb = sem("s_hb")
        s_hmax = sem("s_hmax")
        s_hall = sem("s_hall")
        s_hg = sem("s_hg")
        s_hq = sem("s_hq")
        s_hA = [sem(f"s_hA{i}") for i in range(2)]
        s_hT = [sem(f"s_hT{i}") for i in range(2)]
        s_hhi = [sem(f"s_hhi{i}") for i in range(2)]
        s_hlo = [sem(f"s_hlo{i}") for i in range(2)]
        s_y = [sem(f"s_y{i}") for i in range(2)]
        s_xl = [sem(f"s_xl{i}") for i in range(2)]
        s_f = [sem(f"s_f{i}") for i in range(2)]
        s_out = [sem(f"s_out{i}") for i in range(2)]


        def since(eng, sem, count):
            if not isinstance(count, int) or count > 0:
                eng.wait_ge(sem, count)

        def passes(eng, body, first=0):
            body(0)
            with eng.Fori(1, PAIRS) as ii:
                body(ii)

        def passes_peeled(eng, body):
            body(0, True, False)
            with eng.Fori(1, PAIRS - 1) as ii:
                body(ii, False, False)
            body(PAIRS - 1, False, True)

        def products_read(eng, ii, u):
            n = 3 * u + 2
            k = ii * 3 - 3 + n // 2 + 1
            since(eng, s_gu[n % 2], k)

        @block.sync
        def _(sp):
            sp.dma_start(idx_in[:, :], ri_in).then_inc(s_cols, 16)
            sp.dma_start(idx_mid[:, :], ri_mid).then_inc(s_cols, 16)
            sp.dma_start(col[:, :], cols).then_inc(s_cols, 16)
            sp.wait_ge(s_zero, 1)
            for h in range(2):
                lo, hi = h * CH, (h + 1) * CH
                sp.dma_start(wq2[lo:hi, h * QK:(h + 1) * QK], wq_t).then_inc(s_w2, 16)
                sp.dma_start(wk2[lo:hi, h * QK:(h + 1) * QK], wk_t).then_inc(s_w2, 16)
                sp.dma_start(wv2[lo:hi, lo:hi], wv_t).then_inc(s_w2, 16)
            for it in range(IT):
                sp.wait_ge(s_wst, it + 1)
                sp.dma_start(wt_scratch[it * P:it * P + rows(it), :], wst[it % 2][0:rows(it), :]).then_inc(s_wsd[it % 2], 16)
            sp.wait_ge(s_whi, IT * 2 + IT)
            sp.wait_ge(s_wlo, IT * 2 + IT)
            for t in range(TILES):
                sp.dma_start(X[:, t * N:(t + 1) * N], x[t * P:(t + 1) * P, :]).then_inc(s_ld, 16)
            def a_pass(ii):
                for u in range(2):
                    since(sp, s_z1[u], ii)
                    since(sp, s_prv[u], ii)
                    since(sp, s_prk[u], ii)
                    sp.dma_start(ct[u], ctx_in[bass.ds(ii * (2 * P) + u * P, P), :]).then_inc(s_ct[u], 16)

            passes(sp, a_pass)
            def a_pass(ii):
                for u in range(2):
                    since(sp, s_x1[u], ii + 1)
                    sp.dma_start(x1_scratch[bass.ds(ii * (2 * P) + u * P, P), :],
                                 X[:, bass.ds(ii * (2 * N) + u * N, N)]).then_inc(s_x1d, 16)

            passes(sp, a_pass)
            xt_v = xt_scratch.rearrange("(a p) t -> p a t", p=P)
            def a_pass(ii):
                for u in range(2):
                    since(sp, s_x2s[u], ii + 1)
                    sp.dma_start(xt_v[:, :, bass.ds(ii * (2 * P) + u * P, P)],
                                 xts[u].rearrange("p (a t) -> p a t", a=NT)).then_inc(s_x2d[u], 16)

            passes(sp, a_pass)
            sp.wait_ge(s_x1d, TILES * 16)
            for u in range(2):
                sp.wait_ge(s_gx[u], PAIRS)
            def a_pass(ii):
                for u in range(2):
                    since(sp, s_out[u], ii * 16)
                    sp.dma_start(xg[u][:, :], x1_scratch[bass.ds(ii * (2 * P) + u * P, P), :]).then_inc(s_xl[u], 16)
                for u in range(2):
                    since(sp, s_f[u], ii + 1)
                    sp.dma_start(out[bass.ds(ii * (2 * P) + u * P, P), :], xg[u][:, :]).then_inc(s_out[u], 16)

            passes(sp, a_pass)
            for u in range(2):
                sp.wait_ge(s_out[u], PAIRS * 16)
                sp.wait_ge(s_x2d[u], PAIRS * 16)
            sp.wait_ge(s_x1d, TILES * 16)

        @block.gpsimd
        def _(pool):
            nc.gpsimd.memset(wq2[:, :], 0.0)
            nc.gpsimd.memset(wk2[:, :], 0.0)
            nc.gpsimd.memset(sc[:, :], 0.0)
            nc.gpsimd.memset(wv2[:, :], 0.0).then_inc(s_zero, 1)
            nc.gpsimd.memset(ident[:, :], 0.0).then_inc(s_ident0, 1)
            pool.wait_ge(s_ident0, 1)
            nc.gpsimd.affine_select(out=ident[:, :], in_=ident[:, :], compare_op=ALU.not_equal, fill=1.0, base=0,
                                    pattern=[[-1, P]], channel_multiplier=1).then_inc(s_ident, 1)
            pool.wait_ge(s_cols, 48)
            for jt in range(NT):
                pool.indirect_dma_start(GT[:, jt * GU:(jt + 1) * GU], None, w_gu_t,
                                        bass.IndirectOffsetOnAxis(ap=idx_in[:, jt:jt + 1], axis=0)).then_inc(s_gt, 16)
            for it in range(IT):
                r = rows(it)
                pool.indirect_dma_start(WDG[0:r, it * N:(it + 1) * N], None, w_down_t,
                                        bass.IndirectOffsetOnAxis(ap=idx_mid[0:r, it:it + 1], axis=0)).then_inc(s_wdg, 16)
            for i in range(2):
                pool.wait_ge(s_wsd[i], 16 * len(range(i, IT, 2)))
            for it in range(IT):
                r = rows(it)
                pool.indirect_dma_start(WR[0:r, it * 2 * N:(it + 1) * 2 * N], None, wt_scratch,
                                        bass.IndirectOffsetOnAxis(ap=idx_mid[0:r, it:it + 1], axis=0)).then_inc(s_wr, 16)
            pool.wait_ge(s_wmax, 1)
            nc.gpsimd.partition_all_reduce(W_POW, W_MAX, P, RMAX).then_inc(s_wall, 1)
            pool.wait_ge(s_ln1, 1)
            def a_pass(ii):
                for u in range(2):
                    since(pool, s_ct[u], ii * 16 + 16)
                    since(pool, s_x1[u], ii)
                    nc.gpsimd.tensor_tensor(z[u], ct[u], T1.broadcast_to([P, N]), ALU.mult).then_inc(s_z1[u], 1)
                    since(pool, s_z1[u], ii + 1)
                    nc.gpsimd.tensor_tensor(z[u], z[u], T1GBV.broadcast_to([P, N]), ALU.add).then_inc(s_z2, 1)
                    since(pool, s_z2, ii * 2 + u + 1)
                    nc.gpsimd.tensor_tensor(z[u], z[u], X[:, bass.ds(ii * (2 * N) + u * N, N)],
                                            ALU.add).then_inc(s_z[u], 1)

            passes(pool, a_pass)
            pool.wait_ge(s_amax, 1)
            nc.gpsimd.partition_all_reduce(A_MAX, sc[:, 25:26], P, RMAX).then_inc(s_aall, 1)
            for i in range(2):
                pool.wait_ge(s_x2d[i], PAIRS * 16)
            for jt in range(NT):
                pool.indirect_dma_start(XG[:, jt * TOK:(jt + 1) * TOK], None, xt_scratch,
                                        bass.IndirectOffsetOnAxis(ap=idx_in[:, jt:jt + 1], axis=0)).then_inc(s_xg, 16)
            pool.wait_ge(s_xg, NT * 16)
            xg_v = XG[:, :].rearrange("p (a t) -> p a t", a=NT)
            def a_pass(ii):
                for u in range(2):
                    since(pool, s_gx[u], ii)
                    nc.gpsimd.tensor_copy(xg[u][:, :].rearrange("p (a t) -> p a t", a=NT),
                                          xg_v[:, :, bass.ds(ii * (2 * P) + u * P, P)]).then_inc(s_gc[u], 1)

            passes(pool, a_pass)
            pool.wait_ge(s_hmax, 1)
            nc.gpsimd.partition_all_reduce(H_MAX, sc[:, 26:27], P, RMAX).then_inc(s_hall, 1)

        @block.tensor
        def _(pe):
            pe.wait_ge(s_ident, 1)
            pe.wait_ge(s_gt, NT * 16)
            for it in range(IT):
                b = 2 * (it % 2)
                if it >= 2:
                    pe.wait_ge(s_wst, it - 1)
                r = rows(it)
                for w in range(2):
                    for jt in range(NT):
                        c = jt * GU + w * HID + it * P
                        last = nc.tensor.transpose(PS[0:r, b + w, jt * P:(jt + 1) * P], GT[:, c:c + r], ident[:, :])
                last.then_inc(s_wt, 1)
            pe.wait_ge(s_wdg, IT * 16)
            for ot in range(NT):
                if ot >= 1:
                    pe.wait_ge(s_wdr, ot)
                for it in range(IT):
                    r = rows(it)
                    last = nc.tensor.transpose(PS[:, 4 + it // 4, (it % 4) * P:(it % 4) * P + r],
                                               WDG[0:r, it * N + ot * P:it * N + (ot + 1) * P], ident[0:r, 0:r])
                last.then_inc(s_dt, 1)
            pe.wait_ge(s_wst, IT)
            n = 0
            for it in range(IT):
                pe.wait_ge(s_wq, it + 1)
                r = rows(it)
                for w in range(2):
                    if n >= 2:
                        pe.wait_ge(s_whi, n - 1)
                        pe.wait_ge(s_wlo, n - 1)
                    for jt in range(NT):
                        c = it * 2 * N + w * N + jt * P
                        last = nc.tensor.transpose(PS[:, n % 2, jt * P:jt * P + r], WR[0:r, c:c + P], ident[0:r, 0:r])
                    last.then_inc(s_wtq, 1)
                    n += 1
            pe.wait_ge(s_wq, IT + NT)
            for it in range(IT):
                r = rows(it)
                pe.wait_ge(s_whi, n - 1)
                pe.wait_ge(s_wlo, n - 1)
                for ot in range(NT):
                    last = nc.tensor.transpose(PS[0:r, n % 2, ot * P:(ot + 1) * P],
                                               WDR[:, ot * HID + it * P:ot * HID + it * P + r], ident[:, :])
                last.then_inc(s_wtq, 1)
                n += 1
            pe.wait_ge(s_whi, n)
            pe.wait_ge(s_wlo, n)

            pe.wait_ge(s_w2, 6 * 16)
            PR, OB = PS[:, 7, :], PS[:, 6, :]

            def project_q(ii, u):
                since(pe, s_xn[u], ii + 1)
                nc.tensor.matmul(PR[0:2 * QK, :], wq2[:, :], xn[u], start=True, stop=True).then_inc(s_prq[u], 1)

            def project_k(ii, u):
                since(pe, s_ct[u], ii * 16 + 16)
                since(pe, s_q[u], ii + 1)
                nc.tensor.matmul(PR[0:2 * QK, :], wk2[:, :], ct[u], start=True, stop=True).then_inc(s_prk[u], 1)

            def project_v(ii, u):
                since(pe, s_k[u], ii + 1)
                for mt in range(NT):
                    last = nc.tensor.matmul(PR[:, mt * P:(mt + 1) * P], ct[u][:, mt * P:(mt + 1) * P], wv2[:, :],
                                            start=True, stop=True)
                last.then_inc(s_prv[u], 1)

            def scores(ii, n):
                u, b, half, slot = n // 4, n // 2 % 2, n % 2, n % 2
                if n % 4 == 0:
                    since(pe, s_k[u], ii + 1)
                since(pe, s_p[slot], ii * 4 + n // 2)
                for j in range(2):
                    nt = 2 * half + j
                    last = nc.tensor.matmul(PS[:, 2 * slot + j, :],
                                            q_sb[u][b * QK:(b + 1) * QK, nt * P:(nt + 1) * P],
                                            k_sb[u][b * QK:(b + 1) * QK, :], start=True, stop=True)
                last.then_inc(s_e[slot], 1)

            def transposes(ii, n):
                slot = n % 2
                since(pe, s_p[slot], ii * 4 + n // 2 + 1)
                since(pe, s_pe[1 - slot], ii * 4 + (n + 1) // 2)
                for j in range(2):
                    for mt in range(NT):
                        last = nc.tensor.transpose(PS[:, 4 + mt // 2, (mt % 2) * 2 * P + j * P:(mt % 2) * 2 * P + (j + 1) * P],
                                                   Pm[slot][:, j * N + mt * P:j * N + (mt + 1) * P], ident[:, :])
                last.then_inc(s_pt[slot], 1)

            def product_v(ii, n):
                u, b, half, slot = n // 4, n // 2 % 2, n % 2, n % 2
                since(pe, s_pe[slot], ii * 4 + n // 2 + 1)
                if n % 4 == 0:
                    since(pe, s_v[u], ii + 1)
                    since(pe, s_on[1 - u], ii + u)
                for j in range(2):
                    nt = 2 * half + j
                    for mt in range(NT):
                        last = nc.tensor.matmul(OB[:, nt * P + b * CH:nt * P + (b + 1) * CH],
                                                PT[slot][:, mt * 2 * P + j * P:mt * 2 * P + (j + 1) * P],
                                                vt[u][:, mt * P + b * CH:mt * P + (b + 1) * CH],
                                                start=(mt == 0), stop=(mt == NT - 1))
                last.then_inc(s_pv[slot], 1)

            def out_transpose(ii, u):
                since(pe, s_on[u], ii + 1)
                for nt in range(NT):
                    last = nc.tensor.transpose(PR[:, nt * P:(nt + 1) * P], on[u][:, nt * P:(nt + 1) * P], ident[:, :])
                last.then_inc(s_ot[u], 1)

            def attention_pass(ii, first_pass, last_pass):
                for n in range(8):
                    u = n // 4
                    nxt = not (last_pass and u == 1)
                    iin, un = (ii, 1) if u == 0 else (ii + 1, 0)
                    if n < 7:
                        scores(ii, n + 1)
                    elif not last_pass:
                        scores(ii + 1, 0)
                    transposes(ii, n)
                    if n > 0:
                        product_v(ii, n - 1)
                    elif not first_pass:
                        product_v(ii - 1, 7)
                    if n % 4 == 1 and not (first_pass and u == 0):
                        ip, up = (ii - 1, 1) if u == 0 else (ii, 0)
                        out_transpose(ip, up)
                    if nxt:
                        if n % 4 == 1:
                            pass
                        if n % 4 == 2:
                            if not (first_pass and u == 0):
                                ip, up = (ii - 1, 1) if u == 0 else (ii, 0)
                                since(pe, s_x1[up], ip + 1)
                            project_q(iin, un)
                            project_k(iin, un)
                            project_v(iin, un)

            project_q(0, 0)
            project_k(0, 0)
            project_v(0, 0)
            scores(0, 0)
            passes_peeled(pe, attention_pass)
            product_v(PAIRS - 1, 7)
            pe.wait_ge(s_x1[0], PAIRS)
            out_transpose(PAIRS - 1, 1)

            def a_pass(ii):
                for u in range(2):
                    since(pe, s_x2n[u], ii + 1)
                    since(pe, s_x2s[u], ii)
                    for nt in range(NT):
                        last = nc.tensor.transpose(PS[:, u, nt * P:(nt + 1) * P], xn[u][:, nt * P:(nt + 1) * P], ident[:, :])
                    last.then_inc(s_x2t[u], 1)

            passes(pe, a_pass)
            for u in range(2):
                pe.wait_ge(s_x2s[u], PAIRS)

            def gathered_back(ii, u):
                since(pe, s_gc[u], ii + 1)
                since(pe, s_ga[u], ii)
                for jt in range(NT):
                    last = nc.tensor.transpose(PS[:, 4 + u, jt * P:(jt + 1) * P], xg[u][:, jt * P:(jt + 1) * P], ident[:, :])
                last.then_inc(s_gx[u], 1)

            def a_transpose(ii, u):
                since(pe, s_ga[u], ii + 1)
                since(pe, s_ghi[u], ii)
                since(pe, s_glo[u], ii)
                for jt in range(NT):
                    last = nc.tensor.transpose(PS[:, 6 + u, jt * P:(jt + 1) * P], qa[0][:, jt * P:(jt + 1) * P], ident[:, :])
                last.then_inc(s_gt2[u], 1)

            def gate_up(ii, u, c):
                n = 3 * u + c
                slot = n % 2
                since(pe, s_sg[slot], ii * 3 + n // 2)
                since(pe, s_h[slot], ii * 3 + n // 2)
                w_n = CHUNK[c]
                for w in range(2):
                    k = 0
                    for jt in range(NT):
                        for a, b in ((at_hi, w_hi), (at_hi, w_lo), (at_lo, w_hi)):
                            cc = jt * GU + w * HID + CSTART[c]
                            last = nc.tensor.matmul(PS[:, 2 * w + slot, 0:w_n], a[u][:, jt * P:(jt + 1) * P],
                                                    b[:, cc:cc + w_n], start=(k == 0), stop=(k == 3 * NT - 1))
                            k += 1
                last.then_inc(s_gu[slot], 1)

            def gate_up_pass(ii, first_pass, last_pass):
                for u in range(2):
                    nxt = not (last_pass and u == 1)
                    iin, un = (ii, 1) if u == 0 else (ii + 1, 0)
                    if nxt:
                        gathered_back(iin, un)
                    since(pe, s_ghi[u], ii + 1)
                    since(pe, s_glo[u], ii + 1)
                    gate_up(ii, u, 0)
                    gate_up(ii, u, 1)
                    if nxt:
                        a_transpose(iin, un)
                    gate_up(ii, u, 2)

            gathered_back(0, 0)
            a_transpose(0, 0)
            passes_peeled(pe, gate_up_pass)

            for slot in range(2):
                pe.wait_ge(s_sg[slot], PAIRS * 3)
                pe.wait_ge(s_h[slot], PAIRS * 3)

            def h_transpose(ii, u):
                since(pe, s_hA[u], ii + 1)
                since(pe, s_hhi[u], ii)
                since(pe, s_hlo[u], ii)
                for it in range(IT):
                    r = rows(it)
                    last = nc.tensor.transpose(PS[0:r, 3 * u + it // 4, (it % 4) * P:(it % 4 + 1) * P],
                                               hA[u][:, it * P:it * P + r], ident[:, :])
                last.then_inc(s_hT[u], 1)

            def down(ii, u):
                since(pe, s_hhi[u], ii + 1)
                since(pe, s_hlo[u], ii + 1)
                since(pe, s_f[u], ii)
                k = 0
                for it in range(IT):
                    r = rows(it)
                    for a, b in ((ht_hi, wd_hi), (ht_hi, wd_lo), (ht_lo, wd_hi)):
                        last = nc.tensor.matmul(PS[:, 6 + u, :], a[u][0:r, it * P:(it + 1) * P],
                                                b[0:r, it * N:(it + 1) * N], start=(k == 0), stop=(k == 3 * IT - 1))
                        k += 1
                last.then_inc(s_y[u], 1)

            h_transpose(0, 0)

            def down_pass(ii, first_pass, last_pass):
                h_transpose(ii, 1)
                down(ii, 0)
                if not last_pass:
                    h_transpose(ii + 1, 0)
                down(ii, 1)

            passes_peeled(pe, down_pass)

        @block.scalar
        def _(act):
            act.wait_ge(s_cols, 48)
            act.wait_ge(s_zero, 1)
            nc.scalar.activation(T1, col[:, 1:2], ACT.Tanh)
            nc.scalar.activation(T2, col[:, 2:3], ACT.Tanh).then_inc(s_t, 1)
            for it in range(IT):
                act.wait_ge(s_wt, it + 1)
                if it >= 2:
                    act.wait_ge(s_wsd[it % 2], 16 * (it // 2))
                r = rows(it)
                b = 2 * (it % 2)
                nc.scalar.copy(wst[it % 2][0:r, :].rearrange("p (w j) -> p w j", w=2),
                               PS[0:r, b:b + 2, :]).then_inc(s_wst, 1)
            ps_d = PS[:, 4:7, :].rearrange("p b c -> p (b c)")
            for ot in range(NT):
                act.wait_ge(s_dt, ot + 1)
                nc.scalar.copy(WDR[:, ot * HID:(ot + 1) * HID], ps_d[:, 0:HID]).then_inc(s_wdr, 1)
            n = 0
            for it in range(IT):
                r = rows(it)
                for w in range(2):
                    act.wait_ge(s_wtq, n + 1)
                    nc.scalar.copy(w_hi[:, :].rearrange("p (j w i) -> p j w i", j=NT, w=2)[:, :, w, it * P:it * P + r],
                                   PS[:, n % 2, :].rearrange("p (j i) -> p j i", j=NT)[:, :, 0:r]).then_inc(s_whi, 1)
                    n += 1
            for it in range(IT):
                r = rows(it)
                act.wait_ge(s_wtq, n + 1)
                nc.scalar.copy(wd_hi[0:r, it * N:(it + 1) * N], PS[0:r, n % 2, :]).then_inc(s_whi, 1)
                n += 1

            act.wait_ge(s_lnv, 1)
            nc.scalar.activation(ln_a, var, ACT.Sqrt).then_inc(s_lna, 1)

            PR = PS[:, 7, :]

            def evac_q(ii, u):
                since(act, s_prq[u], ii + 1)
                since(act, s_e[1], ii * 4 - 4 + 2 * u + 2 if not isinstance(ii, int) or ii else 0)
                nc.scalar.activation(q_sb[u][0:2 * QK, :], PR[0:2 * QK, :], ACT.Identity,
                                     bias=col[0:2 * QK, 4:5]).then_inc(s_q[u], 1)

            def evac_k(ii, u):
                since(act, s_prk[u], ii + 1)
                nc.scalar.activation(k_sb[u][0:2 * QK, :], PR[0:2 * QK, :], ACT.Identity,
                                     bias=col[0:2 * QK, 5:6]).then_inc(s_k[u], 1)

            def exps(ii, n, first_pass):
                slot = n % 2
                u = n // 4
                since(act, s_mx[slot], ii * 4 + n // 2 + 1)
                since(act, s_pt[slot], ii * 4 + n // 2)
                if n % 4 == 0:
                    since(act, s_rsum[u], ii)
                for j in range(2):
                    k = 2 * n + j
                    last = nc.scalar.activation(Pm[slot][:, j * N:(j + 1) * N], PS[:, 2 * slot + j, :], ACT.Exp,
                                                bias=nmx[:, k:k + 1], accum_out=esum[:, k:k + 1])
                last.then_inc(s_p[slot], 1)

            def attention_pass(ii, first_pass, last_pass):
                for n in range(8):
                    u = n // 4
                    exps(ii, n, first_pass)
                    nxt = not (last_pass and u == 1)
                    iin, un = (ii, 1) if u == 0 else (ii + 1, 0)
                    if nxt and n % 4 == 2:
                        evac_q(iin, un)
                        evac_k(iin, un)

            evac_q(0, 0)
            evac_k(0, 0)
            passes_peeled(act, attention_pass)

            act.wait_ge(s_lnv, 2)
            nc.scalar.activation(ln_a, var, ACT.Sqrt).then_inc(s_lna, 1)
            def a_pass(ii):
                for u in range(2):
                    since(act, s_x2t[u], ii + 1)
                    since(act, s_x2d[u], ii * 16)
                    nc.scalar.copy(xts[u], PS[:, u, :]).then_inc(s_x2s[u], 1)

            passes(act, a_pass)
            def a_hi(ii, u):
                since(act, s_gt2[u], ii + 1)
                products_read(act, ii, u)
                nc.scalar.copy(at_hi[u][:, :], PS[:, 6 + u, :]).then_inc(s_ghi[u], 1)

            def silu(ii, n):
                slot = n % 2
                w_n = CHUNK[n % 3]
                since(act, s_gu[slot], ii * 3 + n // 2 + 1)
                since(act, s_h[slot], ii * 3 + n // 2)
                nc.scalar.activation(sg[slot][:, 0:w_n], PS[:, slot, 0:w_n], ACT.Silu,
                                     scale=A_OUT).then_inc(s_sg[slot], 1)

            def gate_up_pass(ii, first_pass, last_pass):
                for u in range(2):
                    nxt = not (last_pass and u == 1)
                    iin, un = (ii, 1) if u == 0 else (ii + 1, 0)
                    silu(ii, 3 * u)
                    silu(ii, 3 * u + 1)
                    if nxt:
                        a_hi(iin, un)
                    silu(ii, 3 * u + 2)

            act.wait_ge(s_ag, 1)
            a_hi(0, 0)
            passes_peeled(act, gate_up_pass)

            def a_pass(ii):
                for u in range(2):
                    since(act, s_hT[u], ii + 1)
                    since(act, s_y[u], ii)
                    src = PS[:, 3 * u:3 * u + 3, :].rearrange("p b c -> p (b c)")
                    FULL = HID // P * P
                    nc.scalar.copy(ht_hi[u][:, 0:FULL], src[:, 0:FULL])
                    nc.scalar.copy(ht_hi[u][0:rows(IT - 1), FULL:FULL + P],
                                   src[0:rows(IT - 1), FULL:FULL + P]).then_inc(s_hhi[u], 1)

            passes(act, a_pass)
        @block.vector
        def _(dve):
            ts, tt, stt = nc.vector.tensor_scalar, nc.vector.tensor_tensor, nc.vector.scalar_tensor_tensor
            W1 = IT * 2 * NB
            wv = Chain(dve, s_wv, 0, 0)
            wv.step(nc.vector.memset(ws, 0.0))
            dve.wait_ge(s_wr, IT * 16)
            for it in range(IT):
                r = rows(it)
                last = nc.vector.tensor_reduce(ws[0:r, it * 2 * NB:(it + 1) * 2 * NB], blk(WR[0:r, it * 2 * N:(it + 1) * 2 * N]),
                                               AX_X, ALU.max, apply_absolute_value=True)
            dve.wait_ge(s_wdr, NT)
            wv.step(nc.vector.tensor_reduce(ws[:, W1:NWB], blk(WDR), AX_X, ALU.max, apply_absolute_value=True))
            dve.wait_ge(s_zero, 1)
            nc.vector.reduce_max(W_MAX[:, 0:1], ws[:, 0:W1], AX_X)
            nc.vector.reduce_max(W_MAX[:, 1:2], ws[:, W1:NWB], AX_X).then_inc(s_wmax, 1)
            dve.wait_ge(s_wmax, 1)
            wv.step(ts(ws, ws, 1.0 / INT4_MAX, SCALE_FLOOR, ALU.mult, ALU.max))
            wv.step(nc.vector.reciprocal(wr, ws))
            dve.wait_ge(s_wall, 1)
            wv.step(ts(W_POW, W_POW, 1e-30, None, ALU.max))
            wv.step(ts(W_POW.bitcast(I32), W_POW.bitcast(I32), EXPONENT, None, ALU.bitwise_and))
            wv.step(nc.vector.reciprocal(W_UP, W_POW))
            wv.step(ts(W_UP, W_UP, W_TOP, None, ALU.mult))
            wv.step(ts(W_DOWN, W_POW, 1.0 / W_TOP, None, ALU.mult))
            wv.step(ts(ws[:, 0:W1], ws[:, 0:W1], W_UP[:, 0:1], None, ALU.mult))
            wv.step(ts(ws[:, W1:NWB], ws[:, W1:NWB], W_UP[:, 1:2], None, ALU.mult))

            def quantise_w(w, r, b0, nb):
                wv.step(tt(blk(w), blk(w), bc(wr[0:r, b0:b0 + nb], nb), ALU.mult))
                wv.step(ts(w, w, INT4_MAX, ROUND_INT, ALU.min, ALU.add))
                stt(blk(w), blk(w), -ROUND_INT, bc(ws[0:r, b0:b0 + nb], nb), ALU.add, ALU.mult).then_inc(s_wq, 1)

            n = 0

            def lower_gu(it):
                nonlocal n
                r = rows(it)
                for w in range(2):
                    dve.wait_ge(s_whi, n + 1)
                    v = lambda a: a[:, :].rearrange("p (j w i) -> p j w i", j=NT, w=2)[:, :, w, it * P:it * P + r]
                    tt(v(w_lo), PS[:, n % 2, :].rearrange("p (j i) -> p j i", j=NT)[:, :, 0:r], v(w_hi),
                       ALU.subtract).then_inc(s_wlo, 1)
                    n += 1

            for it in range(IT):
                quantise_w(WR[0:rows(it), it * 2 * N:(it + 1) * 2 * N], rows(it), it * 2 * NB, 2 * NB)
                if it >= 1:
                    lower_gu(it - 1)
            lower_gu(IT - 1)
            for ot in range(NT):
                quantise_w(WDR[:, ot * HID:(ot + 1) * HID], P, W1 + ot * HB, HB)
            for it in range(IT):
                r = rows(it)
                dve.wait_ge(s_whi, n + 1)
                tt(wd_lo[0:r, it * N:(it + 1) * N], PS[0:r, n % 2, :], wd_hi[0:r, it * N:(it + 1) * N],
                   ALU.subtract).then_inc(s_wlo, 1)
                n += 1
            dve.wait_ge(s_t, 1)
            wv.step(tt(T1G, T1, col[:, 0:1], ALU.mult))
            wv.step(tt(T1GBV, T1G, col[:, 3:4], ALU.mult))

            def layernorm_scales(k):
                for t in range(TILES):
                    last = nc.vector.bn_aggr(mv[:, 2 * t:2 * t + 2], stats[:, 6 * t:6 * t + 6])
                wv.step(last)
                m3 = mv[:, :].rearrange("p (t s) -> p t s", s=2)
                ts(var, m3[:, :, 1], LN_EPS, None, ALU.add).then_inc(s_lnv, 1)
                since(dve, s_lnv, k)
                since(dve, s_lna, k)
                wv.step(nc.vector.reciprocal(rstd, ln_a))
                wv.step(tt(ln_b, rstd, rstd, ALU.mult))
                wv.step(tt(ln_b, ln_b, var, ALU.mult))
                wv.step(ts(ln_b, ln_b, -0.5, 1.5, ALU.mult, ALU.add))
                wv.step(tt(rstd, rstd, ln_b, ALU.mult))
                stt(nmr, m3[:, :, 0], -1.0, rstd, ALU.mult, ALU.mult).then_inc(s_ln1, 1)
                since(dve, s_ln1, k)

            for t in range(TILES):
                dve.wait_ge(s_ld, (t + 1) * 16) if t == TILES - 1 else None
            for t in range(TILES):
                last = nc.vector.bn_stats(stats[:, 6 * t:6 * t + 6], X[:, t * N:(t + 1) * N])
            wv.step(last)
            layernorm_scales(1)

            PR, OB = PS[:, 7, :], PS[:, 6, :]

            def normalise(ii, u):
                since(dve, s_prq[u], ii)
                t = ii * 2 + u
                ts(xn[u], X[:, bass.ds(t * N, N)], rstd[:, bass.ds(t, 1)], nmr[:, bass.ds(t, 1)],
                   ALU.mult, ALU.add).then_inc(s_xn[u], 1)

            def evac_v(ii, u):
                since(dve, s_prv[u], ii + 1)
                nc.vector.tensor_copy(vt[u], PR).then_inc(s_v[u], 1)

            def row_max(ii, n):
                slot = n % 2
                since(dve, s_e[slot], ii * 4 + n // 2 + 1)
                nc.vector.tensor_reduce(nmx[:, 2 * n:2 * n + 2], PS[:, 2 * slot:2 * slot + 2, :], AX_X, ALU.max,
                                        negate=True).then_inc(s_mx[slot], 1)

            def evac_pt(ii, n):
                slot = n % 2
                since(dve, s_pt[slot], ii * 4 + n // 2 + 1)
                since(dve, s_pv[slot], ii * 4 + n // 2)
                nc.vector.tensor_copy(PT[slot], PS[:, 4:6, :].rearrange("p b c -> p (b c)")).then_inc(s_pe[slot], 1)

            def attention_out(ii, u):
                since(dve, s_pv[1], ii * 4 + 2 * u + 2)
                nc.vector.reciprocal(rsum[:, 8 * u:8 * u + 8], esum[:, 8 * u:8 * u + 8]).then_inc(s_rsum[u], 1)
                since(dve, s_rsum[u], ii + 1)
                rb = rsum[:, 8 * u:8 * u + 8].rearrange("p (b n) -> p n b", b=2)
                for b in range(2):
                    v = lambda a: a.rearrange("p (n b c) -> p n b c", n=NT, b=2)[:, :, b, :]
                    last = tt(v(on[u]), v(OB), rb[:, :, b:b + 1].broadcast_to([P, NT, CH]), ALU.mult)
                last.then_inc(s_on[u], 1)

            def residual(ii, u):
                since(dve, s_ot[u], ii + 1)
                since(dve, s_z[u], ii + 1)
                t = ii * 2 + u
                stt(X[:, bass.ds(t * N, N)], PR, T1G, z[u], ALU.mult, ALU.add).then_inc(s_x1[u], 1)

            def attention_pass(ii, first_pass, last_pass):
                for n in range(8):
                    u = n // 4
                    nxt = not (last_pass and u == 1)
                    iin, un = (ii, 1) if u == 0 else (ii + 1, 0)
                    before = not (first_pass and u == 0)
                    ip, up = (ii - 1, 1) if u == 0 else (ii, 0)
                    if n < 7:
                        row_max(ii, n + 1)
                    elif not last_pass:
                        row_max(ii + 1, 0)
                    evac_pt(ii, n)
                    if n % 4 == 0 and before:
                        attention_out(ip, up)
                    if n % 4 == 1:
                        if before:
                            residual(ip, up)
                        if nxt:
                            normalise(iin, un)
                    if n % 4 == 2 and nxt:
                        evac_v(iin, un)

            normalise(0, 0)
            evac_v(0, 0)
            row_max(0, 0)
            passes_peeled(dve, attention_pass)
            attention_out(PAIRS - 1, 1)
            residual(PAIRS - 1, 1)
            for u in range(2):
                dve.wait_ge(s_x1[u], PAIRS)

            for t in range(TILES):
                last = nc.vector.bn_stats(stats[:, 6 * t:6 * t + 6], X[:, t * N:(t + 1) * N])
            wv.step(last)
            layernorm_scales(2)
            def a_pass(ii):
                for u in range(2):
                    t = ii * 2 + u
                    since(dve, s_x2t[u], ii)
                    ts(xn[u], X[:, bass.ds(t * N, N)], rstd[:, bass.ds(t, 1)], nmr[:, bass.ds(t, 1)],
                       ALU.mult, ALU.add).then_inc(s_x2n[u], 1)
                    since(dve, s_x2n[u], ii + 1)
                    last = nc.vector.tensor_reduce(a_max[:, bass.ds(t, 1)], xn[u], AX_X, ALU.max,
                                                   apply_absolute_value=True)
                    last.then_inc(s_st2, 1)

            passes(dve, a_pass)
            dve.wait_ge(s_st2, TILES)
            nc.vector.reduce_max(sc[:, 25:26], a_max[:, :], AX_X).then_inc(s_amax, 1)
            dve.wait_ge(s_aall, 1)

            def global_scale(M, g, rg, c1):
                wv.step(ts(g, M, 1.0 / (FP8_MAX * 6.0), SCALE_FLOOR, ALU.mult, ALU.max))
                wv.step(nc.vector.reciprocal(rg, g))
                wv.step(ts(c1, rg, 1.0 / FP8_MAX, None, ALU.mult))

            global_scale(A_MAX, A_G, A_RG, A_C1)
            tt(A_OUT, A_G, W_DOWN[:, 0:1], ALU.mult).then_inc(s_ag, 1)
            dve.wait_ge(s_ag, 1)

            OB_N = SELECT // BLK

            def second_quantisation(ch, A, v, rg, tmp):
                o_res, o_m = tmp[:, 0:SELECT], tmp[:, SELECT:2 * SELECT]
                o_s, o_rs = tmp[:, 2 * SELECT:2 * SELECT + OB_N], tmp[:, 2 * SELECT + OB_N:2 * SELECT + 2 * OB_N]
                ch.step(stt(o_res, v, rg, A, ALU.mult, ALU.subtract))
                ch.step(nc.vector.tensor_reduce(o_s, blk(o_res), AX_X, ALU.max, apply_absolute_value=True))
                ch.step(ts(o_s, o_s, 1.0 / FP8_MAX, SCALE_FLOOR, ALU.mult, ALU.max))
                ch.step(nc.vector.reciprocal(o_rs, o_s))
                ch.step(tt(blk(o_res), blk(o_res), bc(o_rs, OB_N), ALU.mult))
                ch.step(ts(o_m.bitcast(I32), o_res.bitcast(I32), EXPONENT, None, ALU.bitwise_and))
                ch.step(ts(o_m, o_m, ROUND_FP8, ROUND_FP8_LEAST, ALU.mult, ALU.max))
                ch.step(tt(o_res, o_res, o_m, ALU.add))
                ch.step(tt(o_res, o_res, o_m, ALU.subtract))
                ch.step(tt(blk(o_res), blk(o_res), bc(o_s, OB_N), ALU.mult))
                return tt(A, A, o_res, ALU.add)

            QA_STEPS = 20
            s_blk, sg_blk, rs_blk = (a_blk[:, i * NB:(i + 1) * NB] for i in range(3))

            def quantise_x(ii, u):
                ch = Chain(dve, s_gq, (ii * 2 + u) * QA_STEPS, QA_STEPS)
                src = PS[:, 4 + u, :]
                A, t, m = qa
                since(dve, s_gx[u], ii + 1)
                ch.step(nc.vector.tensor_reduce(s_blk, blk(src), AX_X, ALU.max, apply_absolute_value=True))
                ch.step(ts(s_blk, s_blk, A_C1, SCALE_FLOOR, ALU.mult, ALU.max))
                ch.step(ts(sg_blk, s_blk, A_G, None, ALU.mult))
                ch.step(nc.vector.reciprocal(rs_blk, sg_blk))
                ch.step(tt(blk(t), blk(src), bc(rs_blk, NB), ALU.mult))
                ch.step(ts(m.bitcast(I32), t.bitcast(I32), EXPONENT, None, ALU.bitwise_and))
                ch.step(ts(m, m, ROUND_FP8, ROUND_FP8_LEAST, ALU.mult, ALU.max))
                ch.step(tt(t, t, m, ALU.add))
                if u == 1:
                    since(dve, s_gt2[0], ii + 1)
                else:
                    since(dve, s_gt2[1], ii)
                ch.step(tt(t, t, m, ALU.subtract))
                ch.step(tt(blk(A), blk(t), bc(s_blk, NB), ALU.mult))
                second_quantisation(ch, A[:, N - SELECT:N], src[:, N - SELECT:N], A_RG, m).then_inc(s_ga[u], 1)
                ch.close()
                since(dve, s_ga[u], ii + 1)

            def a_lower(ii, u):
                since(dve, s_ghi[u], ii + 1)
                products_read(dve, ii, u)
                tt(at_lo[u][:, :], PS[:, 6 + u, :], at_hi[u][:, :], ALU.subtract).then_inc(s_glo[u], 1)

            def hidden(ii, n):
                slot, u, c = n % 2, n // 3, n % 3
                w_n = CHUNK[c]
                since(dve, s_sg[slot], ii * 3 + n // 2 + 1)
                t = ii * 2 + u
                stt(H[:, bass.ds(t * HID + CSTART[c], w_n)], PS[:, 2 + slot, 0:w_n], A_OUT, sg[slot][:, 0:w_n],
                    ALU.mult, ALU.mult).then_inc(s_h[slot], 1)

            def hidden_max(ii, u):
                for slot in range(2):
                    n = 3 * u + 2
                    k = ii * 3 + (n // 2 + 1 if slot == n % 2 else (n + 1) // 2)
                    since(dve, s_h[slot], k)
                t = ii * 2 + u
                hb = h_blk[:, bass.ds(t * HB, HB)]
                nc.vector.tensor_reduce(hb, blk(H[:, bass.ds(t * HID, HID)]), AX_X, ALU.max,
                                        apply_absolute_value=True).then_inc(s_hb, 1)

            def gate_up_pass(ii, first_pass, last_pass):
                for u in range(2):
                    nxt = not (last_pass and u == 1)
                    iin, un = (ii, 1) if u == 0 else (ii + 1, 0)
                    if nxt:
                        quantise_x(iin, un)
                    hidden(ii, 3 * u)
                    hidden(ii, 3 * u + 1)
                    if nxt:
                        a_lower(iin, un)
                    hidden(ii, 3 * u + 2)
                    hidden_max(ii, u)

            quantise_x(0, 0)
            a_lower(0, 0)
            for i in range(2):
                dve.wait_ge(s_x2t[i], PAIRS)
                dve.wait_ge(s_x2d[i], PAIRS * 16)
            dve.wait_ge(s_x1d, TILES * 16)
            passes_peeled(dve, gate_up_pass)

            dve.wait_ge(s_hb, TILES)
            nc.vector.reduce_max(sc[:, 26:27], h_blk[:, :], AX_X).then_inc(s_hmax, 1)
            dve.wait_ge(s_hmax, 1)
            wv.step(ts(h_rcp, h_blk[:, :], 1e-30, None, ALU.max))
            wv.step(nc.vector.reciprocal(h_rcp, h_rcp))
            dve.wait_ge(s_hall, 1)
            global_scale(H_MAX, H_G, H_RG, H_C1)
            wv.step(ts(H_LIM, H_RG, 1.0 / SCALE_FLOOR, None, ALU.mult))
            wv.step(tt(H_OUT, H_G, W_DOWN[:, 1:2], ALU.mult))
            wv.step(tt(H_OUT, H_OUT, T2, ALU.mult))
            dve.wait_ge(s_gc[1], PAIRS)

            HQ_STEPS = 17

            def quantise_h(ii, u):
                t = ii * 2 + u
                ch = Chain(dve, s_hq, t * HQ_STEPS, HQ_STEPS)
                hv = H[:, bass.ds(t * HID, HID)]
                A = hA[u]
                nc.vector.tensor_scalar(h_s, h_blk[:, bass.ds(t * HB, HB)], H_C1, SCALE_FLOOR, ALU.mult, ALU.max)
                ch.step(ts(h_rs, h_rcp[:, bass.ds(t * HB, HB)], FP8_MAX, H_LIM, ALU.mult, ALU.min))
                since(dve, s_hT[u], ii)
                ch.step(tt(blk(A), blk(hv), bc(h_rs, HB), ALU.mult))
                ch.step(ts(hm.bitcast(I32), A.bitcast(I32), EXPONENT, None, ALU.bitwise_and))
                ch.step(ts(hm, hm, ROUND_FP8, ROUND_FP8_LEAST, ALU.mult, ALU.max))
                ch.step(tt(A, A, hm, ALU.add))
                ch.step(tt(A, A, hm, ALU.subtract))
                ch.step(tt(blk(A), blk(A), bc(h_s, HB), ALU.mult))
                ho = H[:, bass.ds(t * HID + HID - SELECT, SELECT)]
                second_quantisation(ch, A[:, HID - SELECT:HID], ho, H_RG, hm).then_inc(s_hA[u], 1)
                ch.close()
                since(dve, s_hA[u], ii + 1)

            def h_lower(ii, u):
                since(dve, s_hhi[u], ii + 1)
                src = PS[:, 3 * u:3 * u + 3, :].rearrange("p b c -> p (b c)")
                FULL, r = HID // P * P, rows(IT - 1)
                since(dve, s_y[u], ii)
                tt(ht_lo[u][:, 0:FULL], src[:, 0:FULL], ht_hi[u][:, 0:FULL], ALU.subtract)
                tt(ht_lo[u][0:r, FULL:FULL + P], src[0:r, FULL:FULL + P], ht_hi[u][0:r, FULL:FULL + P],
                   ALU.subtract).then_inc(s_hlo[u], 1)

            def final(ii, u):
                since(dve, s_y[u], ii + 1)
                since(dve, s_xl[u], ii * 16 + 16)
                stt(xg[u][:, :], PS[:, 6 + u, :], H_OUT, xg[u][:, :], ALU.mult, ALU.add).then_inc(s_f[u], 1)

            quantise_h(0, 0)
            h_lower(0, 0)

            def down_pass(ii, first_pass, last_pass):
                quantise_h(ii, 1)
                h_lower(ii, 1)
                final(ii, 0)
                if not last_pass:
                    quantise_h(ii + 1, 0)
                    h_lower(ii + 1, 0)
                final(ii, 1)

            passes_peeled(dve, down_pass)


def kernel(x, ctx_4096, g_xattn, g_ffn, L0_xattn_Wq, L0_xattn_bq, L0_xattn_Wk, L0_xattn_bk, L0_xattn_Wv,
           L0_xattn_bv, L0_xattn_gamma, L0_ffn_w_gate, L0_ffn_w_up, L0_ffn_w_down, L0_ffn_ri_in, L0_ffn_ri_mid):
    import numpy as np
    import concourse.bacc as bacc
    from concourse.bass_utils import run_bass_kernel_spmd

    B, C, N = x.shape
    HID = L0_ffn_w_down.shape[1]
    IT = -(-HID // P)
    x, ctx_in = np.asarray(x), np.asarray(ctx_4096)
    cols = np.zeros((P, 8), np.float32)
    cols[:, 0] = np.asarray(L0_xattn_gamma)[0]
    cols[:, 1] = np.asarray(g_xattn)[0]
    cols[:, 2] = np.asarray(g_ffn)[0]
    cols[:, 3] = np.tile(np.asarray(L0_xattn_bv), 2)
    cols[:C, 4] = np.tile(np.asarray(L0_xattn_bq), 2)
    cols[:C, 5] = np.tile(np.asarray(L0_xattn_bk), 2)
    mid = np.zeros(IT * P, np.int32)
    mid[:HID] = np.asarray(L0_ffn_ri_mid)
    arrays = {
        "x": np.ascontiguousarray(x.reshape(B * C, N)),
        "ctx_in": np.ascontiguousarray(ctx_in.reshape(B * C, N)),
        "w_gu_t": np.ascontiguousarray(np.concatenate([np.asarray(L0_ffn_w_gate).T, np.asarray(L0_ffn_w_up).T], axis=1)),
        "w_down_t": np.ascontiguousarray(np.asarray(L0_ffn_w_down).T),
        "wq_t": np.ascontiguousarray(np.asarray(L0_xattn_Wq).T),
        "wk_t": np.ascontiguousarray(np.asarray(L0_xattn_Wk).T),
        "wv_t": np.ascontiguousarray(np.asarray(L0_xattn_Wv).T),
        "cols": cols,
        "ri_in": np.ascontiguousarray(np.asarray(L0_ffn_ri_in).reshape(-1, P).T),
        "ri_mid": np.ascontiguousarray(mid.reshape(-1, P).T),
    }
    nc = bacc.Bacc("TRN2", target_bir_lowering=False, num_devices=1)
    args = {k: nc.dram_tensor(f"in_{k}", a.shape, mybir.dt.from_np(a.dtype), kind="ExternalInput").ap()
            for k, a in arrays.items()}
    out = nc.dram_tensor("out_y", (B * C, N), F32, kind="ExternalOutput").ap()
    flamingo_block(nc, *args.values(), out)
    r = run_bass_kernel_spmd(nc, [{f"in_{k}": a for k, a in arrays.items()}], core_ids=[0])
    return r.results[0]["out_y"].reshape(B, C, N)
```

```python
import math
from contextlib import ExitStack

import concourse.bass as bass
from concourse import mybir

ALU = mybir.AluOpType
ACT = mybir.ActivationFunctionType
AX_X = mybir.AxisListType.X
F32 = mybir.dt.float32
F16 = mybir.dt.float16
I32 = mybir.dt.int32
RMAX = bass.bass_isa.ReduceOp.max

P = 128
BLK = 16
FP8_MAX = 448.0
INT4_MAX = 7.0
SELECT = 128
SCALE_FLOOR = 1e-8
LN_EPS = 1e-5
LN_P_SCALE = 10 * math.log(2)
EXPONENT = 0x7F800000
ROUND_INT = 1.5 * 2.0 ** 23
ROUND_FP8 = 1.5 * 2.0 ** 20
ROUND_FP8_LEAST = ROUND_FP8 * 2.0 ** -6
W_TOP = 16.0


class Chain:

    def __init__(self, eng, sem, start, per_pass):
        self.eng, self.sem, self.start, self.per_pass, self.k = eng, sem, start, per_pass, 0

    def mark(self, ins):
        ins.then_inc(self.sem, 1)
        self.k += 1
        return self.start + self.k

    def step(self, ins):
        self.eng.wait_ge(self.sem, self.mark(ins))

    def wait(self):
        self.eng.wait_ge(self.sem, self.start + self.k)

    def close(self):
        assert self.k == self.per_pass, (self.k, self.per_pass)


def flamingo_block(nc, x, ctx_in, w_gu_t, w_down_t, wq_t, wk_t, wv_t, cols, ri_in, ri_mid, out):
    TOK, N = x.shape
    HID = w_down_t.shape[0]
    CH = wv_t.shape[0]
    QK = wq_t.shape[1]
    TILES = TOK // P
    NT = N // P
    IT = -(-HID // P)
    NB, HB = N // BLK, HID // BLK
    GU = 2 * HID
    CHUNK = [464, 464, 448]
    CSTART = [0, 464, 928]
    PAIRS = TILES // 2
    assert sum(CHUNK) == HID and 2 * CH == P and 2 * QK == CH and NT == 4 and TOK % (2 * P) == 0

    def rows(it):
        return min(P, HID - it * P)

    wt_scratch = nc.dram_tensor("wt_scratch", (HID, 2 * N), F32, kind="Internal").ap()
    HALF = TOK // 2
    xt_scratch = [nc.dram_tensor(f"xt_scratch{i}", (N, HALF), F32, kind="Internal").ap() for i in range(2)]
    x1_scratch = nc.dram_tensor("x1_scratch", (TOK, N), F32, kind="Internal").ap()

    ctx = ExitStack()
    with ctx:
        def sb(name, shape, dt=F32):
            return ctx.enter_context(nc.sbuf_tensor(name, shape, dt))

        def sem(name):
            return ctx.enter_context(nc.semaphore(name))

        PS = ctx.enter_context(nc.psum_tensor("PS", [P, 8, 512], F32))

        GT = sb("w_gu", [P, NT * GU])
        w_hi = GT[:, 0:NT * GU // 2].bitcast(F16)
        w_lo = GT[:, NT * GU // 2:NT * GU].bitcast(F16)
        WDG = sb("w_down", [P, IT * N])
        wd_hi = WDG[:, 0:IT * N // 2].bitcast(F16)
        wd_lo = WDG[:, IT * N // 2:IT * N].bitcast(F16)
        H = sb("H", [P, TILES * HID])
        XG = sb("XG", [P, NT * TOK])
        ident = sb("ident", [P, P])
        col = sb("col", [P, 8])
        idx_in = sb("idx_in", [P, NT], I32)
        idx_mid = sb("idx_mid", [P, IT], I32)
        wq2, wk2 = (XG[:, NT * TOK - 256 + 64 * i:NT * TOK - 192 + 64 * i] for i in range(2))
        wv2 = XG[:, NT * TOK - 128:NT * TOK]
        sc = sb("sc", [P, 32])
        T1, T1G, T1GBV, T2 = (sc[:, i:i + 1] for i in range(4))
        W_MAX, W_POW, W_UP, W_DOWN = (sc[:, 4 + 2 * i:6 + 2 * i] for i in range(4))
        A_G, A_RG, A_C1, A_OUT = (sc[:, 12 + i:13 + i] for i in range(4))
        H_G, H_RG, H_C1, H_OUT, H_LIM = (sc[:, 16 + i:17 + i] for i in range(5))
        A_MAX, H_MAX = sc[:, 22:23], sc[:, 23:24]
        NEG_LEAST, ROUND = sc[:, 28:29], sc[:, 29:30]
        ln = sb("ln", [P, 7 * TILES])
        mv = ln[:, 5 * TILES:7 * TILES]
        var, rstd, nmr, ln_a, ln_b = (ln[:, i * TILES:(i + 1) * TILES] for i in range(5))
        a_max = sb("a_max", [P, TILES])

        xg = [sb(f"xg{i}", [P, N]) for i in range(2)]
        qa_all = sb("qa_all", [P, 3 * N])
        mixed = sb("mixed", [P, 2 * NT * P + 2 * 464])

        def cut(buf, n, taken={}):
            lo = taken.get(buf.name, 0)
            taken[buf.name] = lo + n
            assert lo + n <= buf.shape[1]
            return buf[:, lo:lo + n]

        WR = H[:, 0:IT * 2 * N]
        wst = [WR[:, it * 2 * N:(it + 1) * 2 * N] for it in range(IT)]
        WDR = XG[:, 0:NT * HID]
        NWB = IT * 2 * NB + NT * HB
        wsc = XG[:, NT * HID:NT * HID + 2 * NWB]
        ws, wr = wsc[:, 0:NWB], wsc[:, NWB:2 * NWB]
        assert NT * HID + 2 * NWB <= NT * TOK - 256

        X0 = (TILES * HID - TILES * N)
        X = H[:, X0:]
        h_at = 0

        def in_h(n):
            nonlocal h_at
            h_at += n
            assert h_at <= X0
            return H[:, h_at - n:h_at]

        qk_hl = [XG[:, (8 + 2 * i) * N:(10 + 2 * i) * N].bitcast(F16) for i in range(2)]
        p32 = [in_h(2 * N) for _ in range(2)]
        z0 = [in_h(N) for _ in range(2)]
        z = [in_h(N) for _ in range(2)]
        on = [in_h(N) for _ in range(2)]
        xts = [in_h(N) for _ in range(4)]
        p_hi = [in_h(N).bitcast(F16) for _ in range(4)]
        p_lo = [in_h(N).bitcast(F16) for _ in range(4)]
        assert h_at <= IT * 2 * N
        h_at = IT * 2 * N
        q_st = [in_h(N // 2).bitcast(F16) for _ in range(4)]
        k_st = [in_h(N // 2).bitcast(F16) for _ in range(4)]
        assert h_at == IT * 2 * N + 4 * N
        stats = in_h(TILES * 6)
        xn = [xg[i][:, :] for i in range(2)]
        ct = [cut(qa_all, N) for _ in range(2)]
        VW = NT * 2 * (CH + 1)
        v_hi = [cut(mixed, VW // 2 + 4).bitcast(F16) for _ in range(2)]
        v_lo = [cut(mixed, VW // 2 + 4).bitcast(F16) for _ in range(2)]
        nmx = cut(mixed, 4 * 2)
        nm16 = cut(mixed, 4 * 2).bitcast(F16)
        rsum = cut(mixed, 4 * 2)
        ident16 = cut(mixed, P // 2).bitcast(F16)

        qa = [qa_all[:, i * N:(i + 1) * N] for i in range(3)]
        a_blk = sb("a_blk", [P, 4 * NB])
        at_hi = [mixed[:, i * NT * P // 2:(i + 1) * NT * P // 2].bitcast(F16) for i in range(2)]
        at_lo = [mixed[:, (2 + i) * NT * P // 2:(3 + i) * NT * P // 2].bitcast(F16) for i in range(2)]
        sg = [mixed[:, 2 * NT * P + 464 * i:2 * NT * P + 464 * (i + 1)] for i in range(2)]
        h_blk = sb("h_blk", [P, TILES * HB])
        h_top = sb("h_top", [P, TILES])
        rc_tmp = ln[:, 0:HB]

        hA = [XG[:, i * HID:(i + 1) * HID] for i in range(2)]
        hm = [XG[:, (2 + i) * HID:(3 + i) * HID] for i in range(2)]
        ATW = IT * P
        ht_hi = [qa_all[:, i * ATW // 2:(i + 1) * ATW // 2].bitcast(F16) for i in range(2)]
        ht_lo = [mixed[:, i * ATW // 2:(i + 1) * ATW // 2].bitcast(F16) for i in range(2)]
        y_out = [GT[:, i * N:(i + 1) * N] for i in range(2)]
        h_tmp = XG[:, 4 * HID:4 * HID + 2 * SELECT + 2 * SELECT // BLK]
        RCP = (NT - 1) * TOK
        assert 4 * HID + 2 * SELECT + 2 * SELECT // BLK <= RCP and HB <= P

        s_cols = sem("s_cols")
        s_ld = sem("s_ld")
        s_ident0 = sem("s_ident0")
        s_ident = sem("s_ident")
        s_zero = sem("s_zero")
        s_w2 = sem("s_w2")
        s_gt = sem("s_gt")
        s_wdg = sem("s_wdg")
        s_wt = sem("s_wt")
        s_wst = sem("s_wst")
        s_wrc = sem("s_wrc")
        s_wmul = sem("s_wmul")
        s_wround = sem("s_wround")
        s_wsd = sem("s_wsd")
        s_wr = sem("s_wr")
        s_dt = sem("s_dt")
        s_wdr = sem("s_wdr")
        s_wv = sem("s_wv")
        s_wmax = sem("s_wmax")
        s_wall = sem("s_wall")
        s_wup = sem("s_wup")
        s_wq = sem("s_wq")
        s_wtq = sem("s_wtq")
        s_whi = sem("s_whi")
        s_wlo = sem("s_wlo")
        s_t = sem("s_t")
        s_lnv = sem("s_lnv")
        s_lna = sem("s_lna")
        s_ln1 = sem("s_ln1")

        block = ctx.enter_context(nc.Block())
        bc = lambda ap, nb: ap.rearrange("p (b o) -> p b o", o=1).broadcast_to([ap.shape[0], nb, BLK])
        blk = lambda ap: ap.rearrange("p (b e) -> p b e", e=BLK)

        s_ct = [sem(f"s_ct{i}") for i in range(2)]
        s_xn = [sem(f"s_xn{i}") for i in range(2)]
        s_prq = sem("s_prq")
        s_prk = sem("s_prk")
        s_prv = sem("s_prv")
        s_qh = sem("s_qh")
        s_ql = sem("s_ql")
        s_kh = sem("s_kh")
        s_kl = sem("s_kl")
        s_vh = sem("s_vh")
        s_vl = sem("s_vl")
        s_one = sem("s_one")
        s_st = [sem(f"s_stack{i}") for i in range(4)]
        s_e = [sem(f"s_e{i}") for i in range(2)]
        s_mx = [sem(f"s_mx{i}") for i in range(2)]
        s_nmh = sem("s_nmh")
        s_nm = sem("s_nm")
        s_row = sem("s_row")
        s_rowe = sem("s_rowe")
        s_et = [sem(f"s_et{i}") for i in range(2)]
        s_p = [sem(f"s_p{i}") for i in range(2)]
        s_phi = [sem(f"s_phi{i}") for i in range(2)]
        s_plo = [sem(f"s_plo{i}") for i in range(2)]
        s_pv = [sem(f"s_pv{i}") for i in range(2)]
        s_rsum = sem("s_rsum")
        s_on = sem("s_on")
        s_ot = [sem(f"s_ot{i}") for i in range(2)]
        s_z0 = [sem(f"s_z0{i}") for i in range(2)]
        s_z = [sem(f"s_z{i}") for i in range(2)]
        s_x1 = [sem(f"s_x1{i}") for i in range(2)]
        s_x1d = sem("s_x1d")
        s_st2 = sem("s_st2")
        s_x2n = sem("s_x2n")
        s_x2t = sem("s_x2t")
        s_x2s = sem("s_x2s")
        s_x2d = [sem(f"s_x2d{i}") for i in range(4)]
        s_amax = sem("s_amax")
        s_aall = sem("s_aall")
        s_ag = sem("s_ag")
        s_xg = [sem(f"s_xg{i}") for i in range(2)]
        s_gc = [sem(f"s_gc{i}") for i in range(2)]
        s_gx = [sem(f"s_gx{i}") for i in range(2)]
        s_g1 = sem("s_g1")
        s_g2 = sem("s_g2")
        s_gm = [sem(f"s_gm{i}") for i in range(2)]
        s_gm2 = [sem(f"s_gm2{i}") for i in range(2)]
        s_gr = [sem(f"s_gr{i}") for i in range(2)]
        s_go = [sem(f"s_go{i}") for i in range(2)]
        s_gA0 = [sem(f"s_gA0{i}") for i in range(2)]
        s_ga = [sem(f"s_ga{i}") for i in range(2)]
        s_gt2 = [sem(f"s_gat{i}") for i in range(2)]
        s_ghi = [sem(f"s_ghi{i}") for i in range(2)]
        s_glo = [sem(f"s_glo{i}") for i in range(2)]
        s_gu = [sem(f"s_gu{i}") for i in range(2)]
        s_sg = [sem(f"s_sg{i}") for i in range(2)]
        s_h = [sem(f"s_h{i}") for i in range(2)]
        s_hb = sem("s_hb")
        s_hrc = sem("s_hrc")
        s_htop = sem("s_htop")
        s_hmax = sem("s_hmax")
        s_hall = sem("s_hall")
        s_hround = sem("s_hround")
        s_houtl = sem("s_houtl")
        s_ht = [sem(f"s_ht{i}") for i in range(2)]
        s_hm = [sem(f"s_hm{i}") for i in range(2)]
        s_hm2 = [sem(f"s_hm2{i}") for i in range(2)]
        s_hr = [sem(f"s_hr{i}") for i in range(2)]
        s_ho = [sem(f"s_ho{i}") for i in range(2)]
        s_hA0 = [sem(f"s_hA0{i}") for i in range(2)]
        s_hsc = sem("s_hsc")
        s_hA = [sem(f"s_hA{i}") for i in range(2)]
        s_hT = [sem(f"s_hT{i}") for i in range(2)]
        s_hhi = [sem(f"s_hhi{i}") for i in range(2)]
        s_hlo = [sem(f"s_hlo{i}") for i in range(2)]
        s_y = [sem(f"s_y{i}") for i in range(2)]
        s_ys = sem("s_ys")
        s_xl = [sem(f"s_xl{i}") for i in range(2)]
        s_f = [sem(f"s_f{i}") for i in range(2)]
        s_out = [sem(f"s_out{i}") for i in range(2)]


        def since(eng, sem, count):
            if not isinstance(count, int) or count > 0:
                eng.wait_ge(sem, count)

        def passes(eng, body, first=0):
            body(0)
            with eng.Fori(1, PAIRS) as ii:
                body(ii)

        def passes_peeled(eng, body):
            body(0, True, False)
            with eng.Fori(1, PAIRS - 1) as ii:
                body(ii, False, False)
            body(PAIRS - 1, False, True)

        def passes_ahead(eng, body):
            body(0, 2)
            with eng.Fori(1, PAIRS - 2) as ii:
                body(ii, 2)
            body(PAIRS - 2, 1)
            body(PAIRS - 1, 0)

        def later(ii, u, d):
            return ii + (u + d) // 2, (u + d) % 2, (u + d) // 2

        def products_read(eng, ii, u):
            n = 3 * u + 2
            k = ii * 3 - 3 + n // 2 + 1
            since(eng, s_gu[n % 2], k)

        E = TILES // 2
        W1 = IT * 2 * NB
        w_items = [(WDR[:, ot * HID:(ot + 1) * HID], P, W1 + ot * HB, HB) for ot in range(NT)] + \
                  [(wst[it][0:rows(it), :], rows(it), it * 2 * NB, 2 * NB) for it in range(IT)]

        @block.sync
        def _(sp):
            sp.dma_start(idx_in[:, :], ri_in).then_inc(s_cols, 16)
            sp.dma_start(idx_mid[:, :], ri_mid).then_inc(s_cols, 16)
            sp.dma_start(col[:, :], cols).then_inc(s_cols, 16)
            sp.wait_ge(s_zero, 1)
            for h in range(2):
                lo, hi = h * CH, (h + 1) * CH
                sp.dma_start(wq2[lo:hi, h * QK:(h + 1) * QK], wq_t).then_inc(s_w2, 16)
                sp.dma_start(wk2[lo:hi, h * QK:(h + 1) * QK], wk_t).then_inc(s_w2, 16)
                sp.dma_start(wv2[lo:hi, lo:hi], wv_t).then_inc(s_w2, 16)
            sp.wait_ge(s_gt, NT * 16)
            for t in range(TILES):
                sp.dma_start(X[:, t * N:(t + 1) * N], x[t * P:(t + 1) * P, :]).then_inc(s_ld, 16)
            for it in range(IT):
                sp.wait_ge(s_wq, NT + it + 1)
                sp.dma_start(wt_scratch[it * P:it * P + rows(it), :], wst[it][0:rows(it), :]).then_inc(s_wsd, 16)
            def load_ctx(ii, u):
                src = ctx_in[bass.ds(ii * (2 * P) + u * P, P), :]
                since(sp, s_z0[u], ii)
                since(sp, s_prv, ii * 2 + u - 1)
                since(sp, s_prk, ii * 2 + u - 1)
                sp.dma_start(ct[u], src).then_inc(s_ct[u], 16)

            def stack(ii, u, b):
                n = 2 * u + b
                if b == 0:
                    since(sp, s_prk, ii * 2 + u + 1)
                else:
                    since(sp, s_et[1], ii * 4 + n - 3)
                r = slice(b * QK, (b + 1) * QK)
                qh, ql, kh, kl = (qk_hl[u][r, i * N:(i + 1) * N] for i in range(4))
                for dst, parts in ((q_st[n], (qh, qh, ql)), (k_st[n], (kh, kl, kh))):
                    if b == 0 and dst is k_st[n]:
                        since(sp, s_kl, ii * 2 + u + 1)
                    for i, part in enumerate(parts):
                        sp.dma_start(dst[i * QK:(i + 1) * QK, :], part).then_inc(s_st[n], 16)

            def store_x1(ii, u):
                made = ii + 1
                dst, src = x1_scratch[bass.ds(ii * (2 * P) + u * P, P), :], X[:, bass.ds(ii * (2 * N) + u * N, N)]
                since(sp, s_x1[u], made)
                sp.dma_start(dst, src).then_inc(s_x1d, 16)

            def attention_pass(ii, ahead):
                for u in range(2):
                    i2, u2, a2 = later(ii, u, 2)
                    i3, u3, a3 = later(ii, u, 3)
                    if a2 <= ahead:
                        stack(i2, u2, 0)
                    if a3 <= ahead:
                        load_ctx(i3, u3)
                    if a2 <= ahead:
                        stack(i2, u2, 1)
                    if u == 1:
                        if ahead > 0:
                            store_x1(ii, 0)
                    elif not (isinstance(ii, int) and ii == 0):
                        store_x1(ii - 1, 1)

            load_ctx(0, 0)
            load_ctx(0, 1)
            for n in range(4):
                stack(0, n // 2, n % 2)
            load_ctx(1, 0)
            passes_ahead(sp, attention_pass)
            for t in range(TILES):
                if t == E:
                    store_x1(PAIRS - 1, 0)
                    store_x1(PAIRS - 1, 1)
                sp.wait_ge(s_x2s, t + 1)
                half, c = divmod(t * P, HALF)
                sp.dma_start(xt_scratch[half].rearrange("(a p) t -> p a t", p=P)[:, :, c:c + P],
                             xts[t % 4].rearrange("p (a t) -> p a t", a=NT)).then_inc(s_x2d[t % 4], 16)
            sp.wait_ge(s_x1d, TILES * 16)
            for u in range(2):
                sp.wait_ge(s_gx[u], PAIRS)
            def a_pass(ii):
                for u in range(2):
                    since(sp, s_out[u], ii * 16)
                    sp.dma_start(xg[u][:, :], x1_scratch[bass.ds(ii * (2 * P) + u * P, P), :]).then_inc(s_xl[u], 16)
                for u in range(2):
                    since(sp, s_f[u], ii + 1)
                    sp.dma_start(out[bass.ds(ii * (2 * P) + u * P, P), :], xg[u][:, :]).then_inc(s_out[u], 16)

            passes(sp, a_pass)
            for u in range(2):
                sp.wait_ge(s_out[u], PAIRS * 16)
            for i in range(4):
                sp.wait_ge(s_x2d[i], TILES // 4 * 16)
            sp.wait_ge(s_x1d, TILES * 16)

        @block.gpsimd
        def _(pool):
            nc.gpsimd.memset(wq2[:, :], 0.0)
            nc.gpsimd.memset(wk2[:, :], 0.0)
            nc.gpsimd.memset(sc[:, :], 0.0)
            nc.gpsimd.memset(wv2[:, :], 0.0).then_inc(s_zero, 1)
            pool.wait_ge(s_zero, 1)
            nc.gpsimd.memset(NEG_LEAST, -ROUND_FP8_LEAST)
            nc.gpsimd.memset(ROUND, ROUND_INT)
            nc.gpsimd.memset(ident[:, :], 0.0).then_inc(s_ident0, 1)
            pool.wait_ge(s_ident0, 1)
            nc.gpsimd.affine_select(out=ident[:, :], in_=ident[:, :], compare_op=ALU.not_equal, fill=1.0, base=0,
                                    pattern=[[-1, P]], channel_multiplier=1).then_inc(s_ident, 1)
            pool.wait_ge(s_cols, 48)
            for it in range(IT):
                r = rows(it)
                pool.indirect_dma_start(WDG[0:r, it * N:(it + 1) * N], None, w_down_t,
                                        bass.IndirectOffsetOnAxis(ap=idx_mid[0:r, it:it + 1], axis=0)).then_inc(s_wdg, 16)
            for jt in range(NT):
                pool.indirect_dma_start(GT[:, jt * GU:(jt + 1) * GU], None, w_gu_t,
                                        bass.IndirectOffsetOnAxis(ap=idx_in[:, jt:jt + 1], axis=0)).then_inc(s_gt, 16)
            nc.gpsimd.memset(ident16, 0.0).then_inc(s_ident0, 1)
            pool.wait_ge(s_ident0, 2)
            nc.gpsimd.affine_select(out=ident16, in_=ident16, compare_op=ALU.not_equal, fill=1.0, base=0,
                                    pattern=[[-1, P]], channel_multiplier=1).then_inc(s_one, 1)
            pool.wait_ge(s_one, 1)
            for n in range(4):
                nc.gpsimd.memset(k_st[n][3 * QK:3 * QK + 2, :], 1.0).then_inc(s_one, 1)
                pool.wait_ge(s_one, n + 2)
            for u in range(2):
                nc.gpsimd.memset(v_hi[u], 1.0)
                nc.gpsimd.memset(v_lo[u], 0.0).then_inc(s_one, 1)
                pool.wait_ge(s_one, u + 6)
            for k, (w, r, b0, nb) in enumerate(w_items):
                pool.wait_ge(s_wrc, k + 1)
                nc.gpsimd.tensor_tensor(blk(w), blk(w), bc(wr[0:r, b0:b0 + nb], nb), ALU.mult).then_inc(s_wmul, 1)
            pool.wait_ge(s_wmax, 1)
            nc.gpsimd.partition_all_reduce(W_POW, W_MAX, P, RMAX).then_inc(s_wall, 1)
            pool.wait_ge(s_wsd, 16 * IT)
            for it in range(IT):
                r = rows(it)
                pool.indirect_dma_start(WR[0:r, it * 2 * N:(it + 1) * 2 * N], None, wt_scratch,
                                        bass.IndirectOffsetOnAxis(ap=idx_mid[0:r, it:it + 1], axis=0)).then_inc(s_wr, 16)
            pool.wait_ge(s_ln1, 1)

            def p_lower(ii, n, half):
                slot = 2 * (n % 2) + half
                since(pool, s_phi[half], ii * 4 + n + 1)
                since(pool, s_pv[half], ii * 4 + n - 1)
                nc.gpsimd.tensor_tensor(p_lo[slot], p32[half], p_hi[slot], ALU.subtract).then_inc(s_plo[half], 1)

            def residual_base(ii, u):
                since(pool, s_z0[u], ii + 1)
                since(pool, s_x1[u], ii)
                nc.gpsimd.tensor_tensor(z[u], z0[u], X[:, bass.ds(ii * (2 * N) + u * N, N)],
                                        ALU.add).then_inc(s_z[u], 1)

            def attention_pass(ii, ahead):
                for n in range(4):
                    for half in range(2):
                        p_lower(ii, n, half)
                    i1, u1, a1 = later(ii, n // 2, 1)
                    if n % 2 == 1 and a1 <= ahead:
                        residual_base(i1, u1)

            residual_base(0, 0)
            passes_ahead(pool, attention_pass)

            def gather_half(half):
                for i in range(4):
                    pool.wait_ge(s_x2d[i], (half + 1) * PAIRS // 4 * 16)
                for jt in range(NT):
                    c = jt * TOK + half * HALF
                    pool.indirect_dma_start(XG[:, c:c + HALF], None, xt_scratch[half],
                                            bass.IndirectOffsetOnAxis(ap=idx_in[:, jt:jt + 1],
                                                                      axis=0)).then_inc(s_xg[half], 16)

            gather_half(0)
            pool.wait_ge(s_amax, 1)
            nc.gpsimd.partition_all_reduce(A_MAX, sc[:, 25:26], P, RMAX).then_inc(s_aall, 1)
            pool.wait_ge(s_x2t, TILES)
            xg_v = XG[:, :].rearrange("p (a t) -> p a t", a=NT)
            def copy_out(ii, u):
                since(pool, s_gx[u], ii)
                nc.gpsimd.tensor_copy(xg[u][:, :].rearrange("p (a t) -> p a t", a=NT),
                                      xg_v[:, :, bass.ds(ii * (2 * P) + u * P, P)]).then_inc(s_gc[u], 1)

            def times_scale(ii, u):
                A = qa[0]
                since(pool, s_gr[u], ii + 1)
                nc.gpsimd.tensor_tensor(blk(A), blk(A), bc(a_blk[:, u * NB:(u + 1) * NB], NB), ALU.mult).then_inc(s_gA0[u], 1)

            def add_outliers(ii, u):
                A = qa[0]
                since(pool, s_gA0[u], ii + 1)
                since(pool, s_go[u], ii + 1)
                nc.gpsimd.tensor_tensor(A[:, N - SELECT:N], A[:, N - SELECT:N], qa[1][:, 0:SELECT],
                                        ALU.add).then_inc(s_ga[u], 1)

            def gate_up_pass(ii, ahead):
                for u in range(2):
                    i1, u1, a1 = later(ii, u, 1)
                    i3, u3, a3 = later(ii, u, 3)
                    if a1 <= ahead:
                        times_scale(i1, u1)
                        add_outliers(i1, u1)
                    if a3 <= ahead:
                        copy_out(i3, u3)

            gather_half(1)
            pool.wait_ge(s_xg[0], NT * 16)
            times_scale(0, 0)
            copy_out(1, 0)
            add_outliers(0, 0)
            gate_up_pass(0, 2)
            pool.wait_ge(s_xg[1], NT * 16)
            with pool.Fori(1, PAIRS - 2) as ii:
                gate_up_pass(ii, 2)
            gate_up_pass(PAIRS - 2, 1)
            gate_up_pass(PAIRS - 1, 0)
            pool.wait_ge(s_hmax, 1)
            nc.gpsimd.partition_all_reduce(H_MAX, sc[:, 26:27], P, RMAX).then_inc(s_hall, 1)

            def over_scale(ii, u):
                t = ii * 2 + u
                h = H[:, bass.ds(t * HID, HID)]
                nc.gpsimd.tensor_tensor(blk(h), blk(h), bc(XG[:, bass.ds(t * P + RCP, HB)], HB),
                                        ALU.mult).then_inc(s_ht[u], 1)

            def times_scale_h(ii, u):
                t = ii * 2 + u
                A = hA[u]
                since(pool, s_hr[u], ii + 1)
                nc.gpsimd.tensor_tensor(blk(A), blk(A), bc(h_blk[:, bass.ds(t * HB, HB)], HB),
                                        ALU.mult).then_inc(s_hA0[u], 1)

            def add_outliers_h(ii, u):
                A = hA[u]
                since(pool, s_hA0[u], ii + 1)
                since(pool, s_ho[u], ii + 1)
                nc.gpsimd.tensor_tensor(A[:, HID - SELECT:HID], A[:, HID - SELECT:HID], h_tmp[:, 0:SELECT],
                                        ALU.add).then_inc(s_hA[u], 1)

            def final(ii, u):
                since(pool, s_ys, ii * 2 + u + 1)
                since(pool, s_xl[u], ii * 16 + 16)
                nc.gpsimd.tensor_tensor(xg[u][:, :], y_out[u], xg[u][:, :], ALU.add).then_inc(s_f[u], 1)

            def down_pass(ii, ahead):
                for u in range(2):
                    i2, u2, a2 = later(ii, u, 2)
                    i4, u4, a4 = later(ii, u, 4)
                    if u == 1:
                        final(ii, 0)
                    elif not (isinstance(ii, int) and ii == 0):
                        final(ii - 1, 1)
                    if a2 <= ahead:
                        times_scale_h(i2, u2)
                    if a4 <= ahead:
                        over_scale(i4, u4)
                    if a2 <= ahead:
                        add_outliers_h(i2, u2)

            pool.wait_ge(s_hsc, 1)
            over_scale(0, 0)
            pool.wait_ge(s_hsc, 2)
            over_scale(0, 1)
            over_scale(1, 0)
            pool.wait_ge(s_hsc, 3)
            times_scale_h(0, 0)
            add_outliers_h(0, 0)
            over_scale(1, 1)
            times_scale_h(0, 1)
            add_outliers_h(0, 1)
            passes_ahead(pool, down_pass)
            final(PAIRS - 1, 1)

        @block.tensor
        def _(pe):
            pe.wait_ge(s_ident, 1)
            pe.wait_ge(s_wdg, IT * 16)
            for ot in range(NT):
                b = 1 + 3 * (ot % 2)
                if ot >= 2:
                    pe.wait_ge(s_wdr, ot - 1)
                for it in range(IT):
                    r = rows(it)
                    last = nc.tensor.transpose(PS[:, b + it // 4, (it % 4) * P:(it % 4) * P + r],
                                               WDG[0:r, it * N + ot * P:it * N + (ot + 1) * P], ident[0:r, 0:r])
                last.then_inc(s_dt, 1)
            pe.wait_ge(s_wdr, NT)
            pe.wait_ge(s_gt, NT * 16)
            for it in range(IT):
                b = 2 * (it % 2)
                if it >= 2:
                    pe.wait_ge(s_wst, it - 1)
                r = rows(it)
                for w in range(2):
                    for jt in range(NT):
                        c = jt * GU + w * HID + it * P
                        last = nc.tensor.transpose(PS[0:r, b + w, jt * P:(jt + 1) * P], GT[:, c:c + r], ident[:, :])
                last.then_inc(s_wt, 1)
            pe.wait_ge(s_wst, IT)
            pe.wait_ge(s_wq, NT)
            for it in range(IT):
                r = rows(it)
                if it >= 4:
                    pe.wait_ge(s_whi, it - 3)
                    pe.wait_ge(s_wlo, it - 3)
                for ot in range(NT):
                    last = nc.tensor.transpose(PS[0:r, 2 + it % 4, ot * P:(ot + 1) * P],
                                               WDR[:, ot * HID + it * P:ot * HID + it * P + r], ident[:, :])
                last.then_inc(s_wtq, 1)

            def gate_up_weights_back(first, last):
                for n in range(IT + first, IT + last):
                    it, w = divmod(n - IT, 2)
                    pe.wait_ge(s_wr, IT * 16)
                    pe.wait_ge(s_whi, n - 3)
                    pe.wait_ge(s_wlo, n - 3)
                    r = rows(it)
                    for jt in range(NT):
                        c = it * 2 * N + w * N + jt * P
                        done = nc.tensor.transpose(PS[:, 2 + n % 4, jt * P:jt * P + r], WR[0:r, c:c + P], ident[0:r, 0:r])
                    done.then_inc(s_wtq, 1)

            pe.wait_ge(s_w2, 6 * 16)
            pe.wait_ge(s_one, 7)
            PR, RT = PS[:, 6, :], PS[:, 7, :]

            def project_q(ii, u):
                since(pe, s_xn[u], ii + 1)
                since(pe, s_vh, ii * 2 + u - 1)
                since(pe, s_vl, ii * 2 + u - 1)
                nc.tensor.matmul(PR[0:2 * QK, :], wq2[:, :], xn[u], start=True, stop=True).then_inc(s_prq, 1)

            def project_k(ii, u):
                since(pe, s_ct[u], ii * 16 + 16)
                since(pe, s_qh, ii * 2 + u + 1)
                since(pe, s_ql, ii * 2 + u + 1)
                nc.tensor.matmul(PR[0:2 * QK, :], wk2[:, :], ct[u], start=True, stop=True).then_inc(s_prk, 1)

            def project_v(ii, u, bank_of):
                ik, uk = bank_of
                since(pe, s_kh, ik * 2 + uk + 1)
                since(pe, s_kl, ik * 2 + uk + 1)
                for mt in range(NT):
                    last = nc.tensor.matmul(PR[:, mt * P:(mt + 1) * P], ct[u][:, mt * P:(mt + 1) * P], wv2[:, :],
                                            start=True, stop=True)
                last.then_inc(s_prv, 1)

            def scores(ii, n, half):
                since(pe, s_st[n], (ii + 1) * 96)
                if half == 0:
                    since(pe, s_mx[1], ii * 4 + n)
                else:
                    since(pe, s_mx[0], ii * 4 + n + 1)
                for j in range(2):
                    nt = 2 * half + j
                    last = nc.tensor.matmul(PS[:, j, :], q_st[n][0:3 * QK, nt * P:(nt + 1) * P], k_st[n][0:3 * QK, :],
                                            start=True, stop=True)
                last.then_inc(s_e[half], 1)

            def maxima_to_rows(ii, n, before):
                g = ii * 4 + n
                since(pe, s_nm, g + 1)
                since(pe, s_rowe, g)
                if before is not None:
                    since(pe, s_x1[before[1]], before[0] + 1)
                for nt in range(NT):
                    c = (n % 2) * 2 * NT + 2 * nt
                    last = nc.tensor.matmul(RT[3 * QK:3 * QK + 2, nt * P:(nt + 1) * P], nm16[:, c:c + 2], ident16,
                                            start=True, stop=True)
                last.then_inc(s_row, 1)

            def scores_less_max(ii, n, half):
                g = ii * 4 + n
                if half == 0:
                    since(pe, s_rowe, g + 1)
                    since(pe, s_p[1], g)
                else:
                    since(pe, s_p[0], g + 1)
                for j in range(2):
                    mt = 2 * half + j
                    last = nc.tensor.matmul(PS[:, 2 + j, :], k_st[n][0:3 * QK + 2, mt * P:(mt + 1) * P],
                                            q_st[n][0:3 * QK + 2, :], start=True, stop=True)
                last.then_inc(s_et[half], 1)

            def product_v(ii, n, half):
                g = ii * 4 + n
                u, b, slot = n // 2, n % 2, 2 * (n % 2) + half
                since(pe, s_phi[half], g + 1)
                since(pe, s_plo[half], g + 1)
                if half == 0:
                    since(pe, s_vh, ii * 2 + u + 1)
                    since(pe, s_vl, ii * 2 + u + 1)
                    since(pe, s_on, g - 1)
                for j in range(2):
                    mt = 2 * half + j
                    c = (mt * 2 + b) * (CH + 1)
                    for nt in range(NT):
                        for k, (p, v) in enumerate(((p_hi, v_hi), (p_hi, v_lo), (p_lo, v_hi))):
                            last = nc.tensor.matmul(PS[:, 4 + b, nt * (CH + 1):(nt + 1) * (CH + 1)],
                                                    p[slot][:, j * N + nt * P:j * N + (nt + 1) * P],
                                                    v[u][:, c:c + CH + 1],
                                                    start=(mt == 0 and nt == 0 and k == 0),
                                                    stop=(mt == NT - 1 and nt == NT - 1 and k == 2),
                                                    skip_group_check=True)
                last.then_inc(s_pv[half], 1)

            def out_transpose(ii, u, rows_done):
                since(pe, s_on, ii * 4 + 2 * u + 2)
                since(pe, s_rowe, rows_done)
                for nt in range(NT):
                    last = nc.tensor.transpose(RT[:, nt * P:(nt + 1) * P], on[u][:, nt * P:(nt + 1) * P], ident[:, :])
                last.then_inc(s_ot[u], 1)

            def attention_pass(ii, ahead):
                first = isinstance(ii, int) and ii == 0
                for n in range(4):
                    u, b, g = n // 2, n % 2, ii * 4 + n
                    i2, u2, a2 = later(ii, u, 2)
                    i1, u1, a1 = later(ii, u, 1)
                    ip, up = (ii, 0) if u else (ii - 1, 1)
                    i2b, n2 = (ii, n + 2) if n < 2 else (ii + 1, n - 2)
                    i1b, n1 = (ii, n + 1) if n < 3 else (ii + 1, 0)
                    ipb, np_ = (ii, n - 1) if n else (ii - 1, 3)
                    more2 = n < 2 or ahead >= 1
                    more1 = n < 3 or ahead >= 1
                    if more2:
                        scores(i2b, n2, 0)
                    scores_less_max(ii, n, 0)
                    if b == 0 and a2 <= ahead:
                        project_q(i2, u2)
                    if not (first and n == 0):
                        product_v(ipb, np_, 0)
                    if more1:
                        if b == 0 and not (first and n < 4):
                            before = (ii - 1, u)
                        else:
                            before = None
                        maxima_to_rows(i1b, n1, before)
                    if more2:
                        scores(i2b, n2, 1)
                    scores_less_max(ii, n, 1)
                    if b == 0 and a2 <= ahead:
                        project_k(i2, u2)
                    if b == 1:
                        if a1 <= ahead:
                            project_v(i1, u1, (i2, u2) if a2 <= ahead else (ii, u))
                        if not (first and u == 0):
                            out_transpose(ip, up, g + 2 if more1 else g + 1)
                    if not (first and n == 0):
                        product_v(ipb, np_, 1)
                    if ahead == 0 and n >= 2:
                        x1_transpose(2 * n - 4)
                        x1_transpose(2 * n - 3)

            def x1_transpose(t):
                pe.wait_ge(s_x2n, t + 1)
                if t >= 2:
                    pe.wait_ge(s_x2s, t - 1)
                else:
                    pe.wait_ge(s_mx[1], 4 * PAIRS)
                for nt in range(NT):
                    last = nc.tensor.transpose(PS[:, t % 2, nt * P:(nt + 1) * P], xn[t % 2][:, nt * P:(nt + 1) * P], ident[:, :])
                last.then_inc(s_x2t, 1)

            project_q(0, 0)
            gate_up_weights_back(0, 3)
            project_k(0, 0)
            gate_up_weights_back(3, 6)
            pe.wait_ge(s_kh, 1)
            pe.wait_ge(s_kl, 1)
            project_q(0, 1)
            gate_up_weights_back(6, 9)
            project_k(0, 1)
            gate_up_weights_back(9, 12)
            project_v(0, 0, (0, 1))
            scores(0, 0, 0)
            gate_up_weights_back(12, 14)
            scores(0, 0, 1)
            gate_up_weights_back(14, 17)
            maxima_to_rows(0, 0, None)
            scores(0, 1, 0)
            gate_up_weights_back(17, 19)
            scores(0, 1, 1)
            gate_up_weights_back(19, 22)
            pe.wait_ge(s_whi, 3 * IT)
            pe.wait_ge(s_wlo, 3 * IT)
            passes_ahead(pe, attention_pass)
            product_v(PAIRS - 1, 3, 0)
            x1_transpose(4)
            product_v(PAIRS - 1, 3, 1)
            x1_transpose(5)
            pe.wait_ge(s_x1[0], PAIRS)
            out_transpose(PAIRS - 1, 1, PAIRS * 4)

            for t in range(6, TILES):
                x1_transpose(t)

            pe.wait_ge(s_x2s, TILES)

            def gathered_back(ii, u):
                since(pe, s_gc[u], ii)
                since(pe, s_gm[u], ii)
                for jt in range(NT):
                    if isinstance(ii, int) and ii == 0:
                        pe.wait_ge(s_xg[0], NT * 16)
                        tile = XG[:, jt * TOK + u * P:jt * TOK + (u + 1) * P]
                    else:
                        tile = xg[u][:, jt * P:(jt + 1) * P]
                    last = nc.tensor.transpose(PS[:, 4 + u, jt * P:(jt + 1) * P], tile, ident[:, :])
                last.then_inc(s_gx[u], 1)

            def a_transpose(ii, u):
                since(pe, s_ga[u], ii + 1)
                since(pe, s_ghi[u], ii)
                since(pe, s_glo[u], ii)
                for jt in range(NT):
                    last = nc.tensor.transpose(PS[:, 6 + u, jt * P:(jt + 1) * P], qa[0][:, jt * P:(jt + 1) * P], ident[:, :])
                last.then_inc(s_gt2[u], 1)

            def gate_up(ii, u, c):
                n = 3 * u + c
                slot = n % 2
                since(pe, s_sg[slot], ii * 3 + n // 2)
                since(pe, s_h[slot], ii * 3 + n // 2)
                w_n = CHUNK[c]
                for w in range(2):
                    k = 0
                    for jt in range(NT):
                        for a, b in ((at_hi, w_hi), (at_hi, w_lo), (at_lo, w_hi)):
                            cc = jt * GU + w * HID + CSTART[c]
                            last = nc.tensor.matmul(PS[:, 2 * w + slot, 0:w_n], a[u][:, jt * P:(jt + 1) * P],
                                                    b[:, cc:cc + w_n], start=(k == 0), stop=(k == 3 * NT - 1))
                            k += 1
                last.then_inc(s_gu[slot], 1)

            def gate_up_pass(ii, ahead):
                for u in range(2):
                    i1, u1, a1 = later(ii, u, 1)
                    i2, u2, a2 = later(ii, u, 2)
                    if a2 <= ahead:
                        gathered_back(i2, u2)
                    since(pe, s_ghi[u], ii + 1)
                    since(pe, s_glo[u], ii + 1)
                    gate_up(ii, u, 0)
                    gate_up(ii, u, 1)
                    if a1 <= ahead:
                        a_transpose(i1, u1)
                    gate_up(ii, u, 2)

            gathered_back(0, 0)
            gathered_back(0, 1)
            a_transpose(0, 0)
            passes_ahead(pe, gate_up_pass)

            for slot in range(2):
                pe.wait_ge(s_sg[slot], PAIRS * 3)
                pe.wait_ge(s_h[slot], PAIRS * 3)

            def h_transpose(ii, u):
                since(pe, s_hA[u], ii + 1)
                since(pe, s_hhi[u], ii)
                since(pe, s_hlo[u], ii)
                for it in range(IT):
                    r = rows(it)
                    last = nc.tensor.transpose(PS[0:r, 3 * u + it // 4, (it % 4) * P:(it % 4 + 1) * P],
                                               hA[u][:, it * P:it * P + r], ident[:, :])
                last.then_inc(s_hT[u], 1)

            def down(ii, u):
                since(pe, s_hhi[u], ii + 1)
                since(pe, s_hlo[u], ii + 1)
                since(pe, s_ys, ii * 2 + u - 1)
                k = 0
                for it in range(IT):
                    r = rows(it)
                    for a, b in ((ht_hi, wd_hi), (ht_hi, wd_lo), (ht_lo, wd_hi)):
                        last = nc.tensor.matmul(PS[:, 6 + u, :], a[u][0:r, it * P:(it + 1) * P],
                                                b[0:r, it * N:(it + 1) * N], start=(k == 0), stop=(k == 3 * IT - 1))
                        k += 1
                last.then_inc(s_y[u], 1)

            def down_pass(ii, ahead):
                for u in range(2):
                    i1, u1, a1 = later(ii, u, 1)
                    if a1 <= ahead:
                        h_transpose(i1, u1)
                    down(ii, u)

            h_transpose(0, 0)
            passes_ahead(pe, down_pass)

        @block.scalar
        def _(act):
            act.wait_ge(s_cols, 48)
            act.wait_ge(s_zero, 1)
            nc.scalar.activation(T1, col[:, 1:2], ACT.Tanh)
            nc.scalar.activation(T2, col[:, 2:3], ACT.Tanh).then_inc(s_t, 1)

            def down_weights_out(ot):
                b = 1 + 3 * (ot % 2)
                act.wait_ge(s_dt, ot + 1)
                nc.scalar.copy(WDR[:, ot * HID:(ot + 1) * HID],
                               PS[:, b:b + 3, :].rearrange("p b c -> p (b c)")[:, 0:HID]).then_inc(s_wdr, 1)

            def gate_up_weights_out(it):
                act.wait_ge(s_wt, it + 1)
                r = rows(it)
                b = 2 * (it % 2)
                nc.scalar.copy(wst[it][0:r, :].rearrange("p (w j) -> p w j", w=2),
                               PS[0:r, b:b + 2, :]).then_inc(s_wst, 1)

            def round_w(k):
                w, r, b0, nb = w_items[k]
                act.wait_ge(s_wmul, k + 1)
                nc.scalar.activation(w, w, ACT.Identity, bias=ROUND[0:r, :]).then_inc(s_wround, 1)

            for ot in range(NT):
                down_weights_out(ot)
            round_w(0)
            round_w(1)
            out = 0
            for k in range(2, len(w_items)):
                while out < min(IT, 2 * k - 2):
                    gate_up_weights_out(out)
                    out += 1
                round_w(k)
            act.wait_ge(s_wup, 1)
            for it in range(IT):
                r = rows(it)
                act.wait_ge(s_wtq, it + 1)
                nc.scalar.activation(wd_hi[0:r, it * N:(it + 1) * N], PS[0:r, 2 + it % 4, :], ACT.Identity,
                                     scale=W_UP[0:r, 1:2]).then_inc(s_whi, 1)

            def gate_up_weights_upper(first, last):
                for n in range(IT + first, IT + last):
                    it, w = divmod(n - IT, 2)
                    r = rows(it)
                    act.wait_ge(s_wtq, n + 1)
                    nc.scalar.activation(w_hi.rearrange("p (j w i) -> p j w i", j=NT, w=2)[:, :, w, it * P:it * P + r],
                                         PS[:, 2 + n % 4, :].rearrange("p (j i) -> p j i", j=NT)[:, :, 0:r], ACT.Identity,
                                         scale=W_UP[:, 0:1]).then_inc(s_whi, 1)


            def sqrt_var(k, lo, hi):
                act.wait_ge(s_lnv, k)
                nc.scalar.activation(ln_a[:, lo:hi], var[:, lo:hi], ACT.Sqrt).then_inc(s_lna, 1)

            sqrt_var(1, 0, TILES)

            PR, RT = PS[:, 6, :], PS[:, 7, :]
            R = slice(0, 2 * QK)

            def halves_free(ii, u):
                for b in range(2):
                    since(act, s_st[2 * u + b], ii * 96)

            def q_upper(ii, u):
                since(act, s_prq, ii * 2 + u + 1)
                halves_free(ii, u)
                nc.scalar.activation(qk_hl[u][R, 0:N], PR[R, :], ACT.Identity, bias=col[R, 4:5]).then_inc(s_qh, 1)

            def k_upper(ii, u):
                since(act, s_prk, ii * 2 + u + 1)
                nc.scalar.activation(qk_hl[u][R, 2 * N:3 * N], PR[R, :], ACT.Identity,
                                     bias=col[R, 5:6]).then_inc(s_kh, 1)

            def v_upper(ii, u):
                since(act, s_prv, ii * 2 + u + 1)
                since(act, s_pv[1], ii * 4 - 4 + 2 * u + 2)
                nc.scalar.copy(v_hi[u][:, 0:NT * 2 * (CH + 1)].rearrange("p (m c) -> p m c", c=CH + 1)[:, :, 0:CH],
                               PR.rearrange("p (m c) -> p m c", c=CH)).then_inc(s_vh, 1)

            def rows_out(ii, n):
                since(act, s_row, ii * 4 + n + 1)
                since(act, s_et[1], ii * 4 + n - 3)
                r = slice(3 * QK, 3 * QK + 2)
                nc.scalar.copy(q_st[n][r, :], RT[r, :]).then_inc(s_rowe, 1)

            def exp(ii, n, half):
                g = ii * 4 + n
                since(act, s_et[half], g + 1)
                since(act, s_plo[half], g)
                nc.scalar.activation(p32[half], PS[:, 2:4, :].rearrange("p b c -> p (b c)"), ACT.Exp).then_inc(s_p[half], 1)

            def p_upper(ii, n, half):
                g = ii * 4 + n
                since(act, s_p[half], g + 1)
                since(act, s_pv[half], g - 1)
                nc.scalar.copy(p_hi[2 * (n % 2) + half], p32[half]).then_inc(s_phi[half], 1)

            def attention_pass(ii, ahead):
                for n in range(4):
                    u, b = n // 2, n % 2
                    i2, u2, a2 = later(ii, u, 2)
                    i1, u1, a1 = later(ii, u, 1)
                    i1b, n1 = (ii, n + 1) if n < 3 else (ii + 1, 0)
                    exp(ii, n, 0)
                    if b == 0 and a2 <= ahead:
                        q_upper(i2, u2)
                    p_upper(ii, n, 0)
                    if n < 3 or ahead >= 1:
                        rows_out(i1b, n1)
                    exp(ii, n, 1)
                    if b == 0 and a2 <= ahead:
                        k_upper(i2, u2)
                    if b == 1 and a1 <= ahead:
                        v_upper(i1, u1)
                    p_upper(ii, n, 1)
                    if ahead == 0:
                        if n == 0:
                            sqrt_var(2, 0, E)
                        if n >= 2:
                            x1_out(2 * n - 4)
                            x1_out(2 * n - 3)

            def x1_out(t):
                act.wait_ge(s_x2t, t + 1)
                if t >= 4:
                    act.wait_ge(s_x2d[t % 4], t // 4 * 16)
                nc.scalar.copy(xts[t % 4], PS[:, t % 2, :]).then_inc(s_x2s, 1)

            act.wait_ge(s_one, 7)
            q_upper(0, 0)
            gate_up_weights_upper(0, 3)
            k_upper(0, 0)
            gate_up_weights_upper(3, 6)
            q_upper(0, 1)
            gate_up_weights_upper(6, 9)
            k_upper(0, 1)
            gate_up_weights_upper(9, 12)
            v_upper(0, 0)
            gate_up_weights_upper(12, 17)
            rows_out(0, 0)
            gate_up_weights_upper(17, 22)
            passes_ahead(act, attention_pass)

            for t in range(4, E):
                x1_out(t)
            sqrt_var(3, E, TILES)
            for t in range(E, TILES):
                x1_out(t)

            def a_hi(ii, u):
                since(act, s_gt2[u], ii + 1)
                products_read(act, ii, u)
                nc.scalar.copy(at_hi[u][:, :], PS[:, 6 + u, :]).then_inc(s_ghi[u], 1)

            def silu(ii, n):
                slot = n % 2
                w_n = CHUNK[n % 3]
                since(act, s_gu[slot], ii * 3 + n // 2 + 1)
                since(act, s_h[slot], ii * 3 + n // 2)
                nc.scalar.activation(sg[slot][:, 0:w_n], PS[:, slot, 0:w_n], ACT.Silu,
                                     scale=A_OUT).then_inc(s_sg[slot], 1)

            def round_constant(dst, src):
                return nc.scalar.activation(dst, src, ACT.Relu, scale=ROUND_FP8, bias=NEG_LEAST)

            def a_constant(ii, u):
                since(act, s_gm[u], ii + 1)
                round_constant(qa[2], qa[2]).then_inc(s_gm2[u], 1)

            def gate_up_pass(ii, ahead):
                for u in range(2):
                    i1, u1, a1 = later(ii, u, 1)
                    i2, u2, a2 = later(ii, u, 2)
                    silu(ii, 3 * u)
                    if a2 <= ahead:
                        a_constant(i2, u2)
                    silu(ii, 3 * u + 1)
                    if a1 <= ahead:
                        a_hi(i1, u1)
                    silu(ii, 3 * u + 2)

            act.wait_ge(s_ag, 1)
            a_constant(0, 0)
            a_constant(0, 1)
            a_hi(0, 0)
            passes_ahead(act, gate_up_pass)

            def h_constant(ii, u):
                since(act, s_hm[u], ii + 1)
                round_constant(hm[u], hm[u]).then_inc(s_hm2[u], 1)

            def h_hi(ii, u):
                since(act, s_hT[u], ii + 1)
                since(act, s_y[u], ii)
                src = PS[:, 3 * u:3 * u + 3, :].rearrange("p b c -> p (b c)")
                FULL, r = HID // P * P, rows(IT - 1)
                nc.scalar.copy(ht_hi[u][:, 0:FULL], src[:, 0:FULL])
                nc.scalar.copy(ht_hi[u][0:r, FULL:FULL + P], src[0:r, FULL:FULL + P]).then_inc(s_hhi[u], 1)

            def y_scaled(ii, u):
                since(act, s_y[u], ii + 1)
                since(act, s_f[u], ii)
                nc.scalar.activation(y_out[u], PS[:, 6 + u, :], ACT.Identity, scale=H_OUT).then_inc(s_ys, 1)

            def down_pass(ii, ahead):
                for u in range(2):
                    i1, u1, a1 = later(ii, u, 1)
                    i3, u3, a3 = later(ii, u, 3)
                    if u == 1:
                        y_scaled(ii, 0)
                    elif not (isinstance(ii, int) and ii == 0):
                        y_scaled(ii - 1, 1)
                    if a1 <= ahead:
                        h_hi(i1, u1)
                    if a3 <= ahead:
                        h_constant(i3, u3)

            for t in range(3):
                h_constant(t // 2, t % 2)
            h_hi(0, 0)
            passes_ahead(act, down_pass)
            y_scaled(PAIRS - 1, 1)

        @block.vector
        def _(dve):
            ts, tt, stt = nc.vector.tensor_scalar, nc.vector.tensor_tensor, nc.vector.scalar_tensor_tensor
            wv = Chain(dve, s_wv, 0, 0)
            wv.step(nc.vector.memset(ws, 0.0))
            for k in range(len(w_items) + 3):
                if k < len(w_items):
                    w, r, b0, nb = w_items[k]
                    s_k = ws[0:r, b0:b0 + nb]
                    if k < NT:
                        dve.wait_ge(s_wdr, k + 1)
                    else:
                        dve.wait_ge(s_wst, k - NT + 1)
                    reduced = wv.mark(nc.vector.tensor_reduce(s_k, blk(w), AX_X, ALU.max, apply_absolute_value=True))
                if k >= 3:
                    w0, r0, b00, nb0 = w_items[k - 3]
                    dve.wait_ge(s_wround, k - 2)
                    stt(blk(w0), blk(w0), -ROUND_INT, bc(ws[0:r0, b00:b00 + nb0], nb0), ALU.add, ALU.mult).then_inc(s_wq, 1)
                if k < len(w_items):
                    dve.wait_ge(s_wv, reduced)
                    scaled = wv.mark(ts(s_k, s_k, 1.0 / INT4_MAX, SCALE_FLOOR, ALU.mult, ALU.max))
                    dve.wait_ge(s_wv, scaled)
                    nc.vector.reciprocal(wr[0:r, b0:b0 + nb], s_k).then_inc(s_wrc, 1)
            dve.wait_ge(s_zero, 1)
            nc.vector.reduce_max(W_MAX[:, 0:1], ws[:, 0:W1], AX_X)
            nc.vector.reduce_max(W_MAX[:, 1:2], ws[:, W1:NWB], AX_X).then_inc(s_wmax, 1)
            dve.wait_ge(s_ld, TILES * 16)
            for t in range(TILES):
                last = nc.vector.bn_stats(stats[:, 6 * t:6 * t + 6], X[:, t * N:(t + 1) * N])
            wv.step(last)
            dve.wait_ge(s_wall, 1)
            wv.step(ts(W_POW.bitcast(I32), W_POW.bitcast(I32), EXPONENT, None, ALU.bitwise_and))
            wv.step(nc.vector.reciprocal(W_UP, W_POW))
            wv.step(ts(W_DOWN, W_POW, 1.0 / W_TOP, None, ALU.mult))
            ts(W_UP, W_UP, W_TOP, None, ALU.mult).then_inc(s_wup, 1)
            dve.wait_ge(s_wup, 1)
            for it in range(IT):
                r = rows(it)
                dve.wait_ge(s_whi, it + 1)
                stt(wd_lo[0:r, it * N:(it + 1) * N], PS[0:r, 2 + it % 4, :], W_UP[0:r, 1:2],
                    wd_hi[0:r, it * N:(it + 1) * N], ALU.mult, ALU.subtract).then_inc(s_wlo, 1)

            def gate_up_weights_lower(first, last):
                for n in range(IT + first, IT + last):
                    it, w = divmod(n - IT, 2)
                    r = rows(it)
                    dve.wait_ge(s_whi, n + 1)
                    v = lambda a: a.rearrange("p (j w i) -> p j w i", j=NT, w=2)[:, :, w, it * P:it * P + r]
                    stt(v(w_lo), PS[:, 2 + n % 4, :].rearrange("p (j i) -> p j i", j=NT)[:, :, 0:r], W_UP[:, 0:1],
                        v(w_hi), ALU.mult, ALU.subtract).then_inc(s_wlo, 1)

            dve.wait_ge(s_t, 1)
            wv.step(tt(T1G, T1, col[:, 0:1], ALU.mult))
            wv.step(tt(T1GBV, T1G, col[:, 3:4], ALU.mult))

            def layernorm_scales(k, lo, hi):
                for t in range(lo, hi):
                    last = nc.vector.bn_aggr(mv[:, 2 * t:2 * t + 2], stats[:, 6 * t:6 * t + 6])
                wv.step(last)
                m3 = mv[:, 2 * lo:2 * hi].rearrange("p (t s) -> p t s", s=2)
                v, a, b, r = var[:, lo:hi], ln_a[:, lo:hi], ln_b[:, lo:hi], rstd[:, lo:hi]
                ts(v, m3[:, :, 1], LN_EPS, None, ALU.add).then_inc(s_lnv, 1)
                dve.wait_ge(s_lnv, k)
                dve.wait_ge(s_lna, k)
                wv.step(nc.vector.reciprocal(r, a))
                wv.step(tt(b, r, r, ALU.mult))
                wv.step(tt(b, b, v, ALU.mult))
                wv.step(ts(b, b, -0.5, 1.5, ALU.mult, ALU.add))
                wv.step(tt(r, r, b, ALU.mult))
                stt(nmr[:, lo:hi], m3[:, :, 0], -1.0, r, ALU.mult, ALU.mult).then_inc(s_ln1, 1)
                dve.wait_ge(s_ln1, k)

            layernorm_scales(1, 0, TILES)

            PR, RT = PS[:, 6, :], PS[:, 7, :]
            R = slice(0, 2 * QK)

            def normalise(ii, u):
                since(dve, s_prq, ii * 2 + u - 1)
                t = ii * 2 + u
                ts(xn[u], X[:, bass.ds(t * N, N)], rstd[:, bass.ds(t, 1)], nmr[:, bass.ds(t, 1)],
                   ALU.mult, ALU.add).then_inc(s_xn[u], 1)

            def q_lower(ii, u):
                since(dve, s_qh, ii * 2 + u + 1)
                stt(qk_hl[u][R, N:2 * N], PR[R, :], col[R, 4:5], qk_hl[u][R, 0:N], ALU.add,
                    ALU.subtract).then_inc(s_ql, 1)

            def k_lower(ii, u):
                since(dve, s_kh, ii * 2 + u + 1)
                stt(qk_hl[u][R, 3 * N:4 * N], PR[R, :], col[R, 5:6], qk_hl[u][R, 2 * N:3 * N], ALU.add,
                    ALU.subtract).then_inc(s_kl, 1)

            def v_lower(ii, u):
                since(dve, s_vh, ii * 2 + u + 1)
                v = lambda a: a[:, 0:NT * 2 * (CH + 1)].rearrange("p (m c) -> p m c", c=CH + 1)[:, :, 0:CH]
                tt(v(v_lo[u]), PR.rearrange("p (m c) -> p m c", c=CH), v(v_hi[u]), ALU.subtract).then_inc(s_vl, 1)

            def residual_start(ii, u):
                since(dve, s_ct[u], ii * 16 + 16)
                since(dve, s_z[u], ii)
                ts(z0[u], ct[u], T1, T1GBV, ALU.mult, ALU.add).then_inc(s_z0[u], 1)

            def row_max(ii, n, half):
                since(dve, s_e[half], ii * 4 + n + 1)
                c = (n % 2) * NT + 2 * half
                nc.vector.tensor_reduce(nmx[:, c:c + 2], PS[:, 0:2, :], AX_X, ALU.max, negate=True).then_inc(s_mx[half], 1)

            def split_max(ii, n):
                g = ii * 4 + n
                since(dve, s_mx[0], g + 1)
                since(dve, s_mx[1], g + 1)
                since(dve, s_row, g - 1)
                m = nmx[:, (n % 2) * NT:(n % 2 + 1) * NT]
                v = nm16[:, (n % 2) * 2 * NT:(n % 2 + 1) * 2 * NT].rearrange("p (t s) -> p t s", s=2)
                ts(v[:, :, 0], m, LN_P_SCALE, None, ALU.add).then_inc(s_nmh, 1)
                since(dve, s_nmh, g + 1)
                stt(v[:, :, 1], m, LN_P_SCALE, v[:, :, 0], ALU.add, ALU.subtract).then_inc(s_nm, 1)

            def batch_out(ii, n):
                g = ii * 4 + n
                u, b = n // 2, n % 2
                since(dve, s_pv[1], g + 1)
                o = PS[:, 4 + b, 0:NT * (CH + 1)].rearrange("p (n c) -> p n c", c=CH + 1)
                rs = rsum[:, b * NT:(b + 1) * NT].rearrange("p (n o) -> p n o", o=1)
                nc.vector.reciprocal(rs, o[:, :, CH:CH + 1]).then_inc(s_rsum, 1)
                since(dve, s_rsum, g + 1)
                tt(on[u].rearrange("p (n b c) -> p n b c", n=NT, b=2)[:, :, b, :], o[:, :, 0:CH],
                   rs.broadcast_to([P, NT, CH]), ALU.mult).then_inc(s_on, 1)

            def residual(ii, u):
                since(dve, s_ot[u], ii + 1)
                since(dve, s_z[u], ii + 1)
                t = ii * 2 + u
                stt(X[:, bass.ds(t * N, N)], RT, T1G, z[u], ALU.mult, ALU.add).then_inc(s_x1[u], 1)

            def stats_x1(ii, u):
                t = ii * 2 + u
                nc.vector.bn_stats(stats[:, bass.ds(t * 6, 6)], X[:, bass.ds(t * N, N)])

            def attention_pass(ii, ahead):
                first = isinstance(ii, int) and ii == 0
                for n in range(4):
                    u, b = n // 2, n % 2
                    i1, u1, a1 = later(ii, u, 1)
                    i2, u2, a2 = later(ii, u, 2)
                    i3, u3, a3 = later(ii, u, 3)
                    ip, up = (ii, 0) if u else (ii - 1, 1)
                    i2b, n2 = (ii, n + 2) if n < 2 else (ii + 1, n - 2)
                    m2b, nm2 = (ii, n - 2) if n >= 2 else (ii - 1, n + 2)
                    more2 = n < 2 or ahead >= 1
                    i_s, u_s = (ii - 1, u)
                    stats_now = b == 0 and not (first)
                    if stats_now:
                        since(dve, s_x1[u_s], i_s + 1)
                    if more2:
                        row_max(i2b, n2, 0)
                    if not (first and n < 2):
                        batch_out(m2b, nm2)
                    if b == 0 and a2 <= ahead:
                        q_lower(i2, u2)
                    if stats_now:
                        stats_x1(i_s, u_s)
                    if b == 1:
                        if a3 <= ahead:
                            normalise(i3, u3)
                        if a1 <= ahead:
                            residual_start(i1, u1)
                    if more2:
                        row_max(i2b, n2, 1)
                        split_max(i2b, n2)
                    if b == 0 and a2 <= ahead:
                        k_lower(i2, u2)
                    if b == 1:
                        if a1 <= ahead:
                            v_lower(i1, u1)
                        if not (first and u == 0):
                            residual(ip, up)
                    if ahead == 0:
                        if n == 0:
                            layernorm_scales(2, 0, E)
                        if n == 1:
                            dve.wait_ge(s_prq, TILES)
                            normalise_x1(0)
                            normalise_x1(1)
                        if n >= 2:
                            for t in (2 * n - 4, 2 * n - 3):
                                max_x1(t)
                                normalise_x1(t + 2)

            def normalise_x1(t):
                if t >= 2:
                    dve.wait_ge(s_x2t, t - 1)
                    dve.wait_ge(s_st2, t - 1)
                ts(xn[t % 2], X[:, t * N:(t + 1) * N], rstd[:, t:t + 1], nmr[:, t:t + 1],
                   ALU.mult, ALU.add).then_inc(s_x2n, 1)

            def max_x1(t):
                dve.wait_ge(s_x2n, t + 1)
                nc.vector.tensor_reduce(a_max[:, t:t + 1], xn[t % 2], AX_X, ALU.max,
                                        apply_absolute_value=True).then_inc(s_st2, 1)

            normalise(0, 0)
            normalise(0, 1)
            q_lower(0, 0)
            gate_up_weights_lower(0, 3)
            k_lower(0, 0)
            normalise(1, 0)
            gate_up_weights_lower(3, 6)
            q_lower(0, 1)
            gate_up_weights_lower(6, 9)
            k_lower(0, 1)
            gate_up_weights_lower(9, 12)
            v_lower(0, 0)
            row_max(0, 0, 0)
            gate_up_weights_lower(12, 14)
            row_max(0, 0, 1)
            split_max(0, 0)
            gate_up_weights_lower(14, 17)
            row_max(0, 1, 0)
            gate_up_weights_lower(17, 19)
            row_max(0, 1, 1)
            split_max(0, 1)
            gate_up_weights_lower(19, 22)
            residual_start(0, 0)
            passes_ahead(dve, attention_pass)
            batch_out(PAIRS - 1, 2)
            max_x1(4)
            normalise_x1(6)
            batch_out(PAIRS - 1, 3)
            max_x1(5)
            normalise_x1(7)
            residual(PAIRS - 1, 1)
            for u in range(2):
                dve.wait_ge(s_x1[u], PAIRS)
            for t in range(TILES - 2, TILES):
                last = nc.vector.bn_stats(stats[:, 6 * t:6 * t + 6], X[:, t * N:(t + 1) * N])
            wv.step(last)
            max_x1(6)
            max_x1(7)
            layernorm_scales(3, E, TILES)
            normalise_x1(E)
            for t in range(E + 1, TILES):
                normalise_x1(t)
                max_x1(t - 1)
            max_x1(TILES - 1)
            dve.wait_ge(s_st2, TILES)
            nc.vector.reduce_max(sc[:, 25:26], a_max[:, :], AX_X).then_inc(s_amax, 1)
            dve.wait_ge(s_aall, 1)

            wv.step(ts(A_G, A_MAX, 1.0 / (FP8_MAX * 6.0), SCALE_FLOOR, ALU.mult, ALU.max))
            wv.step(nc.vector.reciprocal(A_RG, A_G))
            wv.step(ts(A_C1, A_RG, 1.0 / FP8_MAX, None, ALU.mult))
            tt(A_OUT, A_G, W_DOWN[:, 0:1], ALU.mult).then_inc(s_ag, 1)
            dve.wait_ge(s_ag, 1)

            OB_N = SELECT // BLK
            CHAIN2 = 12

            def left_over(t, r, tmp, rounded, count):
                tt(tmp[:, 0:SELECT], t, r, ALU.subtract).then_inc(rounded, 1)
                dve.wait_ge(rounded, count)

            def second_quantisation(ch, s, tmp, done):
                o_res, o_m = tmp[:, 0:SELECT], tmp[:, SELECT:2 * SELECT]
                o_s, o_rs = tmp[:, 2 * SELECT:2 * SELECT + OB_N], tmp[:, 2 * SELECT + OB_N:2 * SELECT + 2 * OB_N]
                ch.mark(nc.vector.tensor_reduce(o_s, blk(o_res), AX_X, ALU.max, apply_absolute_value=True))
                yield
                ch.wait()
                ch.mark(tt(o_s, o_s, s, ALU.mult))
                yield
                ch.wait()
                ch.mark(ts(o_s, o_s, 1.0 / FP8_MAX, SCALE_FLOOR, ALU.mult, ALU.max))
                yield
                ch.wait()
                ch.mark(nc.vector.reciprocal(o_rs, o_s))
                yield
                ch.wait()
                ch.mark(tt(o_rs, o_rs, s, ALU.mult))
                yield
                ch.wait()
                ch.mark(tt(blk(o_res), blk(o_res), bc(o_rs, OB_N), ALU.mult))
                yield
                ch.wait()
                ch.mark(ts(o_m.bitcast(I32), o_res.bitcast(I32), EXPONENT, None, ALU.bitwise_and))
                yield
                ch.wait()
                ch.mark(ts(o_m, o_m, ROUND_FP8, ROUND_FP8_LEAST, ALU.mult, ALU.max))
                yield
                ch.wait()
                ch.mark(tt(o_res, o_res, o_m, ALU.add))
                yield
                ch.wait()
                ch.mark(tt(o_res, o_res, o_m, ALU.subtract))
                yield
                ch.wait()
                tt(blk(o_res), blk(o_res), bc(o_s, OB_N), ALU.mult).then_inc(done, 1)

            CHAIN1 = 5

            def scale_x(ii, u):
                ch = Chain(dve, s_g1, (ii * 2 + u) * CHAIN1, CHAIN1)
                src = PS[:, 4 + u, :]
                A, t, m = qa
                s_blk, rs_blk = a_blk[:, u * NB:(u + 1) * NB], a_blk[:, (2 + u) * NB:(3 + u) * NB]
                since(dve, s_gx[u], ii + 1)
                ch.step(nc.vector.tensor_reduce(rs_blk, blk(src), AX_X, ALU.max, apply_absolute_value=True))
                ch.step(ts(s_blk, rs_blk, A_C1, SCALE_FLOOR, ALU.mult, ALU.max))
                ch.step(ts(rs_blk, s_blk, A_G, None, ALU.mult))
                ch.step(nc.vector.reciprocal(rs_blk, rs_blk))
                if u == 1:
                    since(dve, s_ga[0], ii + 1)
                else:
                    since(dve, s_ga[1], ii)
                ch.step(tt(blk(t), blk(src), bc(rs_blk, NB), ALU.mult))
                ts(m.bitcast(I32), t.bitcast(I32), EXPONENT, None, ALU.bitwise_and).then_inc(s_gm[u], 1)
                ch.close()

            def round_x(ii, u):
                A, t, m = qa
                since(dve, s_gm2[u], ii + 1)
                if u == 1:
                    since(dve, s_gt2[0], ii + 1)
                else:
                    since(dve, s_gt2[1], ii)
                ch = Chain(dve, s_g2, (ii * 2 + u) * CHAIN2, CHAIN2)
                ch.step(stt(A, m, ROUND_FP8_LEAST, t, ALU.add, ALU.add))
                ch.step(stt(A, m, ROUND_FP8_LEAST, A, ALU.add, ALU.subtract, reverse1=True))
                left_over(t[:, N - SELECT:N], A[:, N - SELECT:N], t, s_gr[u], ii + 1)
                for _ in second_quantisation(ch, a_blk[:, u * NB + NB - OB_N:(u + 1) * NB], t, s_go[u]):
                    pass
                ch.close()

            def a_lower(ii, u):
                since(dve, s_ghi[u], ii + 1)
                products_read(dve, ii, u)
                tt(at_lo[u][:, :], PS[:, 6 + u, :], at_hi[u][:, :], ALU.subtract).then_inc(s_glo[u], 1)

            def hidden(ii, n):
                slot, u, c = n % 2, n // 3, n % 3
                w_n = CHUNK[c]
                since(dve, s_sg[slot], ii * 3 + n // 2 + 1)
                t = ii * 2 + u
                stt(H[:, bass.ds(t * HID + CSTART[c], w_n)], PS[:, 2 + slot, 0:w_n], A_OUT, sg[slot][:, 0:w_n],
                    ALU.mult, ALU.mult).then_inc(s_h[slot], 1)

            def hidden_max(ii, u):
                for slot in range(2):
                    n = 3 * u + 2
                    k = ii * 3 + (n // 2 + 1 if slot == n % 2 else (n + 1) // 2)
                    since(dve, s_h[slot], k)
                t = ii * 2 + u
                hb = h_blk[:, bass.ds(t * HB, HB)]
                ch = Chain(dve, s_hb, t * 3, 3)
                ch.step(nc.vector.tensor_reduce(hb, blk(H[:, bass.ds(t * HID, HID)]), AX_X, ALU.max,
                                                apply_absolute_value=True))
                nc.vector.tensor_reduce(h_top[:, bass.ds(t, 1)], hb, AX_X, ALU.max).then_inc(s_htop, 1)
                return ch

            def hidden_reciprocals(ii, u, ch):
                t = ii * 2 + u
                hb, hr = h_blk[:, bass.ds(t * HB, HB)], XG[:, bass.ds(t * P + RCP, HB)]
                ch.step(ts(rc_tmp, hb, 1e-30, None, ALU.max))
                ch.step(nc.vector.reciprocal(rc_tmp, rc_tmp))
                ch.close()
                since(dve, s_gx[u], ii + 1)
                ts(hr, rc_tmp, FP8_MAX, None, ALU.mult).then_inc(s_hrc, 1)

            def gate_up_pass(ii, ahead):
                for u in range(2):
                    i1, u1, a1 = later(ii, u, 1)
                    i2, u2, a2 = later(ii, u, 2)
                    if a1 <= ahead:
                        round_x(i1, u1)
                    hidden(ii, 3 * u)
                    if a2 <= ahead:
                        scale_x(i2, u2)
                    hidden(ii, 3 * u + 1)
                    if a1 <= ahead:
                        a_lower(i1, u1)
                    hidden(ii, 3 * u + 2)
                    ch = hidden_max(ii, u)
                    if ahead == 0 and u == 1:
                        dve.wait_ge(s_htop, TILES)
                        nc.vector.reduce_max(sc[:, 26:27], h_top[:, :], AX_X).then_inc(s_hmax, 1)
                    hidden_reciprocals(ii, u, ch)

            scale_x(0, 0)
            round_x(0, 0)
            scale_x(0, 1)
            a_lower(0, 0)
            for i in range(4):
                dve.wait_ge(s_x2d[i], TILES // 4 * 16)
            dve.wait_ge(s_x1d, TILES * 16)
            passes_ahead(dve, gate_up_pass)

            dve.wait_ge(s_hrc, TILES)
            for u in range(2):
                dve.wait_ge(s_gx[u], PAIRS)
            dve.wait_ge(s_hall, 1)
            wv.step(ts(H_G, H_MAX, 1.0 / (FP8_MAX * 6.0), SCALE_FLOOR, ALU.mult, ALU.max))
            wv.step(nc.vector.reciprocal(H_RG, H_G))
            wv.step(ts(H_LIM, H_RG, 1.0 / SCALE_FLOOR, None, ALU.mult))
            rcp = XG[:, RCP:RCP + TILES * P].rearrange("p (t c) -> p t c", c=P)[:, :, 0:HB]
            for lo, hi in ((0, 1), (1, TILES)):
                ts(rcp[:, lo:hi, :], rcp[:, lo:hi, :], H_LIM, None, ALU.min).then_inc(s_hsc, 1)
            tt(H_OUT, H_G, W_DOWN[:, 1:2], ALU.mult)
            wv.step(ts(H_C1, H_RG, 1.0 / FP8_MAX, None, ALU.mult))
            tt(H_OUT, H_OUT, T2, ALU.mult)
            ts(h_blk[:, :], h_blk[:, :], H_C1, SCALE_FLOOR, ALU.mult, ALU.max).then_inc(s_hsc, 1)
            dve.wait_ge(s_hsc, 3)

            def exponents_h(ii, u):
                t = ii * 2 + u
                since(dve, s_ht[u], ii + 1)
                ts(hm[u].bitcast(I32), H[:, bass.ds(t * HID, HID)].bitcast(I32), EXPONENT, None,
                   ALU.bitwise_and).then_inc(s_hm[u], 1)

            def round_h(ii, u):
                t = ii * 2 + u
                A = hA[u]
                since(dve, s_hm2[u], ii + 1)
                since(dve, s_hT[u], ii)
                ch = Chain(dve, s_hround, t * 2, 2)
                ch.step(stt(A, hm[u], ROUND_FP8_LEAST, H[:, bass.ds(t * HID, HID)], ALU.add, ALU.add))
                ch.step(stt(A, hm[u], ROUND_FP8_LEAST, A, ALU.add, ALU.subtract, reverse1=True))
                if u == 1:
                    since(dve, s_hA[0], ii + 1)
                else:
                    since(dve, s_hA[1], ii)
                ch.close()
                left_over(H[:, bass.ds(t * HID + HID - SELECT, SELECT)], A[:, HID - SELECT:HID], h_tmp, s_hr[u], ii + 1)

            def outliers_h(ii, u):
                t = ii * 2 + u
                ch = Chain(dve, s_houtl, t * (CHAIN2 - 2), CHAIN2 - 2)
                yield from second_quantisation(ch, h_blk[:, bass.ds(t * HB + HB - OB_N, OB_N)], h_tmp, s_ho[u])
                ch.close()

            def h_lower(ii, u, part):
                if part == 0:
                    since(dve, s_hhi[u], ii + 1)
                    since(dve, s_y[u], ii)
                lo, hi = part * 4 * P, min((part + 1) * 4 * P, HID // P * P)
                src = PS[:, 3 * u + part, :]
                last = tt(ht_lo[u][:, lo:hi], src[:, 0:hi - lo], ht_hi[u][:, lo:hi], ALU.subtract)
                if hi == HID // P * P:
                    r = rows(IT - 1)
                    last = tt(ht_lo[u][0:r, hi:hi + P], src[0:r, hi - lo:hi - lo + P], ht_hi[u][0:r, hi:hi + P],
                              ALU.subtract)
                    last.then_inc(s_hlo[u], 1)

            def down_pass(ii, ahead):
                for u in range(2):
                    i1, u1, a1 = later(ii, u, 1)
                    i2, u2, a2 = later(ii, u, 2)
                    i3, u3, a3 = later(ii, u, 3)
                    if a2 <= ahead:
                        round_h(i2, u2)
                        outliers = outliers_h(i2, u2)
                        next(outliers)
                    if a3 <= ahead:
                        exponents_h(i3, u3)
                    if a2 <= ahead:
                        next(outliers)
                    if a1 <= ahead:
                        h_lower(i1, u1, 0)
                    if a2 <= ahead:
                        next(outliers)
                        next(outliers)
                    if a1 <= ahead:
                        h_lower(i1, u1, 1)
                    if a2 <= ahead:
                        next(outliers)
                        next(outliers)
                    if a1 <= ahead:
                        h_lower(i1, u1, 2)
                    if a2 <= ahead:
                        next(outliers)
                        next(outliers)
                    if a2 <= ahead:
                        for _ in outliers:
                            pass

            exponents_h(0, 0)
            exponents_h(0, 1)
            round_h(0, 0)
            for _ in outliers_h(0, 0):
                pass
            exponents_h(1, 0)
            round_h(0, 1)
            outliers = outliers_h(0, 1)
            for part in range(3):
                h_lower(0, 0, part)
                next(outliers)
            for _ in outliers:
                pass
            passes_ahead(dve, down_pass)


def kernel(x, ctx_4096, g_xattn, g_ffn, L0_xattn_Wq, L0_xattn_bq, L0_xattn_Wk, L0_xattn_bk, L0_xattn_Wv,
           L0_xattn_bv, L0_xattn_gamma, L0_ffn_w_gate, L0_ffn_w_up, L0_ffn_w_down, L0_ffn_ri_in, L0_ffn_ri_mid):
    import numpy as np
    import concourse.bacc as bacc
    from concourse.bass_utils import run_bass_kernel_spmd

    B, C, N = x.shape
    HID = L0_ffn_w_down.shape[1]
    IT = -(-HID // P)
    x, ctx_in = np.asarray(x), np.asarray(ctx_4096)
    cols = np.zeros((P, 8), np.float32)
    cols[:, 0] = np.asarray(L0_xattn_gamma)[0]
    cols[:, 1] = np.asarray(g_xattn)[0]
    cols[:, 2] = np.asarray(g_ffn)[0]
    cols[:, 3] = np.tile(np.asarray(L0_xattn_bv), 2)
    cols[:C, 4] = np.tile(np.asarray(L0_xattn_bq), 2)
    cols[:C, 5] = np.tile(np.asarray(L0_xattn_bk), 2)
    mid = np.zeros(IT * P, np.int32)
    mid[:HID] = np.asarray(L0_ffn_ri_mid)
    arrays = {
        "x": np.ascontiguousarray(x.reshape(B * C, N)),
        "ctx_in": np.ascontiguousarray(ctx_in.reshape(B * C, N)),
        "w_gu_t": np.ascontiguousarray(np.concatenate([np.asarray(L0_ffn_w_gate).T, np.asarray(L0_ffn_w_up).T], axis=1)),
        "w_down_t": np.ascontiguousarray(np.asarray(L0_ffn_w_down).T),
        "wq_t": np.ascontiguousarray(np.asarray(L0_xattn_Wq).T),
        "wk_t": np.ascontiguousarray(np.asarray(L0_xattn_Wk).T),
        "wv_t": np.ascontiguousarray(np.asarray(L0_xattn_Wv).T),
        "cols": cols,
        "ri_in": np.ascontiguousarray(np.asarray(L0_ffn_ri_in).reshape(-1, P).T),
        "ri_mid": np.ascontiguousarray(mid.reshape(-1, P).T),
    }
    nc = bacc.Bacc("TRN2", target_bir_lowering=False, num_devices=1)
    args = {k: nc.dram_tensor(f"in_{k}", a.shape, mybir.dt.from_np(a.dtype), kind="ExternalInput").ap()
            for k, a in arrays.items()}
    out = nc.dram_tensor("out_y", (B * C, N), F32, kind="ExternalOutput").ap()
    flamingo_block(nc, *args.values(), out)
    r = run_bass_kernel_spmd(nc, [{f"in_{k}": a for k, a in arrays.items()}], core_ids=[0])
    return r.results[0]["out_y"].reshape(B, C, N)
```

```python
import math
from contextlib import ExitStack

import concourse.bass as bass
from concourse import mybir

ALU = mybir.AluOpType
ACT = mybir.ActivationFunctionType
AX_X = mybir.AxisListType.X
F32 = mybir.dt.float32
F16 = mybir.dt.float16
I32 = mybir.dt.int32
RMAX = bass.bass_isa.ReduceOp.max

P = 128
BLK = 16
FP8_MAX = 448.0
INT4_MAX = 7.0
SELECT = 128
SCALE_FLOOR = 1e-8
LN_EPS = 1e-5
LN_P_SCALE = 10 * math.log(2)
MAX_SCALE = 256.0
EXPONENT = 0x7F800000
ROUND_INT = 1.5 * 2.0 ** 23
ROUND_FP8 = 1.5 * 2.0 ** 20
ROUND_FP8_LEAST = ROUND_FP8 * 2.0 ** -6
W_TOP = 16.0


class Chain:

    def __init__(self, eng, sem, start, per_pass):
        self.eng, self.sem, self.start, self.per_pass, self.k = eng, sem, start, per_pass, 0

    def mark(self, ins):
        ins.then_inc(self.sem, 1)
        self.k += 1
        return self.start + self.k

    def step(self, ins):
        self.eng.wait_ge(self.sem, self.mark(ins))

    def wait(self):
        self.eng.wait_ge(self.sem, self.start + self.k)

    def close(self):
        assert self.k == self.per_pass, (self.k, self.per_pass)



def flamingo_block(nc, x, ctx_in, w_gu_t, w_down_t, wq_t, wk_t, wv_t, cols, ri_in, ri_mid, out):
    TOK, N = x.shape
    HID = w_down_t.shape[0]
    CH = wv_t.shape[0]
    QK = wq_t.shape[1]
    TILES = TOK // P
    NT = N // P
    IT = -(-HID // P)
    NB, HB = N // BLK, HID // BLK
    GU = 2 * HID
    CHUNK = [464, 464, 448]
    CSTART = [0, 464, 928]
    PAIRS = TILES // 2
    assert sum(CHUNK) == HID and 2 * CH == P and 2 * QK == CH and NT == 4 and TOK % (2 * P) == 0

    def rows(it):
        return min(P, HID - it * P)

    wt_scratch = nc.dram_tensor("wt_scratch", (HID, 2 * N), F32, kind="Internal").ap()
    HALF = TOK // 2
    xt_scratch = [nc.dram_tensor(f"xt_scratch{i}", (N, HALF), F32, kind="Internal").ap() for i in range(2)]
    x1_scratch = nc.dram_tensor("x1_scratch", (TOK, N), F32, kind="Internal").ap()

    ctx = ExitStack()
    with ctx:
        def sb(name, shape, dt=F32):
            return ctx.enter_context(nc.sbuf_tensor(name, shape, dt))

        def sem(name):
            return ctx.enter_context(nc.semaphore(name))

        PS = ctx.enter_context(nc.psum_tensor("PS", [P, 8, 512], F32))

        GT = sb("w_gu", [P, NT * GU])
        w_hi = GT[:, 0:NT * GU // 2].bitcast(F16)
        w_lo = GT[:, NT * GU // 2:NT * GU].bitcast(F16)
        WDG = sb("w_down", [P, IT * N])
        wd_hi = WDG[:, 0:IT * N // 2].bitcast(F16)
        wd_lo = WDG[:, IT * N // 2:IT * N].bitcast(F16)
        H = sb("H", [P, TILES * HID])
        XG = sb("XG", [P, NT * TOK])
        ident = sb("ident", [P, P])
        col = sb("col", [P, 8])
        idx_in = sb("idx_in", [P, NT], I32)
        idx_mid = sb("idx_mid", [P, IT], I32)
        wq2, wk2 = (XG[:, NT * TOK - 256 + 64 * i:NT * TOK - 192 + 64 * i] for i in range(2))
        wv2 = XG[:, NT * TOK - 128:NT * TOK]
        sc = sb("sc", [P, 32])
        T1, T1G, T1GBV, T2 = (sc[:, i:i + 1] for i in range(4))
        W_MAX, W_POW, W_UP, W_DOWN = (sc[:, 4 + 2 * i:6 + 2 * i] for i in range(4))
        A_G, A_RG, A_C1, A_OUT = (sc[:, 12 + i:13 + i] for i in range(4))
        H_G, H_RG, H_C1, H_OUT, H_LIM = (sc[:, 16 + i:17 + i] for i in range(5))
        A_MAX, H_MAX = sc[:, 22:23], sc[:, 23:24]
        NEG_LEAST, ROUND = sc[:, 28:29], sc[:, 29:30]
        ln = sb("ln", [P, 7 * TILES])
        mv = ln[:, 5 * TILES:7 * TILES]
        var, rstd, nmr, ln_a, ln_b = (ln[:, i * TILES:(i + 1) * TILES] for i in range(5))
        a_max = sb("a_max", [P, TILES])

        xg = [sb(f"xg{i}", [P, N]) for i in range(2)]
        qa_all = sb("qa_all", [P, 3 * N])
        mixed = sb("mixed", [P, 2 * NT * P + 2 * 464])

        def cut(buf, n, taken={}):
            lo = taken.get(buf.name, 0)
            taken[buf.name] = lo + n
            assert lo + n <= buf.shape[1]
            return buf[:, lo:lo + n]

        WR = H[:, 0:IT * 2 * N]
        wst = [WR[:, it * 2 * N:(it + 1) * 2 * N] for it in range(IT)]
        WDR = XG[:, 0:NT * HID]
        NWB = IT * 2 * NB + NT * HB
        wsc = XG[:, NT * HID:NT * HID + 2 * NWB]
        ws, wr = wsc[:, 0:NWB], wsc[:, NWB:2 * NWB]
        assert NT * HID + 2 * NWB <= NT * TOK - 256

        X0 = (TILES * HID - TILES * N)
        X = H[:, X0:]
        h_at = 0

        def in_h(n):
            nonlocal h_at
            h_at += n
            assert h_at <= X0
            return H[:, h_at - n:h_at]

        qk_hl = [XG[:, (8 + 2 * i) * N:(10 + 2 * i) * N].bitcast(F16) for i in range(2)]
        p32 = [in_h(2 * N) for _ in range(2)]
        z0 = [in_h(N) for _ in range(2)]
        z = [in_h(N) for _ in range(2)]
        on = [in_h(N) for _ in range(2)]
        xts = [in_h(N) for _ in range(4)]
        p_hi = [in_h(N).bitcast(F16) for _ in range(4)]
        p_lo = [in_h(N).bitcast(F16) for _ in range(4)]
        assert h_at <= IT * 2 * N
        h_at = IT * 2 * N
        q_st = [in_h(N // 2).bitcast(F16) for _ in range(4)]
        k_st = [in_h(N // 2).bitcast(F16) for _ in range(4)]
        assert h_at == IT * 2 * N + 4 * N
        stats = in_h(TILES * 6)
        xn = [xg[i][:, :] for i in range(2)]
        ct = [cut(qa_all, N) for _ in range(2)]
        VW = NT * 2 * (CH + 1)
        v_hi = [cut(mixed, VW // 2 + 4).bitcast(F16) for _ in range(2)]
        v_lo = [cut(mixed, VW // 2 + 4).bitcast(F16) for _ in range(2)]
        nmx = cut(mixed, 4 * 2)
        nm16 = cut(mixed, 4 * 2).bitcast(F16)
        rsum = cut(mixed, 4 * 2)
        ident16 = cut(mixed, P // 2).bitcast(F16)

        qa = [qa_all[:, i * N:(i + 1) * N] for i in range(3)]
        a_blk = sb("a_blk", [P, 4 * NB])
        at_hi = [mixed[:, i * NT * P // 2:(i + 1) * NT * P // 2].bitcast(F16) for i in range(2)]
        at_lo = [mixed[:, (2 + i) * NT * P // 2:(3 + i) * NT * P // 2].bitcast(F16) for i in range(2)]
        sg = [mixed[:, 2 * NT * P + 464 * i:2 * NT * P + 464 * (i + 1)] for i in range(2)]
        h_blk = sb("h_blk", [P, TILES * HB])
        h_top = sb("h_top", [P, TILES])
        rc_tmp = ln[:, 0:HB]

        hA = [XG[:, i * HID:(i + 1) * HID] for i in range(2)]
        hm = [XG[:, (2 + i) * HID:(3 + i) * HID] for i in range(2)]
        ATW = IT * P
        ht_hi = [qa_all[:, i * ATW // 2:(i + 1) * ATW // 2].bitcast(F16) for i in range(2)]
        ht_lo = [mixed[:, i * ATW // 2:(i + 1) * ATW // 2].bitcast(F16) for i in range(2)]
        y_out = [GT[:, i * N:(i + 1) * N] for i in range(2)]
        h_tmp = XG[:, 4 * HID:4 * HID + 2 * SELECT + 2 * SELECT // BLK]
        RCP = (NT - 1) * TOK
        assert 4 * HID + 2 * SELECT + 2 * SELECT // BLK <= RCP and HB <= P

        small_loaded = sem("small_loaded")
        x_loaded = sem("x_loaded")
        ident_zeroed = sem("ident_zeroed")
        ident_ready = sem("ident_ready")
        zeros_set = sem("zeros_set")
        attn_weights_loaded = sem("attn_weights_loaded")
        gu_gathered = sem("gu_gathered")
        down_gathered = sem("down_gathered")
        gu_transposed = sem("gu_transposed")
        gu_staged = sem("gu_staged")
        w_scaled = sem("w_scaled")
        w_divided = sem("w_divided")
        w_rounded = sem("w_rounded")
        gu_stored = sem("gu_stored")
        gu_regathered = sem("gu_regathered")
        down_transposed = sem("down_transposed")
        down_staged = sem("down_staged")
        dve_steps = sem("dve_steps")
        w_max_rows = sem("w_max_rows")
        w_max_all = sem("w_max_all")
        w_power = sem("w_power")
        w_quantised = sem("w_quantised")
        w_back = sem("w_back")
        w_upper = sem("w_upper")
        w_lower = sem("w_lower")
        tanh_done = sem("tanh_done")
        ln_var = sem("ln_var")
        ln_root = sem("ln_root")
        ln_scales = sem("ln_scales")

        block = ctx.enter_context(nc.Block())
        bc = lambda ap, nb: ap.rearrange("p (b o) -> p b o", o=1).broadcast_to([ap.shape[0], nb, BLK])
        blk = lambda ap: ap.rearrange("p (b e) -> p b e", e=BLK)

        ctx_loaded = [sem(f"ctx_loaded{i}") for i in range(2)]
        xn_ready = [sem(f"xn_ready{i}") for i in range(2)]
        q_projected = sem("q_projected")
        k_projected = sem("k_projected")
        v_projected = sem("v_projected")
        q_upper_ready = sem("q_upper_ready")
        q_lower_ready = sem("q_lower_ready")
        k_upper_ready = sem("k_upper_ready")
        k_lower_ready = sem("k_lower_ready")
        v_upper_ready = sem("v_upper_ready")
        v_lower_ready = sem("v_lower_ready")
        constants_set = sem("constants_set")
        qk_stacked = [sem(f"qk_stacked{i}") for i in range(4)]
        scores_ready = [sem(f"scores_ready{i}") for i in range(2)]
        maxima_ready = [sem(f"maxima_ready{i}") for i in range(2)]
        max_upper_ready = sem("max_upper_ready")
        max_split = sem("max_split")
        max_rows_made = sem("max_rows_made")
        max_rows_stacked = sem("max_rows_stacked")
        scores_t_ready = [sem(f"scores_t_ready{i}") for i in range(2)]
        exp_ready = [sem(f"exp_ready{i}") for i in range(2)]
        p_upper_ready = [sem(f"p_upper_ready{i}") for i in range(2)]
        p_lower_ready = [sem(f"p_lower_ready{i}") for i in range(2)]
        pv_done = [sem(f"pv_done{i}") for i in range(2)]
        sums_inverted = sem("sums_inverted")
        attn_normalised = sem("attn_normalised")
        attn_transposed = [sem(f"attn_transposed{i}") for i in range(2)]
        z0_ready = [sem(f"z0_ready{i}") for i in range(2)]
        z_ready = [sem(f"z_ready{i}") for i in range(2)]
        x1_ready = [sem(f"x1_ready{i}") for i in range(2)]
        x1_stored = sem("x1_stored")
        x1_max_taken = sem("x1_max_taken")
        x1_normalised = sem("x1_normalised")
        x1_transposed = sem("x1_transposed")
        x1_staged = sem("x1_staged")
        x1t_stored = [sem(f"x1t_stored{i}") for i in range(4)]
        a_max_rows = sem("a_max_rows")
        a_max_all = sem("a_max_all")
        a_scale_ready = sem("a_scale_ready")
        x_gathered = [sem(f"x_gathered{i}") for i in range(2)]
        gathered_out = [sem(f"gathered_out{i}") for i in range(2)]
        tokens_back = [sem(f"tokens_back{i}") for i in range(2)]
        scale_steps = sem("scale_steps")
        round_steps = sem("round_steps")
        a_exponents = [sem(f"a_exponents{i}") for i in range(2)]
        a_constants = [sem(f"a_constants{i}") for i in range(2)]
        a_rounded = [sem(f"a_rounded{i}") for i in range(2)]
        a_outliers = [sem(f"a_outliers{i}") for i in range(2)]
        a_rescaled = [sem(f"a_rescaled{i}") for i in range(2)]
        outliers_scaled = sem("outliers_scaled")
        a_quantised = [sem(f"a_quantised{i}") for i in range(2)]
        a_transposed = [sem(f"a_transposed{i}") for i in range(2)]
        a_upper = [sem(f"a_upper{i}") for i in range(2)]
        a_lower_ready = [sem(f"a_lower_ready{i}") for i in range(2)]
        gate_up_done = [sem(f"gate_up_done{i}") for i in range(2)]
        silu_done = [sem(f"silu_done{i}") for i in range(2)]
        h_ready = [sem(f"h_ready{i}") for i in range(2)]
        h_max_steps = sem("h_max_steps")
        h_inverted = sem("h_inverted")
        h_top_ready = sem("h_top_ready")
        h_max_rows = sem("h_max_rows")
        h_max_all = sem("h_max_all")
        h_round_steps = sem("h_round_steps")
        h_outlier_steps = sem("h_outlier_steps")
        h_divided = [sem(f"h_divided{i}") for i in range(2)]
        h_exponents = [sem(f"h_exponents{i}") for i in range(2)]
        h_constants = [sem(f"h_constants{i}") for i in range(2)]
        h_rounded = [sem(f"h_rounded{i}") for i in range(2)]
        h_outliers = [sem(f"h_outliers{i}") for i in range(2)]
        h_rescaled = [sem(f"h_rescaled{i}") for i in range(2)]
        h_scales = sem("h_scales")
        h_quantised = [sem(f"h_quantised{i}") for i in range(2)]
        h_transposed = [sem(f"h_transposed{i}") for i in range(2)]
        h_upper = [sem(f"h_upper{i}") for i in range(2)]
        h_lower_ready = [sem(f"h_lower_ready{i}") for i in range(2)]
        y_done = [sem(f"y_done{i}") for i in range(2)]
        y_scaled_ready = sem("y_scaled_ready")
        x1_loaded = [sem(f"x1_loaded{i}") for i in range(2)]
        out_ready = [sem(f"out_ready{i}") for i in range(2)]
        out_stored = [sem(f"out_stored{i}") for i in range(2)]


        def since(eng, sem, count):
            if not isinstance(count, int) or count > 0:
                eng.wait_ge(sem, count)

        def passes_ahead(eng, body):
            body(0, 2)
            with eng.Fori(1, PAIRS - 2) as ii:
                body(ii, 2)
            body(PAIRS - 2, 1)
            body(PAIRS - 1, 0)

        def later(ii, u, d):
            return ii + (u + d) // 2, (u + d) % 2, (u + d) // 2

        def products_read(eng, ii, u):
            n = 3 * u + 2
            k = ii * 3 - 3 + n // 2 + 1
            since(eng, gate_up_done[n % 2], k)

        E = TILES // 2
        W1 = IT * 2 * NB
        w_items = [(WDR[:, ot * HID:(ot + 1) * HID], P, W1 + ot * HB, HB) for ot in range(NT)] + \
                  [(wst[it][0:rows(it), :], rows(it), it * 2 * NB, 2 * NB) for it in range(IT)]

        @block.sync
        def _(sp):
            sp.dma_start(idx_in[:, :], ri_in).then_inc(small_loaded, 16)
            sp.dma_start(idx_mid[:, :], ri_mid).then_inc(small_loaded, 16)
            sp.dma_start(col[:, :], cols).then_inc(small_loaded, 16)
            sp.wait_ge(zeros_set, 1)
            for h in range(2):
                lo, hi = h * CH, (h + 1) * CH
                sp.dma_start(wq2[lo:hi, h * QK:(h + 1) * QK], wq_t).then_inc(attn_weights_loaded, 16)
                sp.dma_start(wk2[lo:hi, h * QK:(h + 1) * QK], wk_t).then_inc(attn_weights_loaded, 16)
                sp.dma_start(wv2[lo:hi, lo:hi], wv_t).then_inc(attn_weights_loaded, 16)
            sp.wait_ge(gu_gathered, NT * 16)
            for t in range(TILES):
                sp.dma_start(X[:, t * N:(t + 1) * N], x[t * P:(t + 1) * P, :]).then_inc(x_loaded, 16)
            for it in range(IT):
                sp.wait_ge(w_quantised, NT + it + 1)
                sp.dma_start(wt_scratch[it * P:it * P + rows(it), :], wst[it][0:rows(it), :]).then_inc(gu_stored, 16)
            def load_ctx(ii, u):
                src = ctx_in[bass.ds(ii * (2 * P) + u * P, P), :]
                since(sp, z0_ready[u], ii)
                since(sp, v_projected, ii * 2 + u - 1)
                since(sp, k_projected, ii * 2 + u - 1)
                sp.dma_start(ct[u], src).then_inc(ctx_loaded[u], 16)

            def stack(ii, u, b):
                n = 2 * u + b
                if b == 0:
                    since(sp, k_projected, ii * 2 + u + 1)
                else:
                    since(sp, scores_t_ready[1], ii * 4 + n - 3)
                r = slice(b * QK, (b + 1) * QK)
                qh, ql, kh, kl = (qk_hl[u][r, i * N:(i + 1) * N] for i in range(4))
                for dst, parts in ((q_st[n], (qh, qh, ql)), (k_st[n], (kh, kl, kh))):
                    if b == 0 and dst is k_st[n]:
                        since(sp, k_lower_ready, ii * 2 + u + 1)
                    for i, part in enumerate(parts):
                        sp.dma_start(dst[i * QK:(i + 1) * QK, :], part).then_inc(qk_stacked[n], 16)

            def store_x1(ii, u):
                made = ii + 1
                dst, src = x1_scratch[bass.ds(ii * (2 * P) + u * P, P), :], X[:, bass.ds(ii * (2 * N) + u * N, N)]
                since(sp, x1_ready[u], made)
                sp.dma_start(dst, src).then_inc(x1_stored, 16)

            def attention_pass(ii, ahead):
                for u in range(2):
                    i2, u2, a2 = later(ii, u, 2)
                    i3, u3, a3 = later(ii, u, 3)
                    if a2 <= ahead:
                        stack(i2, u2, 0)
                    if a3 <= ahead:
                        load_ctx(i3, u3)
                    if a2 <= ahead:
                        stack(i2, u2, 1)
                    if u == 1:
                        if ahead > 0:
                            store_x1(ii, 0)
                    elif not (isinstance(ii, int) and ii == 0):
                        store_x1(ii - 1, 1)

            load_ctx(0, 0)
            load_ctx(0, 1)
            for n in range(4):
                stack(0, n // 2, n % 2)
            load_ctx(1, 0)
            passes_ahead(sp, attention_pass)
            for t in range(TILES):
                if t == E:
                    store_x1(PAIRS - 1, 0)
                    store_x1(PAIRS - 1, 1)
                sp.wait_ge(x1_staged, t + 1)
                half, c = divmod(t * P, HALF)
                sp.dma_start(xt_scratch[half].rearrange("(a p) t -> p a t", p=P)[:, :, c:c + P],
                             xts[t % 4].rearrange("p (a t) -> p a t", a=NT)).then_inc(x1t_stored[t % 4], 16)
            sp.wait_ge(x1_stored, TILES * 16)
            for u in range(2):
                sp.wait_ge(tokens_back[u], PAIRS)
            def output_pass(ii):
                for u in range(2):
                    since(sp, out_stored[u], ii * 16)
                    sp.dma_start(xg[u][:, :], x1_scratch[bass.ds(ii * (2 * P) + u * P, P), :]).then_inc(x1_loaded[u], 16)
                for u in range(2):
                    since(sp, out_ready[u], ii + 1)
                    sp.dma_start(out[bass.ds(ii * (2 * P) + u * P, P), :], xg[u][:, :]).then_inc(out_stored[u], 16)

            output_pass(0)
            with sp.Fori(1, PAIRS) as ii:
                output_pass(ii)
            for u in range(2):
                sp.wait_ge(out_stored[u], PAIRS * 16)
            for i in range(4):
                sp.wait_ge(x1t_stored[i], TILES // 4 * 16)
            sp.wait_ge(x1_stored, TILES * 16)

        @block.gpsimd
        def _(pool):
            nc.gpsimd.memset(wq2[:, :], 0.0)
            nc.gpsimd.memset(wk2[:, :], 0.0)
            nc.gpsimd.memset(sc[:, :], 0.0)
            nc.gpsimd.memset(wv2[:, :], 0.0).then_inc(zeros_set, 1)
            pool.wait_ge(zeros_set, 1)
            nc.gpsimd.memset(NEG_LEAST, -ROUND_FP8_LEAST)
            nc.gpsimd.memset(ROUND, ROUND_INT)
            nc.gpsimd.memset(ident[:, :], 0.0).then_inc(ident_zeroed, 1)
            pool.wait_ge(ident_zeroed, 1)
            nc.gpsimd.affine_select(out=ident[:, :], in_=ident[:, :], compare_op=ALU.not_equal, fill=1.0, base=0,
                                    pattern=[[-1, P]], channel_multiplier=1).then_inc(ident_ready, 1)
            pool.wait_ge(small_loaded, 48)
            for it in range(IT):
                r = rows(it)
                pool.indirect_dma_start(WDG[0:r, it * N:(it + 1) * N], None, w_down_t,
                                        bass.IndirectOffsetOnAxis(ap=idx_mid[0:r, it:it + 1], axis=0)).then_inc(down_gathered, 16)
            for jt in range(NT):
                pool.indirect_dma_start(GT[:, jt * GU:(jt + 1) * GU], None, w_gu_t,
                                        bass.IndirectOffsetOnAxis(ap=idx_in[:, jt:jt + 1], axis=0)).then_inc(gu_gathered, 16)
            nc.gpsimd.memset(ident16, 0.0).then_inc(ident_zeroed, 1)
            pool.wait_ge(ident_zeroed, 2)
            nc.gpsimd.affine_select(out=ident16, in_=ident16, compare_op=ALU.not_equal, fill=1.0, base=0,
                                    pattern=[[-1, P]], channel_multiplier=1).then_inc(constants_set, 1)
            pool.wait_ge(constants_set, 1)
            for n in range(4):
                nc.gpsimd.memset(k_st[n][3 * QK:3 * QK + 3, :], MAX_SCALE).then_inc(constants_set, 1)
                pool.wait_ge(constants_set, 2 * n + 2)
                nc.gpsimd.memset(q_st[n][3 * QK:3 * QK + 3, :], LN_P_SCALE / MAX_SCALE).then_inc(constants_set, 1)
                pool.wait_ge(constants_set, 2 * n + 3)
            for u in range(2):
                nc.gpsimd.memset(v_hi[u], 1.0)
                nc.gpsimd.memset(v_lo[u], 0.0).then_inc(constants_set, 1)
                pool.wait_ge(constants_set, u + 10)
            for k, (w, r, b0, nb) in enumerate(w_items):
                pool.wait_ge(w_scaled, k + 1)
                nc.gpsimd.tensor_tensor(blk(w), blk(w), bc(wr[0:r, b0:b0 + nb], nb), ALU.mult).then_inc(w_divided, 1)
            pool.wait_ge(w_max_rows, 1)
            nc.gpsimd.partition_all_reduce(W_POW, W_MAX, P, RMAX).then_inc(w_max_all, 1)
            pool.wait_ge(gu_stored, 16 * IT)
            for it in range(IT):
                r = rows(it)
                pool.indirect_dma_start(WR[0:r, it * 2 * N:(it + 1) * 2 * N], None, wt_scratch,
                                        bass.IndirectOffsetOnAxis(ap=idx_mid[0:r, it:it + 1], axis=0)).then_inc(gu_regathered, 16)
            pool.wait_ge(ln_scales, 1)

            def p_lower(ii, n, half):
                slot = 2 * (n % 2) + half
                since(pool, p_upper_ready[half], ii * 4 + n + 1)
                since(pool, pv_done[half], ii * 4 + n - 1)
                nc.gpsimd.tensor_tensor(p_lo[slot], p32[half], p_hi[slot], ALU.subtract).then_inc(p_lower_ready[half], 1)

            def residual_base(ii, u):
                since(pool, z0_ready[u], ii + 1)
                since(pool, x1_ready[u], ii)
                nc.gpsimd.tensor_tensor(z[u], z0[u], X[:, bass.ds(ii * (2 * N) + u * N, N)],
                                        ALU.add).then_inc(z_ready[u], 1)

            def attention_pass(ii, ahead):
                for n in range(4):
                    for half in range(2):
                        p_lower(ii, n, half)
                    i1, u1, a1 = later(ii, n // 2, 1)
                    if n % 2 == 1 and a1 <= ahead:
                        residual_base(i1, u1)

            residual_base(0, 0)
            passes_ahead(pool, attention_pass)

            def gather_half(half):
                for i in range(4):
                    pool.wait_ge(x1t_stored[i], (half + 1) * PAIRS // 4 * 16)
                for jt in range(NT):
                    c = jt * TOK + half * HALF
                    pool.indirect_dma_start(XG[:, c:c + HALF], None, xt_scratch[half],
                                            bass.IndirectOffsetOnAxis(ap=idx_in[:, jt:jt + 1],
                                                                      axis=0)).then_inc(x_gathered[half], 16)

            gather_half(0)
            pool.wait_ge(a_max_rows, 1)
            nc.gpsimd.partition_all_reduce(A_MAX, sc[:, 25:26], P, RMAX).then_inc(a_max_all, 1)
            pool.wait_ge(x1_transposed, TILES)
            xg_v = XG[:, :].rearrange("p (a t) -> p a t", a=NT)
            def copy_out(ii, u):
                since(pool, tokens_back[u], ii)
                nc.gpsimd.tensor_copy(xg[u][:, :].rearrange("p (a t) -> p a t", a=NT),
                                      xg_v[:, :, bass.ds(ii * (2 * P) + u * P, P)]).then_inc(gathered_out[u], 1)

            def times_scale(ii, u):
                A = qa[0]
                since(pool, a_rounded[u], ii + 1)
                nc.gpsimd.tensor_tensor(blk(A), blk(A), bc(a_blk[:, u * NB:(u + 1) * NB], NB), ALU.mult).then_inc(a_rescaled[u], 1)

            def outliers_times_scale(tmp, done, count):
                o_res, o_s = tmp[:, 0:SELECT], tmp[:, 2 * SELECT:2 * SELECT + SELECT // BLK]
                nc.gpsimd.tensor_tensor(blk(o_res), blk(o_res), bc(o_s, SELECT // BLK), ALU.mult).then_inc(done, 1)
                since(pool, done, count)

            def add_outliers(ii, u):
                A = qa[0]
                since(pool, a_outliers[u], ii + 1)
                outliers_times_scale(qa[1], outliers_scaled, ii * 2 + u + 1)
                since(pool, a_rescaled[u], ii + 1)
                nc.gpsimd.tensor_tensor(A[:, N - SELECT:N], A[:, N - SELECT:N], qa[1][:, 0:SELECT],
                                        ALU.add).then_inc(a_quantised[u], 1)

            def gate_up_pass(ii, ahead):
                for u in range(2):
                    i1, u1, a1 = later(ii, u, 1)
                    i3, u3, a3 = later(ii, u, 3)
                    if a1 <= ahead:
                        times_scale(i1, u1)
                        add_outliers(i1, u1)
                    if a3 <= ahead:
                        copy_out(i3, u3)

            gather_half(1)
            pool.wait_ge(x_gathered[0], NT * 16)
            times_scale(0, 0)
            copy_out(1, 0)
            add_outliers(0, 0)
            gate_up_pass(0, 2)
            pool.wait_ge(x_gathered[1], NT * 16)
            with pool.Fori(1, PAIRS - 2) as ii:
                gate_up_pass(ii, 2)
            gate_up_pass(PAIRS - 2, 1)
            gate_up_pass(PAIRS - 1, 0)
            pool.wait_ge(h_max_rows, 1)
            nc.gpsimd.partition_all_reduce(H_MAX, sc[:, 26:27], P, RMAX).then_inc(h_max_all, 1)

            def over_scale(ii, u):
                t = ii * 2 + u
                h = H[:, bass.ds(t * HID, HID)]
                nc.gpsimd.tensor_tensor(blk(h), blk(h), bc(XG[:, bass.ds(t * P + RCP, HB)], HB),
                                        ALU.mult).then_inc(h_divided[u], 1)

            def times_scale_h(ii, u):
                t = ii * 2 + u
                A = hA[u]
                since(pool, h_rounded[u], ii + 1)
                nc.gpsimd.tensor_tensor(blk(A), blk(A), bc(h_blk[:, bass.ds(t * HB, HB)], HB),
                                        ALU.mult).then_inc(h_rescaled[u], 1)

            def add_outliers_h(ii, u):
                A = hA[u]
                since(pool, h_outliers[u], ii + 1)
                outliers_times_scale(h_tmp, outliers_scaled, TILES + (ii * 2 + u + 1))
                since(pool, h_rescaled[u], ii + 1)
                nc.gpsimd.tensor_tensor(A[:, HID - SELECT:HID], A[:, HID - SELECT:HID], h_tmp[:, 0:SELECT],
                                        ALU.add).then_inc(h_quantised[u], 1)

            def final(ii, u):
                since(pool, y_scaled_ready, ii * 2 + u + 1)
                since(pool, x1_loaded[u], ii * 16 + 16)
                nc.gpsimd.tensor_tensor(xg[u][:, :], y_out[u], xg[u][:, :], ALU.add).then_inc(out_ready[u], 1)

            def down_pass(ii, ahead):
                for u in range(2):
                    i2, u2, a2 = later(ii, u, 2)
                    i4, u4, a4 = later(ii, u, 4)
                    if u == 1:
                        final(ii, 0)
                    elif not (isinstance(ii, int) and ii == 0):
                        final(ii - 1, 1)
                    if a2 <= ahead:
                        times_scale_h(i2, u2)
                    if a4 <= ahead:
                        over_scale(i4, u4)
                    if a2 <= ahead:
                        add_outliers_h(i2, u2)

            pool.wait_ge(h_scales, 1)
            over_scale(0, 0)
            pool.wait_ge(h_scales, 2)
            over_scale(0, 1)
            over_scale(1, 0)
            pool.wait_ge(h_scales, 3)
            times_scale_h(0, 0)
            add_outliers_h(0, 0)
            over_scale(1, 1)
            times_scale_h(0, 1)
            add_outliers_h(0, 1)
            passes_ahead(pool, down_pass)
            final(PAIRS - 1, 1)

        @block.tensor
        def _(pe):
            pe.wait_ge(ident_ready, 1)
            pe.wait_ge(down_gathered, IT * 16)
            for ot in range(NT):
                b = 1 + 3 * (ot % 2)
                if ot >= 2:
                    pe.wait_ge(down_staged, ot - 1)
                for it in range(IT):
                    r = rows(it)
                    last = nc.tensor.transpose(PS[:, b + it // 4, (it % 4) * P:(it % 4) * P + r],
                                               WDG[0:r, it * N + ot * P:it * N + (ot + 1) * P], ident[0:r, 0:r])
                last.then_inc(down_transposed, 1)
            pe.wait_ge(down_staged, NT)
            pe.wait_ge(gu_gathered, NT * 16)
            for it in range(IT):
                b = 2 * (it % 2)
                if it >= 2:
                    pe.wait_ge(gu_staged, it - 1)
                r = rows(it)
                for w in range(2):
                    for jt in range(NT):
                        c = jt * GU + w * HID + it * P
                        last = nc.tensor.transpose(PS[0:r, b + w, jt * P:(jt + 1) * P], GT[:, c:c + r], ident[:, :])
                last.then_inc(gu_transposed, 1)
            pe.wait_ge(gu_staged, IT)
            pe.wait_ge(w_quantised, NT)
            for it in range(IT):
                r = rows(it)
                if it >= 4:
                    pe.wait_ge(w_upper, it - 3)
                    pe.wait_ge(w_lower, it - 3)
                for ot in range(NT):
                    last = nc.tensor.transpose(PS[0:r, 2 + it % 4, ot * P:(ot + 1) * P],
                                               WDR[:, ot * HID + it * P:ot * HID + it * P + r], ident[:, :])
                last.then_inc(w_back, 1)

            def gate_up_weights_back(first, last):
                for n in range(IT + first, IT + last):
                    it, w = divmod(n - IT, 2)
                    pe.wait_ge(gu_regathered, IT * 16)
                    pe.wait_ge(w_upper, n - 3)
                    pe.wait_ge(w_lower, n - 3)
                    r = rows(it)
                    for jt in range(NT):
                        c = it * 2 * N + w * N + jt * P
                        done = nc.tensor.transpose(PS[:, 2 + n % 4, jt * P:jt * P + r], WR[0:r, c:c + P], ident[0:r, 0:r])
                    done.then_inc(w_back, 1)

            pe.wait_ge(attn_weights_loaded, 6 * 16)
            pe.wait_ge(constants_set, 11)
            PR, RT = PS[:, 6, :], PS[:, 7, :]

            def project_q(ii, u):
                since(pe, xn_ready[u], ii + 1)
                since(pe, v_upper_ready, ii * 2 + u - 1)
                since(pe, v_lower_ready, ii * 2 + u - 1)
                nc.tensor.matmul(PR[0:2 * QK, :], wq2[:, :], xn[u], start=True, stop=True).then_inc(q_projected, 1)

            def project_k(ii, u):
                since(pe, ctx_loaded[u], ii * 16 + 16)
                since(pe, q_upper_ready, ii * 2 + u + 1)
                since(pe, q_lower_ready, ii * 2 + u + 1)
                nc.tensor.matmul(PR[0:2 * QK, :], wk2[:, :], ct[u], start=True, stop=True).then_inc(k_projected, 1)

            def project_v(ii, u, bank_of):
                ik, uk = bank_of
                since(pe, k_upper_ready, ik * 2 + uk + 1)
                since(pe, k_lower_ready, ik * 2 + uk + 1)
                for mt in range(NT):
                    last = nc.tensor.matmul(PR[:, mt * P:(mt + 1) * P], ct[u][:, mt * P:(mt + 1) * P], wv2[:, :],
                                            start=True, stop=True)
                last.then_inc(v_projected, 1)

            def scores(ii, n, half):
                since(pe, qk_stacked[n], (ii + 1) * 96)
                if half == 0:
                    since(pe, maxima_ready[1], ii * 4 + n)
                else:
                    since(pe, maxima_ready[0], ii * 4 + n + 1)
                for j in range(2):
                    nt = 2 * half + j
                    last = nc.tensor.matmul(PS[:, j, :], q_st[n][0:3 * QK, nt * P:(nt + 1) * P], k_st[n][0:3 * QK, :],
                                            start=True, stop=True)
                last.then_inc(scores_ready[half], 1)

            def maxima_to_rows(ii, n, before):
                g = ii * 4 + n
                since(pe, max_split, g + 1)
                since(pe, max_rows_stacked, g)
                if before is not None:
                    since(pe, x1_ready[before[1]], before[0] + 1)
                for nt in range(NT):
                    c = (n % 2) * 2 * NT + 2 * nt
                    last = nc.tensor.matmul(RT[3 * QK:3 * QK + 2, nt * P:(nt + 1) * P], nm16[:, c:c + 2], ident16,
                                            start=True, stop=True)
                last.then_inc(max_rows_made, 1)

            def scores_less_max(ii, n, half):
                g = ii * 4 + n
                if half == 0:
                    since(pe, max_rows_stacked, g + 1)
                    since(pe, exp_ready[1], g)
                else:
                    since(pe, exp_ready[0], g + 1)
                for j in range(2):
                    mt = 2 * half + j
                    last = nc.tensor.matmul(PS[:, 2 + j, :], k_st[n][0:3 * QK + 3, mt * P:(mt + 1) * P],
                                            q_st[n][0:3 * QK + 3, :], start=True, stop=True)
                last.then_inc(scores_t_ready[half], 1)

            def product_v(ii, n, half):
                g = ii * 4 + n
                u, b, slot = n // 2, n % 2, 2 * (n % 2) + half
                since(pe, p_upper_ready[half], g + 1)
                since(pe, p_lower_ready[half], g + 1)
                if half == 0:
                    since(pe, v_upper_ready, ii * 2 + u + 1)
                    since(pe, v_lower_ready, ii * 2 + u + 1)
                    since(pe, attn_normalised, g - 1)
                for j in range(2):
                    mt = 2 * half + j
                    c = (mt * 2 + b) * (CH + 1)
                    for nt in range(NT):
                        for k, (p, v) in enumerate(((p_hi, v_hi), (p_hi, v_lo), (p_lo, v_hi))):
                            last = nc.tensor.matmul(PS[:, 4 + b, nt * (CH + 1):(nt + 1) * (CH + 1)],
                                                    p[slot][:, j * N + nt * P:j * N + (nt + 1) * P],
                                                    v[u][:, c:c + CH + 1],
                                                    start=(mt == 0 and nt == 0 and k == 0),
                                                    stop=(mt == NT - 1 and nt == NT - 1 and k == 2),
                                                    skip_group_check=True)
                last.then_inc(pv_done[half], 1)

            def out_transpose(ii, u, rows_done):
                since(pe, attn_normalised, ii * 4 + 2 * u + 2)
                since(pe, max_rows_stacked, rows_done)
                for nt in range(NT):
                    last = nc.tensor.transpose(RT[:, nt * P:(nt + 1) * P], on[u][:, nt * P:(nt + 1) * P], ident[:, :])
                last.then_inc(attn_transposed[u], 1)

            def attention_pass(ii, ahead):
                first = isinstance(ii, int) and ii == 0
                for n in range(4):
                    u, b, g = n // 2, n % 2, ii * 4 + n
                    i2, u2, a2 = later(ii, u, 2)
                    i1, u1, a1 = later(ii, u, 1)
                    ip, up = (ii, 0) if u else (ii - 1, 1)
                    i2b, n2 = (ii, n + 2) if n < 2 else (ii + 1, n - 2)
                    i1b, n1 = (ii, n + 1) if n < 3 else (ii + 1, 0)
                    ipb, np_ = (ii, n - 1) if n else (ii - 1, 3)
                    more2 = n < 2 or ahead >= 1
                    more1 = n < 3 or ahead >= 1
                    if more2:
                        scores(i2b, n2, 0)
                    scores_less_max(ii, n, 0)
                    if b == 0 and a2 <= ahead:
                        project_q(i2, u2)
                    if not (first and n == 0):
                        product_v(ipb, np_, 0)
                    if more1:
                        if b == 0 and not (first and n < 4):
                            before = (ii - 1, u)
                        else:
                            before = None
                        maxima_to_rows(i1b, n1, before)
                    if more2:
                        scores(i2b, n2, 1)
                    scores_less_max(ii, n, 1)
                    if b == 0 and a2 <= ahead:
                        project_k(i2, u2)
                    if b == 1:
                        if a1 <= ahead:
                            project_v(i1, u1, (i2, u2) if a2 <= ahead else (ii, u))
                        if not (first and u == 0):
                            out_transpose(ip, up, g + 2 if more1 else g + 1)
                    if not (first and n == 0):
                        product_v(ipb, np_, 1)
                    if ahead == 0 and n >= 2:
                        x1_transpose(2 * n - 4)
                        x1_transpose(2 * n - 3)

            def x1_transpose(t):
                pe.wait_ge(x1_normalised, t + 1)
                if t >= 2:
                    pe.wait_ge(x1_staged, t - 1)
                else:
                    pe.wait_ge(maxima_ready[1], 4 * PAIRS)
                for nt in range(NT):
                    last = nc.tensor.transpose(PS[:, t % 2, nt * P:(nt + 1) * P], xn[t % 2][:, nt * P:(nt + 1) * P], ident[:, :])
                last.then_inc(x1_transposed, 1)

            project_q(0, 0)
            gate_up_weights_back(0, 3)
            project_k(0, 0)
            gate_up_weights_back(3, 6)
            pe.wait_ge(k_upper_ready, 1)
            pe.wait_ge(k_lower_ready, 1)
            project_q(0, 1)
            gate_up_weights_back(6, 9)
            project_k(0, 1)
            gate_up_weights_back(9, 12)
            project_v(0, 0, (0, 1))
            scores(0, 0, 0)
            gate_up_weights_back(12, 14)
            scores(0, 0, 1)
            gate_up_weights_back(14, 17)
            maxima_to_rows(0, 0, None)
            scores(0, 1, 0)
            gate_up_weights_back(17, 19)
            scores(0, 1, 1)
            gate_up_weights_back(19, 22)
            pe.wait_ge(w_upper, 3 * IT)
            pe.wait_ge(w_lower, 3 * IT)
            passes_ahead(pe, attention_pass)
            product_v(PAIRS - 1, 3, 0)
            x1_transpose(4)
            product_v(PAIRS - 1, 3, 1)
            x1_transpose(5)
            pe.wait_ge(x1_ready[0], PAIRS)
            out_transpose(PAIRS - 1, 1, PAIRS * 4)

            for t in range(6, TILES):
                x1_transpose(t)

            pe.wait_ge(x1_staged, TILES)

            def gathered_back(ii, u):
                since(pe, gathered_out[u], ii)
                since(pe, a_exponents[u], ii)
                for jt in range(NT):
                    if isinstance(ii, int) and ii == 0:
                        pe.wait_ge(x_gathered[0], NT * 16)
                        tile = XG[:, jt * TOK + u * P:jt * TOK + (u + 1) * P]
                    else:
                        tile = xg[u][:, jt * P:(jt + 1) * P]
                    last = nc.tensor.transpose(PS[:, 4 + u, jt * P:(jt + 1) * P], tile, ident[:, :])
                last.then_inc(tokens_back[u], 1)

            def a_transpose(ii, u):
                since(pe, a_quantised[u], ii + 1)
                since(pe, a_upper[u], ii)
                since(pe, a_lower_ready[u], ii)
                for jt in range(NT):
                    last = nc.tensor.transpose(PS[:, 6 + u, jt * P:(jt + 1) * P], qa[0][:, jt * P:(jt + 1) * P], ident[:, :])
                last.then_inc(a_transposed[u], 1)

            def gate_up(ii, u, c):
                n = 3 * u + c
                slot = n % 2
                since(pe, silu_done[slot], ii * 3 + n // 2)
                since(pe, h_ready[slot], ii * 3 + n // 2)
                w_n = CHUNK[c]
                for w in range(2):
                    k = 0
                    for jt in range(NT):
                        for a, b in ((at_hi, w_hi), (at_hi, w_lo), (at_lo, w_hi)):
                            cc = jt * GU + w * HID + CSTART[c]
                            last = nc.tensor.matmul(PS[:, 2 * w + slot, 0:w_n], a[u][:, jt * P:(jt + 1) * P],
                                                    b[:, cc:cc + w_n], start=(k == 0), stop=(k == 3 * NT - 1))
                            k += 1
                last.then_inc(gate_up_done[slot], 1)

            def gate_up_pass(ii, ahead):
                for u in range(2):
                    i1, u1, a1 = later(ii, u, 1)
                    i2, u2, a2 = later(ii, u, 2)
                    if a2 <= ahead:
                        gathered_back(i2, u2)
                    since(pe, a_upper[u], ii + 1)
                    since(pe, a_lower_ready[u], ii + 1)
                    gate_up(ii, u, 0)
                    gate_up(ii, u, 1)
                    if a1 <= ahead:
                        a_transpose(i1, u1)
                    gate_up(ii, u, 2)

            gathered_back(0, 0)
            gathered_back(0, 1)
            a_transpose(0, 0)
            passes_ahead(pe, gate_up_pass)

            for slot in range(2):
                pe.wait_ge(silu_done[slot], PAIRS * 3)
                pe.wait_ge(h_ready[slot], PAIRS * 3)

            def h_transpose(ii, u):
                since(pe, h_quantised[u], ii + 1)
                since(pe, h_upper[u], ii)
                since(pe, h_lower_ready[u], ii)
                for it in range(IT):
                    r = rows(it)
                    last = nc.tensor.transpose(PS[0:r, 3 * u + it // 4, (it % 4) * P:(it % 4 + 1) * P],
                                               hA[u][:, it * P:it * P + r], ident[:, :])
                last.then_inc(h_transposed[u], 1)

            def down(ii, u):
                since(pe, h_upper[u], ii + 1)
                since(pe, h_lower_ready[u], ii + 1)
                since(pe, y_scaled_ready, ii * 2 + u - 1)
                k = 0
                for it in range(IT):
                    r = rows(it)
                    for a, b in ((ht_hi, wd_hi), (ht_hi, wd_lo), (ht_lo, wd_hi)):
                        last = nc.tensor.matmul(PS[:, 6 + u, :], a[u][0:r, it * P:(it + 1) * P],
                                                b[0:r, it * N:(it + 1) * N], start=(k == 0), stop=(k == 3 * IT - 1))
                        k += 1
                last.then_inc(y_done[u], 1)

            def down_pass(ii, ahead):
                for u in range(2):
                    i1, u1, a1 = later(ii, u, 1)
                    if a1 <= ahead:
                        h_transpose(i1, u1)
                    down(ii, u)

            h_transpose(0, 0)
            passes_ahead(pe, down_pass)

        @block.scalar
        def _(act):
            act.wait_ge(small_loaded, 48)
            act.wait_ge(zeros_set, 1)
            nc.scalar.activation(T1, col[:, 1:2], ACT.Tanh)
            nc.scalar.activation(T2, col[:, 2:3], ACT.Tanh).then_inc(tanh_done, 1)

            def down_weights_out(ot):
                b = 1 + 3 * (ot % 2)
                act.wait_ge(down_transposed, ot + 1)
                nc.scalar.copy(WDR[:, ot * HID:(ot + 1) * HID],
                               PS[:, b:b + 3, :].rearrange("p b c -> p (b c)")[:, 0:HID]).then_inc(down_staged, 1)

            def gate_up_weights_out(it):
                act.wait_ge(gu_transposed, it + 1)
                r = rows(it)
                b = 2 * (it % 2)
                nc.scalar.copy(wst[it][0:r, :].rearrange("p (w j) -> p w j", w=2),
                               PS[0:r, b:b + 2, :]).then_inc(gu_staged, 1)

            def round_w(k):
                w, r, b0, nb = w_items[k]
                act.wait_ge(w_divided, k + 1)
                nc.scalar.activation(w, w, ACT.Identity, bias=ROUND[0:r, :]).then_inc(w_rounded, 1)

            for ot in range(NT):
                down_weights_out(ot)
            round_w(0)
            round_w(1)
            out = 0
            for k in range(2, len(w_items)):
                while out < min(IT, 2 * k - 2):
                    gate_up_weights_out(out)
                    out += 1
                round_w(k)
            act.wait_ge(w_power, 1)
            for it in range(IT):
                r = rows(it)
                act.wait_ge(w_back, it + 1)
                nc.scalar.activation(wd_hi[0:r, it * N:(it + 1) * N], PS[0:r, 2 + it % 4, :], ACT.Identity,
                                     scale=W_UP[0:r, 1:2]).then_inc(w_upper, 1)

            def gate_up_weights_upper(first, last):
                for n in range(IT + first, IT + last):
                    it, w = divmod(n - IT, 2)
                    r = rows(it)
                    act.wait_ge(w_back, n + 1)
                    nc.scalar.activation(w_hi.rearrange("p (j w i) -> p j w i", j=NT, w=2)[:, :, w, it * P:it * P + r],
                                         PS[:, 2 + n % 4, :].rearrange("p (j i) -> p j i", j=NT)[:, :, 0:r], ACT.Identity,
                                         scale=W_UP[:, 0:1]).then_inc(w_upper, 1)


            def sqrt_var(k, lo, hi):
                act.wait_ge(ln_var, k)
                nc.scalar.activation(ln_a[:, lo:hi], var[:, lo:hi], ACT.Sqrt).then_inc(ln_root, 1)

            sqrt_var(1, 0, TILES)

            PR, RT = PS[:, 6, :], PS[:, 7, :]
            R = slice(0, 2 * QK)

            def halves_free(ii, u):
                for b in range(2):
                    since(act, qk_stacked[2 * u + b], ii * 96)

            def q_upper(ii, u):
                since(act, q_projected, ii * 2 + u + 1)
                halves_free(ii, u)
                nc.scalar.activation(qk_hl[u][R, 0:N], PR[R, :], ACT.Identity, bias=col[R, 4:5]).then_inc(q_upper_ready, 1)

            def k_upper(ii, u):
                since(act, k_projected, ii * 2 + u + 1)
                nc.scalar.activation(qk_hl[u][R, 2 * N:3 * N], PR[R, :], ACT.Identity,
                                     bias=col[R, 5:6]).then_inc(k_upper_ready, 1)

            def v_upper(ii, u):
                since(act, v_projected, ii * 2 + u + 1)
                since(act, pv_done[1], ii * 4 - 4 + 2 * u + 2)
                nc.scalar.copy(v_hi[u][:, 0:NT * 2 * (CH + 1)].rearrange("p (m c) -> p m c", c=CH + 1)[:, :, 0:CH],
                               PR.rearrange("p (m c) -> p m c", c=CH)).then_inc(v_upper_ready, 1)

            def rows_out(ii, n):
                since(act, max_rows_made, ii * 4 + n + 1)
                since(act, scores_t_ready[1], ii * 4 + n - 3)
                r = slice(3 * QK, 3 * QK + 2)
                nc.scalar.copy(q_st[n][r, :], RT[r, :]).then_inc(max_rows_stacked, 1)

            def exp(ii, n, half):
                g = ii * 4 + n
                since(act, scores_t_ready[half], g + 1)
                since(act, p_lower_ready[half], g)
                nc.scalar.activation(p32[half], PS[:, 2:4, :].rearrange("p b c -> p (b c)"), ACT.Exp).then_inc(exp_ready[half], 1)

            def p_upper(ii, n, half):
                g = ii * 4 + n
                since(act, exp_ready[half], g + 1)
                since(act, pv_done[half], g - 1)
                nc.scalar.copy(p_hi[2 * (n % 2) + half], p32[half]).then_inc(p_upper_ready[half], 1)

            def attention_pass(ii, ahead):
                for n in range(4):
                    u, b = n // 2, n % 2
                    i2, u2, a2 = later(ii, u, 2)
                    i1, u1, a1 = later(ii, u, 1)
                    i1b, n1 = (ii, n + 1) if n < 3 else (ii + 1, 0)
                    exp(ii, n, 0)
                    if b == 0 and a2 <= ahead:
                        q_upper(i2, u2)
                    p_upper(ii, n, 0)
                    if n < 3 or ahead >= 1:
                        rows_out(i1b, n1)
                    exp(ii, n, 1)
                    if b == 0 and a2 <= ahead:
                        k_upper(i2, u2)
                    if b == 1 and a1 <= ahead:
                        v_upper(i1, u1)
                    p_upper(ii, n, 1)
                    if ahead == 0:
                        if n == 0:
                            sqrt_var(2, 0, E)
                        if n >= 2:
                            x1_out(2 * n - 4)
                            x1_out(2 * n - 3)

            def x1_out(t):
                act.wait_ge(x1_transposed, t + 1)
                if t >= 4:
                    act.wait_ge(x1t_stored[t % 4], t // 4 * 16)
                nc.scalar.copy(xts[t % 4], PS[:, t % 2, :]).then_inc(x1_staged, 1)

            act.wait_ge(constants_set, 11)
            q_upper(0, 0)
            gate_up_weights_upper(0, 3)
            k_upper(0, 0)
            gate_up_weights_upper(3, 6)
            q_upper(0, 1)
            gate_up_weights_upper(6, 9)
            k_upper(0, 1)
            gate_up_weights_upper(9, 12)
            v_upper(0, 0)
            gate_up_weights_upper(12, 17)
            rows_out(0, 0)
            gate_up_weights_upper(17, 22)
            passes_ahead(act, attention_pass)

            for t in range(4, E):
                x1_out(t)
            sqrt_var(3, E, TILES)
            for t in range(E, TILES):
                x1_out(t)

            def a_hi(ii, u):
                since(act, a_transposed[u], ii + 1)
                products_read(act, ii, u)
                nc.scalar.copy(at_hi[u][:, :], PS[:, 6 + u, :]).then_inc(a_upper[u], 1)

            def silu(ii, n):
                slot = n % 2
                w_n = CHUNK[n % 3]
                since(act, gate_up_done[slot], ii * 3 + n // 2 + 1)
                since(act, h_ready[slot], ii * 3 + n // 2)
                nc.scalar.activation(sg[slot][:, 0:w_n], PS[:, slot, 0:w_n], ACT.Silu,
                                     scale=A_OUT).then_inc(silu_done[slot], 1)

            def round_constant(dst, src):
                return nc.scalar.activation(dst, src, ACT.Relu, scale=ROUND_FP8, bias=NEG_LEAST)

            def a_constant(ii, u):
                since(act, a_exponents[u], ii + 1)
                round_constant(qa[2], qa[2]).then_inc(a_constants[u], 1)

            def gate_up_pass(ii, ahead):
                for u in range(2):
                    i1, u1, a1 = later(ii, u, 1)
                    i2, u2, a2 = later(ii, u, 2)
                    silu(ii, 3 * u)
                    if a2 <= ahead:
                        a_constant(i2, u2)
                    silu(ii, 3 * u + 1)
                    if a1 <= ahead:
                        a_hi(i1, u1)
                    silu(ii, 3 * u + 2)

            act.wait_ge(a_scale_ready, 1)
            a_constant(0, 0)
            a_constant(0, 1)
            a_hi(0, 0)
            passes_ahead(act, gate_up_pass)

            def h_constant(ii, u):
                since(act, h_exponents[u], ii + 1)
                round_constant(hm[u], hm[u]).then_inc(h_constants[u], 1)

            def h_hi(ii, u):
                since(act, h_transposed[u], ii + 1)
                since(act, y_done[u], ii)
                src = PS[:, 3 * u:3 * u + 3, :].rearrange("p b c -> p (b c)")
                FULL, r = HID // P * P, rows(IT - 1)
                nc.scalar.copy(ht_hi[u][:, 0:FULL], src[:, 0:FULL])
                nc.scalar.copy(ht_hi[u][0:r, FULL:FULL + P], src[0:r, FULL:FULL + P]).then_inc(h_upper[u], 1)

            def y_scaled(ii, u):
                since(act, y_done[u], ii + 1)
                since(act, out_ready[u], ii)
                nc.scalar.activation(y_out[u], PS[:, 6 + u, :], ACT.Identity, scale=H_OUT).then_inc(y_scaled_ready, 1)

            def down_pass(ii, ahead):
                for u in range(2):
                    i1, u1, a1 = later(ii, u, 1)
                    i3, u3, a3 = later(ii, u, 3)
                    if u == 1:
                        y_scaled(ii, 0)
                    elif not (isinstance(ii, int) and ii == 0):
                        y_scaled(ii - 1, 1)
                    if a1 <= ahead:
                        h_hi(i1, u1)
                    if a3 <= ahead:
                        h_constant(i3, u3)

            for t in range(3):
                h_constant(t // 2, t % 2)
            h_hi(0, 0)
            passes_ahead(act, down_pass)
            y_scaled(PAIRS - 1, 1)

        @block.vector
        def _(dve):
            ts, tt, stt = nc.vector.tensor_scalar, nc.vector.tensor_tensor, nc.vector.scalar_tensor_tensor
            wv = Chain(dve, dve_steps, 0, 0)
            wv.step(nc.vector.memset(ws, 0.0))
            for k in range(len(w_items) + 3):
                if k < len(w_items):
                    w, r, b0, nb = w_items[k]
                    s_k = ws[0:r, b0:b0 + nb]
                    if k < NT:
                        dve.wait_ge(down_staged, k + 1)
                    else:
                        dve.wait_ge(gu_staged, k - NT + 1)
                    reduced = wv.mark(nc.vector.tensor_reduce(s_k, blk(w), AX_X, ALU.max, apply_absolute_value=True))
                if k >= 3:
                    w0, r0, b00, nb0 = w_items[k - 3]
                    dve.wait_ge(w_rounded, k - 2)
                    stt(blk(w0), blk(w0), -ROUND_INT, bc(ws[0:r0, b00:b00 + nb0], nb0), ALU.add, ALU.mult).then_inc(w_quantised, 1)
                if k < len(w_items):
                    dve.wait_ge(dve_steps, reduced)
                    scaled = wv.mark(ts(s_k, s_k, 1.0 / INT4_MAX, SCALE_FLOOR, ALU.mult, ALU.max))
                    dve.wait_ge(dve_steps, scaled)
                    nc.vector.reciprocal(wr[0:r, b0:b0 + nb], s_k).then_inc(w_scaled, 1)
            dve.wait_ge(zeros_set, 1)
            nc.vector.reduce_max(W_MAX[:, 0:1], ws[:, 0:W1], AX_X)
            nc.vector.reduce_max(W_MAX[:, 1:2], ws[:, W1:NWB], AX_X).then_inc(w_max_rows, 1)
            dve.wait_ge(x_loaded, TILES * 16)
            for t in range(TILES):
                last = nc.vector.bn_stats(stats[:, 6 * t:6 * t + 6], X[:, t * N:(t + 1) * N])
            wv.step(last)
            dve.wait_ge(w_max_all, 1)
            wv.step(ts(W_POW.bitcast(I32), W_POW.bitcast(I32), EXPONENT, None, ALU.bitwise_and))
            wv.step(nc.vector.reciprocal(W_UP, W_POW))
            wv.step(ts(W_DOWN, W_POW, 1.0 / W_TOP, None, ALU.mult))
            ts(W_UP, W_UP, W_TOP, None, ALU.mult).then_inc(w_power, 1)
            dve.wait_ge(w_power, 1)
            for it in range(IT):
                r = rows(it)
                dve.wait_ge(w_upper, it + 1)
                stt(wd_lo[0:r, it * N:(it + 1) * N], PS[0:r, 2 + it % 4, :], W_UP[0:r, 1:2],
                    wd_hi[0:r, it * N:(it + 1) * N], ALU.mult, ALU.subtract).then_inc(w_lower, 1)

            def gate_up_weights_lower(first, last):
                for n in range(IT + first, IT + last):
                    it, w = divmod(n - IT, 2)
                    r = rows(it)
                    dve.wait_ge(w_upper, n + 1)
                    v = lambda a: a.rearrange("p (j w i) -> p j w i", j=NT, w=2)[:, :, w, it * P:it * P + r]
                    stt(v(w_lo), PS[:, 2 + n % 4, :].rearrange("p (j i) -> p j i", j=NT)[:, :, 0:r], W_UP[:, 0:1],
                        v(w_hi), ALU.mult, ALU.subtract).then_inc(w_lower, 1)

            dve.wait_ge(tanh_done, 1)
            wv.step(tt(T1G, T1, col[:, 0:1], ALU.mult))
            wv.step(tt(T1GBV, T1G, col[:, 3:4], ALU.mult))

            def layernorm_scales(k, lo, hi):
                for t in range(lo, hi):
                    last = nc.vector.bn_aggr(mv[:, 2 * t:2 * t + 2], stats[:, 6 * t:6 * t + 6])
                wv.step(last)
                m3 = mv[:, 2 * lo:2 * hi].rearrange("p (t s) -> p t s", s=2)
                v, a, b, r = var[:, lo:hi], ln_a[:, lo:hi], ln_b[:, lo:hi], rstd[:, lo:hi]
                ts(v, m3[:, :, 1], LN_EPS, None, ALU.add).then_inc(ln_var, 1)
                dve.wait_ge(ln_var, k)
                dve.wait_ge(ln_root, k)
                wv.step(nc.vector.reciprocal(r, a))
                wv.step(tt(b, r, r, ALU.mult))
                wv.step(tt(b, b, v, ALU.mult))
                wv.step(ts(b, b, -0.5, 1.5, ALU.mult, ALU.add))
                wv.step(tt(r, r, b, ALU.mult))
                stt(nmr[:, lo:hi], m3[:, :, 0], -1.0, r, ALU.mult, ALU.mult).then_inc(ln_scales, 1)
                dve.wait_ge(ln_scales, k)

            layernorm_scales(1, 0, TILES)

            PR, RT = PS[:, 6, :], PS[:, 7, :]
            R = slice(0, 2 * QK)

            def normalise(ii, u):
                since(dve, q_projected, ii * 2 + u - 1)
                t = ii * 2 + u
                ts(xn[u], X[:, bass.ds(t * N, N)], rstd[:, bass.ds(t, 1)], nmr[:, bass.ds(t, 1)],
                   ALU.mult, ALU.add).then_inc(xn_ready[u], 1)

            def q_lower(ii, u):
                since(dve, q_upper_ready, ii * 2 + u + 1)
                stt(qk_hl[u][R, N:2 * N], PR[R, :], col[R, 4:5], qk_hl[u][R, 0:N], ALU.add,
                    ALU.subtract).then_inc(q_lower_ready, 1)

            def k_lower(ii, u):
                since(dve, k_upper_ready, ii * 2 + u + 1)
                stt(qk_hl[u][R, 3 * N:4 * N], PR[R, :], col[R, 5:6], qk_hl[u][R, 2 * N:3 * N], ALU.add,
                    ALU.subtract).then_inc(k_lower_ready, 1)

            def v_lower(ii, u):
                since(dve, v_upper_ready, ii * 2 + u + 1)
                v = lambda a: a[:, 0:NT * 2 * (CH + 1)].rearrange("p (m c) -> p m c", c=CH + 1)[:, :, 0:CH]
                tt(v(v_lo[u]), PR.rearrange("p (m c) -> p m c", c=CH), v(v_hi[u]), ALU.subtract).then_inc(v_lower_ready, 1)

            def residual_start(ii, u):
                since(dve, ctx_loaded[u], ii * 16 + 16)
                since(dve, z_ready[u], ii)
                ts(z0[u], ct[u], T1, T1GBV, ALU.mult, ALU.add).then_inc(z0_ready[u], 1)

            def row_max(ii, n, half):
                since(dve, scores_ready[half], ii * 4 + n + 1)
                c = (n % 2) * NT + 2 * half
                nc.vector.tensor_reduce(nmx[:, c:c + 2], PS[:, 0:2, :], AX_X, ALU.max, negate=True).then_inc(maxima_ready[half], 1)

            def split_max(ii, n):
                g = ii * 4 + n
                since(dve, maxima_ready[0], g + 1)
                since(dve, maxima_ready[1], g + 1)
                since(dve, max_rows_made, g - 1)
                m = nmx[:, (n % 2) * NT:(n % 2 + 1) * NT]
                v = nm16[:, (n % 2) * 2 * NT:(n % 2 + 1) * 2 * NT].rearrange("p (t s) -> p t s", s=2)
                ts(v[:, :, 0], m, 1.0 / MAX_SCALE, None, ALU.mult).then_inc(max_upper_ready, 1)
                since(dve, max_upper_ready, g + 1)
                stt(v[:, :, 1], m, 1.0 / MAX_SCALE, v[:, :, 0], ALU.mult, ALU.subtract).then_inc(max_split, 1)

            def batch_out(ii, n):
                g = ii * 4 + n
                u, b = n // 2, n % 2
                since(dve, pv_done[1], g + 1)
                o = PS[:, 4 + b, 0:NT * (CH + 1)].rearrange("p (n c) -> p n c", c=CH + 1)
                rs = rsum[:, b * NT:(b + 1) * NT].rearrange("p (n o) -> p n o", o=1)
                nc.vector.reciprocal(rs, o[:, :, CH:CH + 1]).then_inc(sums_inverted, 1)
                since(dve, sums_inverted, g + 1)
                tt(on[u].rearrange("p (n b c) -> p n b c", n=NT, b=2)[:, :, b, :], o[:, :, 0:CH],
                   rs.broadcast_to([P, NT, CH]), ALU.mult).then_inc(attn_normalised, 1)

            def residual(ii, u):
                since(dve, attn_transposed[u], ii + 1)
                since(dve, z_ready[u], ii + 1)
                t = ii * 2 + u
                stt(X[:, bass.ds(t * N, N)], RT, T1G, z[u], ALU.mult, ALU.add).then_inc(x1_ready[u], 1)

            def stats_x1(ii, u):
                t = ii * 2 + u
                nc.vector.bn_stats(stats[:, bass.ds(t * 6, 6)], X[:, bass.ds(t * N, N)])

            def attention_pass(ii, ahead):
                first = isinstance(ii, int) and ii == 0
                for n in range(4):
                    u, b = n // 2, n % 2
                    i1, u1, a1 = later(ii, u, 1)
                    i2, u2, a2 = later(ii, u, 2)
                    i3, u3, a3 = later(ii, u, 3)
                    ip, up = (ii, 0) if u else (ii - 1, 1)
                    i2b, n2 = (ii, n + 2) if n < 2 else (ii + 1, n - 2)
                    m2b, nm2 = (ii, n - 2) if n >= 2 else (ii - 1, n + 2)
                    more2 = n < 2 or ahead >= 1
                    i_s, u_s = (ii - 1, u)
                    stats_now = b == 0 and not (first)
                    if stats_now:
                        since(dve, x1_ready[u_s], i_s + 1)
                    if more2:
                        row_max(i2b, n2, 0)
                    if not (first and n < 2):
                        batch_out(m2b, nm2)
                    if b == 0 and a2 <= ahead:
                        q_lower(i2, u2)
                    if stats_now:
                        stats_x1(i_s, u_s)
                    if b == 1:
                        if a3 <= ahead:
                            normalise(i3, u3)
                        if a1 <= ahead:
                            residual_start(i1, u1)
                    if more2:
                        row_max(i2b, n2, 1)
                        split_max(i2b, n2)
                    if b == 0 and a2 <= ahead:
                        k_lower(i2, u2)
                    if b == 1:
                        if a1 <= ahead:
                            v_lower(i1, u1)
                        if not (first and u == 0):
                            residual(ip, up)
                    if ahead == 0:
                        if n == 0:
                            layernorm_scales(2, 0, E)
                        if n == 1:
                            dve.wait_ge(q_projected, TILES)
                            normalise_x1(0)
                            normalise_x1(1)
                        if n >= 2:
                            for t in (2 * n - 4, 2 * n - 3):
                                max_x1(t)
                                normalise_x1(t + 2)

            def normalise_x1(t):
                if t >= 2:
                    dve.wait_ge(x1_transposed, t - 1)
                    dve.wait_ge(x1_max_taken, t - 1)
                ts(xn[t % 2], X[:, t * N:(t + 1) * N], rstd[:, t:t + 1], nmr[:, t:t + 1],
                   ALU.mult, ALU.add).then_inc(x1_normalised, 1)

            def max_x1(t):
                dve.wait_ge(x1_normalised, t + 1)
                nc.vector.tensor_reduce(a_max[:, t:t + 1], xn[t % 2], AX_X, ALU.max,
                                        apply_absolute_value=True).then_inc(x1_max_taken, 1)

            normalise(0, 0)
            normalise(0, 1)
            q_lower(0, 0)
            gate_up_weights_lower(0, 3)
            k_lower(0, 0)
            normalise(1, 0)
            gate_up_weights_lower(3, 6)
            q_lower(0, 1)
            gate_up_weights_lower(6, 9)
            k_lower(0, 1)
            gate_up_weights_lower(9, 12)
            v_lower(0, 0)
            row_max(0, 0, 0)
            gate_up_weights_lower(12, 14)
            row_max(0, 0, 1)
            split_max(0, 0)
            gate_up_weights_lower(14, 17)
            row_max(0, 1, 0)
            gate_up_weights_lower(17, 19)
            row_max(0, 1, 1)
            split_max(0, 1)
            gate_up_weights_lower(19, 22)
            residual_start(0, 0)
            passes_ahead(dve, attention_pass)
            batch_out(PAIRS - 1, 2)
            max_x1(4)
            normalise_x1(6)
            batch_out(PAIRS - 1, 3)
            max_x1(5)
            normalise_x1(7)
            residual(PAIRS - 1, 1)
            for u in range(2):
                dve.wait_ge(x1_ready[u], PAIRS)
            for t in range(TILES - 2, TILES):
                last = nc.vector.bn_stats(stats[:, 6 * t:6 * t + 6], X[:, t * N:(t + 1) * N])
            wv.step(last)
            max_x1(6)
            max_x1(7)
            layernorm_scales(3, E, TILES)
            normalise_x1(E)
            for t in range(E + 1, TILES):
                normalise_x1(t)
                max_x1(t - 1)
            max_x1(TILES - 1)
            dve.wait_ge(x1_max_taken, TILES)
            nc.vector.reduce_max(sc[:, 25:26], a_max[:, :], AX_X).then_inc(a_max_rows, 1)
            dve.wait_ge(a_max_all, 1)

            wv.step(ts(A_G, A_MAX, 1.0 / (FP8_MAX * 6.0), SCALE_FLOOR, ALU.mult, ALU.max))
            wv.step(nc.vector.reciprocal(A_RG, A_G))
            wv.step(ts(A_C1, A_RG, 1.0 / FP8_MAX, None, ALU.mult))
            tt(A_OUT, A_G, W_DOWN[:, 0:1], ALU.mult).then_inc(a_scale_ready, 1)
            dve.wait_ge(a_scale_ready, 1)

            OB_N = SELECT // BLK
            CHAIN2 = 11

            def left_over(t, r, tmp, rounded, count):
                tt(tmp[:, 0:SELECT], t, r, ALU.subtract).then_inc(rounded, 1)
                dve.wait_ge(rounded, count)

            def second_quantisation(ch, s, tmp, done):
                o_res, o_m = tmp[:, 0:SELECT], tmp[:, SELECT:2 * SELECT]
                o_s, o_rs = tmp[:, 2 * SELECT:2 * SELECT + OB_N], tmp[:, 2 * SELECT + OB_N:2 * SELECT + 2 * OB_N]
                ch.mark(nc.vector.tensor_reduce(o_s, blk(o_res), AX_X, ALU.max, apply_absolute_value=True))
                yield
                ch.wait()
                ch.mark(tt(o_s, o_s, s, ALU.mult))
                yield
                ch.wait()
                ch.mark(ts(o_s, o_s, 1.0 / FP8_MAX, SCALE_FLOOR, ALU.mult, ALU.max))
                yield
                ch.wait()
                ch.mark(nc.vector.reciprocal(o_rs, o_s))
                yield
                ch.wait()
                ch.mark(tt(o_rs, o_rs, s, ALU.mult))
                yield
                ch.wait()
                ch.mark(tt(blk(o_res), blk(o_res), bc(o_rs, OB_N), ALU.mult))
                yield
                ch.wait()
                ch.mark(ts(o_m.bitcast(I32), o_res.bitcast(I32), EXPONENT, None, ALU.bitwise_and))
                yield
                ch.wait()
                ch.mark(ts(o_m, o_m, ROUND_FP8, ROUND_FP8_LEAST, ALU.mult, ALU.max))
                yield
                ch.wait()
                ch.mark(tt(o_res, o_res, o_m, ALU.add))
                yield
                ch.wait()
                tt(o_res, o_res, o_m, ALU.subtract).then_inc(done, 1)

            CHAIN1 = 5

            def scale_x(ii, u):
                ch = Chain(dve, scale_steps, (ii * 2 + u) * CHAIN1, CHAIN1)
                src = PS[:, 4 + u, :]
                A, t, m = qa
                s_blk, rs_blk = a_blk[:, u * NB:(u + 1) * NB], a_blk[:, (2 + u) * NB:(3 + u) * NB]
                since(dve, tokens_back[u], ii + 1)
                ch.step(nc.vector.tensor_reduce(rs_blk, blk(src), AX_X, ALU.max, apply_absolute_value=True))
                ch.step(ts(s_blk, rs_blk, A_C1, SCALE_FLOOR, ALU.mult, ALU.max))
                ch.step(ts(rs_blk, s_blk, A_G, None, ALU.mult))
                ch.step(nc.vector.reciprocal(rs_blk, rs_blk))
                if u == 1:
                    since(dve, a_quantised[0], ii + 1)
                else:
                    since(dve, a_quantised[1], ii)
                ch.step(tt(blk(t), blk(src), bc(rs_blk, NB), ALU.mult))
                ts(m.bitcast(I32), t.bitcast(I32), EXPONENT, None, ALU.bitwise_and).then_inc(a_exponents[u], 1)
                ch.close()

            def round_x(ii, u):
                A, t, m = qa
                since(dve, a_constants[u], ii + 1)
                if u == 1:
                    since(dve, a_transposed[0], ii + 1)
                else:
                    since(dve, a_transposed[1], ii)
                ch = Chain(dve, round_steps, (ii * 2 + u) * CHAIN2, CHAIN2)
                ch.step(stt(A, m, ROUND_FP8_LEAST, t, ALU.add, ALU.add))
                ch.step(stt(A, m, ROUND_FP8_LEAST, A, ALU.add, ALU.subtract, reverse1=True))
                left_over(t[:, N - SELECT:N], A[:, N - SELECT:N], t, a_rounded[u], ii + 1)
                for _ in second_quantisation(ch, a_blk[:, u * NB + NB - OB_N:(u + 1) * NB], t, a_outliers[u]):
                    pass
                ch.close()

            def a_lower(ii, u):
                since(dve, a_upper[u], ii + 1)
                products_read(dve, ii, u)
                tt(at_lo[u][:, :], PS[:, 6 + u, :], at_hi[u][:, :], ALU.subtract).then_inc(a_lower_ready[u], 1)

            def hidden(ii, n):
                slot, u, c = n % 2, n // 3, n % 3
                w_n = CHUNK[c]
                since(dve, silu_done[slot], ii * 3 + n // 2 + 1)
                t = ii * 2 + u
                stt(H[:, bass.ds(t * HID + CSTART[c], w_n)], PS[:, 2 + slot, 0:w_n], A_OUT, sg[slot][:, 0:w_n],
                    ALU.mult, ALU.mult).then_inc(h_ready[slot], 1)

            def hidden_max(ii, u):
                for slot in range(2):
                    n = 3 * u + 2
                    k = ii * 3 + (n // 2 + 1 if slot == n % 2 else (n + 1) // 2)
                    since(dve, h_ready[slot], k)
                t = ii * 2 + u
                hb = h_blk[:, bass.ds(t * HB, HB)]
                ch = Chain(dve, h_max_steps, t * 3, 3)
                ch.step(nc.vector.tensor_reduce(hb, blk(H[:, bass.ds(t * HID, HID)]), AX_X, ALU.max,
                                                apply_absolute_value=True))
                nc.vector.tensor_reduce(h_top[:, bass.ds(t, 1)], hb, AX_X, ALU.max).then_inc(h_top_ready, 1)
                return ch

            def hidden_reciprocals(ii, u, ch):
                t = ii * 2 + u
                hb, hr = h_blk[:, bass.ds(t * HB, HB)], XG[:, bass.ds(t * P + RCP, HB)]
                ch.step(ts(rc_tmp, hb, 1e-30, None, ALU.max))
                ch.step(nc.vector.reciprocal(rc_tmp, rc_tmp))
                ch.close()
                since(dve, tokens_back[u], ii + 1)
                ts(hr, rc_tmp, FP8_MAX, None, ALU.mult).then_inc(h_inverted, 1)

            def gate_up_pass(ii, ahead):
                for u in range(2):
                    i1, u1, a1 = later(ii, u, 1)
                    i2, u2, a2 = later(ii, u, 2)
                    if a1 <= ahead:
                        round_x(i1, u1)
                    hidden(ii, 3 * u)
                    if a2 <= ahead:
                        scale_x(i2, u2)
                    hidden(ii, 3 * u + 1)
                    if a1 <= ahead:
                        a_lower(i1, u1)
                    hidden(ii, 3 * u + 2)
                    ch = hidden_max(ii, u)
                    if ahead == 0 and u == 1:
                        dve.wait_ge(h_top_ready, TILES)
                        nc.vector.reduce_max(sc[:, 26:27], h_top[:, :], AX_X).then_inc(h_max_rows, 1)
                    hidden_reciprocals(ii, u, ch)

            scale_x(0, 0)
            round_x(0, 0)
            scale_x(0, 1)
            a_lower(0, 0)
            for i in range(4):
                dve.wait_ge(x1t_stored[i], TILES // 4 * 16)
            dve.wait_ge(x1_stored, TILES * 16)
            passes_ahead(dve, gate_up_pass)

            dve.wait_ge(h_inverted, TILES)
            for u in range(2):
                dve.wait_ge(tokens_back[u], PAIRS)
            dve.wait_ge(h_max_all, 1)
            wv.step(ts(H_G, H_MAX, 1.0 / (FP8_MAX * 6.0), SCALE_FLOOR, ALU.mult, ALU.max))
            wv.step(nc.vector.reciprocal(H_RG, H_G))
            wv.step(ts(H_LIM, H_RG, 1.0 / SCALE_FLOOR, None, ALU.mult))
            rcp = XG[:, RCP:RCP + TILES * P].rearrange("p (t c) -> p t c", c=P)[:, :, 0:HB]
            for lo, hi in ((0, 1), (1, TILES)):
                ts(rcp[:, lo:hi, :], rcp[:, lo:hi, :], H_LIM, None, ALU.min).then_inc(h_scales, 1)
            tt(H_OUT, H_G, W_DOWN[:, 1:2], ALU.mult)
            wv.step(ts(H_C1, H_RG, 1.0 / FP8_MAX, None, ALU.mult))
            tt(H_OUT, H_OUT, T2, ALU.mult)
            ts(h_blk[:, :], h_blk[:, :], H_C1, SCALE_FLOOR, ALU.mult, ALU.max).then_inc(h_scales, 1)
            dve.wait_ge(h_scales, 3)

            def exponents_h(ii, u):
                t = ii * 2 + u
                since(dve, h_divided[u], ii + 1)
                ts(hm[u].bitcast(I32), H[:, bass.ds(t * HID, HID)].bitcast(I32), EXPONENT, None,
                   ALU.bitwise_and).then_inc(h_exponents[u], 1)

            def round_h(ii, u):
                t = ii * 2 + u
                A = hA[u]
                since(dve, h_constants[u], ii + 1)
                since(dve, h_transposed[u], ii)
                ch = Chain(dve, h_round_steps, t * 2, 2)
                ch.step(stt(A, hm[u], ROUND_FP8_LEAST, H[:, bass.ds(t * HID, HID)], ALU.add, ALU.add))
                ch.step(stt(A, hm[u], ROUND_FP8_LEAST, A, ALU.add, ALU.subtract, reverse1=True))
                if u == 1:
                    since(dve, h_quantised[0], ii + 1)
                else:
                    since(dve, h_quantised[1], ii)
                ch.close()
                left_over(H[:, bass.ds(t * HID + HID - SELECT, SELECT)], A[:, HID - SELECT:HID], h_tmp, h_rounded[u], ii + 1)

            def outliers_h(ii, u):
                t = ii * 2 + u
                ch = Chain(dve, h_outlier_steps, t * (CHAIN2 - 2), CHAIN2 - 2)
                yield from second_quantisation(ch, h_blk[:, bass.ds(t * HB + HB - OB_N, OB_N)], h_tmp, h_outliers[u])
                ch.close()

            def h_lower(ii, u, part):
                if part == 0:
                    since(dve, h_upper[u], ii + 1)
                    since(dve, y_done[u], ii)
                lo, hi = part * 4 * P, min((part + 1) * 4 * P, HID // P * P)
                src = PS[:, 3 * u + part, :]
                last = tt(ht_lo[u][:, lo:hi], src[:, 0:hi - lo], ht_hi[u][:, lo:hi], ALU.subtract)
                if hi == HID // P * P:
                    r = rows(IT - 1)
                    last = tt(ht_lo[u][0:r, hi:hi + P], src[0:r, hi - lo:hi - lo + P], ht_hi[u][0:r, hi:hi + P],
                              ALU.subtract)
                    last.then_inc(h_lower_ready[u], 1)

            def down_pass(ii, ahead):
                for u in range(2):
                    i1, u1, a1 = later(ii, u, 1)
                    i2, u2, a2 = later(ii, u, 2)
                    i3, u3, a3 = later(ii, u, 3)
                    if a2 <= ahead:
                        round_h(i2, u2)
                        outliers = outliers_h(i2, u2)
                        next(outliers)
                    if a3 <= ahead:
                        exponents_h(i3, u3)
                    if a2 <= ahead:
                        next(outliers)
                    if a1 <= ahead:
                        h_lower(i1, u1, 0)
                    if a2 <= ahead:
                        next(outliers)
                        next(outliers)
                    if a1 <= ahead:
                        h_lower(i1, u1, 1)
                    if a2 <= ahead:
                        next(outliers)
                        next(outliers)
                    if a1 <= ahead:
                        h_lower(i1, u1, 2)
                    if a2 <= ahead:
                        next(outliers)
                        next(outliers)
                    if a2 <= ahead:
                        for _ in outliers:
                            pass

            exponents_h(0, 0)
            exponents_h(0, 1)
            round_h(0, 0)
            for _ in outliers_h(0, 0):
                pass
            exponents_h(1, 0)
            round_h(0, 1)
            outliers = outliers_h(0, 1)
            for part in range(3):
                h_lower(0, 0, part)
                next(outliers)
            for _ in outliers:
                pass
            passes_ahead(dve, down_pass)


def kernel(x, ctx_4096, g_xattn, g_ffn, L0_xattn_Wq, L0_xattn_bq, L0_xattn_Wk, L0_xattn_bk, L0_xattn_Wv,
           L0_xattn_bv, L0_xattn_gamma, L0_ffn_w_gate, L0_ffn_w_up, L0_ffn_w_down, L0_ffn_ri_in, L0_ffn_ri_mid):
    import numpy as np
    import concourse.bacc as bacc
    from concourse.bass_utils import run_bass_kernel_spmd

    B, C, N = x.shape
    HID = L0_ffn_w_down.shape[1]
    IT = -(-HID // P)
    x, ctx_in = np.asarray(x), np.asarray(ctx_4096)
    cols = np.zeros((P, 8), np.float32)
    cols[:, 0] = np.asarray(L0_xattn_gamma)[0]
    cols[:, 1] = np.asarray(g_xattn)[0]
    cols[:, 2] = np.asarray(g_ffn)[0]
    cols[:, 3] = np.tile(np.asarray(L0_xattn_bv), 2)
    cols[:C, 4] = np.tile(np.asarray(L0_xattn_bq), 2)
    cols[:C, 5] = np.tile(np.asarray(L0_xattn_bk), 2)
    mid = np.zeros(IT * P, np.int32)
    mid[:HID] = np.asarray(L0_ffn_ri_mid)
    arrays = {
        "x": np.ascontiguousarray(x.reshape(B * C, N)),
        "ctx_in": np.ascontiguousarray(ctx_in.reshape(B * C, N)),
        "w_gu_t": np.ascontiguousarray(np.concatenate([np.asarray(L0_ffn_w_gate).T, np.asarray(L0_ffn_w_up).T], axis=1)),
        "w_down_t": np.ascontiguousarray(np.asarray(L0_ffn_w_down).T),
        "wq_t": np.ascontiguousarray(np.asarray(L0_xattn_Wq).T),
        "wk_t": np.ascontiguousarray(np.asarray(L0_xattn_Wk).T),
        "wv_t": np.ascontiguousarray(np.asarray(L0_xattn_Wv).T),
        "cols": cols,
        "ri_in": np.ascontiguousarray(np.asarray(L0_ffn_ri_in).reshape(-1, P).T),
        "ri_mid": np.ascontiguousarray(mid.reshape(-1, P).T),
    }
    nc = bacc.Bacc("TRN2", target_bir_lowering=False, num_devices=1)
    args = {k: nc.dram_tensor(f"in_{k}", a.shape, mybir.dt.from_np(a.dtype), kind="ExternalInput").ap()
            for k, a in arrays.items()}
    out = nc.dram_tensor("out_y", (B * C, N), F32, kind="ExternalOutput").ap()
    flamingo_block(nc, *args.values(), out)
    r = run_bass_kernel_spmd(nc, [{f"in_{k}": a for k, a in arrays.items()}], core_ids=[0])
    return r.results[0]["out_y"].reshape(B, C, N)
```
